# Optimizing a Trainium2 kernel written in Bass

```python
import numpy as np
import jax
import jax.numpy as jnp

def _softmax(x, axis=-1):
    return jax.nn.softmax(x, axis=axis)

def _gelu(x):
    return jax.nn.gelu(x, approximate=True)

def _silu(x):
    return jax.nn.silu(x)

def _sigmoid(x):
    return jax.nn.sigmoid(x)

def _layernorm(x, axis=-1, eps=1e-05):
    m = jnp.mean(x, axis=axis, keepdims=True)
    v = jnp.var(x, axis=axis, keepdims=True)
    return (x - m) / jnp.sqrt(v + eps)

def _scatter_add(tgt, idx, src, axis=0):
    return tgt.at[idx].add(src)

def _segment_sum(src, seg, n):
    return jax.ops.segment_sum(src, seg, n)
kernel_name = 'mk_decoder_preln_d2_seqx_r8_8527ad'

def setup_inputs(seed: int=0):
    np.random.seed(seed)
    _w = jnp.asarray

    def _rec_inputs():
        import jax
        import jax.numpy as jnp
        _rk = jax.random.key(seed)
        x = -0.000125 + 0.9999 * jax.random.normal(jax.random.fold_in(_rk, 1), (4, 256, 256), jnp.float32)
        _lenS = 256 - jax.random.randint(jax.random.fold_in(_rk, 7), (4,), 0, max(1, 256 // 4) + 1, jnp.int32)
        _lenS2 = 1601 - jax.random.randint(jax.random.fold_in(_rk, 8), (4,), 0, max(1, 1601 // 4) + 1, jnp.int32)
        _ctx_2048P = jax.random.normal(jax.random.fold_in(_rk, 11), (4, 16, 256), jnp.float32)
        _ctx_2048c = jax.random.dirichlet(jax.random.fold_in(_rk, 511), 0.3 * jnp.ones((16,), jnp.float32), (4, 1601))
        _ctx_2048t = jnp.einsum('bsk,bkd->bsd', _ctx_2048c, _ctx_2048P)
        _ctx_2048t = _ctx_2048t * jax.lax.rsqrt(jnp.mean(jnp.square(_ctx_2048t)) + 1e-12) * 0.953939
        ctx_2048 = -0.000514642 + 1.00011 * (_ctx_2048t + 0.3 * jax.random.normal(jax.random.fold_in(_rk, 611), (4, 1601, 256), jnp.float32))
        pos_BxS2 = jnp.broadcast_to(jnp.arange(1601, dtype=jnp.int32), (4, 1601))
        itok_BxS_4096_4607 = jax.random.randint(jax.random.fold_in(_rk, 14), (4, 256), 512, 576, jnp.int32)
        _validS = jnp.arange(256)[None, :] < _lenS[:, None]
        _validS2 = jnp.arange(1601)[None, :] < _lenS2[:, None]
        _causal = jnp.tril(jnp.ones((256, 256), dtype=bool))
        mask_BxS2_bk0 = jnp.logical_not(jnp.broadcast_to(_validS2[:, :], (4, 1601)))
        return (x, ctx_2048, pos_BxS2, itok_BxS_4096_4607, mask_BxS2_bk0)
    x, ctx_2048, pos_BxS2, itok_BxS_4096_4607, mask_BxS2_bk0 = _rec_inputs()

    def _L0_attn_setup():
        import jax, jax.numpy as jnp
        import numpy as np
        HEAD = 16
        THETA = 30000.0

        def _layernorm(x, g, b, eps=1e-05):
            mu = jnp.mean(x, axis=-1, keepdims=True)
            var = jnp.mean((x - mu) ** 2, axis=-1, keepdims=True)
            return (x - mu) * jax.lax.rsqrt(var + eps) * g + b

        def _rotary(t, xa):
            B, H, C, D = t.shape
            pos = jnp.arange(C, dtype=t.dtype)
            freqs = jnp.arange(0, D, 2, dtype=t.dtype) / D * jnp.log(jnp.asarray(THETA, t.dtype))
            ang = pos[:, None] * freqs[None, :]
            m = jnp.linalg.norm(xa, axis=-1, keepdims=True)
            fre = (m * jnp.cos(ang))[:, None]
            fim = (m * jnp.sin(ang))[:, None]
            tp = t.reshape(B, H, C, D // 2, 2)
            a, b = (tp[..., 0], tp[..., 1])
            out = jnp.stack([a * fre - b * fim, a * fim + b * fre], axis=-1)
            return out.reshape(B, H, C, D)
        key = jax.random.key(seed)
        ks = jax.random.split(key, 4)
        B, C, Dm = (1, 256, 256)
        hd = Dm // HEAD
        w = 0.02
        return {'x': jax.random.normal(ks[0], (B, C, Dm), jnp.float32), 'qn_g': jnp.ones((Dm,), jnp.float32), 'qn_b': jnp.zeros((Dm,), jnp.float32), 'kvn_g': jnp.ones((Dm,), jnp.float32), 'kvn_b': jnp.zeros((Dm,), jnp.float32), 'Wq': w * jax.random.normal(ks[1], (Dm, Dm), jnp.float32), 'bq': jnp.zeros((Dm,), jnp.float32), 'Wkv': w * jax.random.normal(ks[2], (Dm, 2 * Dm), jnp.float32), 'bkv': jnp.zeros((2 * Dm,), jnp.float32), 'Wo': w * jax.random.normal(ks[3], (Dm, Dm), jnp.float32), 'bo': jnp.zeros((Dm,), jnp.float32), 'ln_g': jnp.ones((hd,), jnp.float32), 'ln_b': jnp.zeros((hd,), jnp.float32)}
    _L0_attn_all = _L0_attn_setup()
    _L0_attn_in = {k: v for k, v in _L0_attn_all.items() if k in ('qn_g', 'qn_b', 'kvn_g', 'kvn_b', 'Wq', 'bq', 'Wkv', 'bkv', 'Wo', 'bo', 'ln_g', 'ln_b')}
    del _L0_attn_all

    def _L0_xattn_setup():
        import jax, jax.numpy as jnp
        import numpy as np
        key = jax.random.key(seed)
        k1, k2, k3 = jax.random.split(key, 3)
        B, S, D, M = (8, 256, 256, 128)
        hidden_states = jax.random.normal(k1, (B, S, D), dtype=jnp.float32)
        memory_tokens = jax.random.normal(k2, (B, M, D), dtype=jnp.float32)
        memory_mask = jax.random.randint(k3, (B, M), 0, 2).astype(jnp.bool_)
        return {'hidden_states': hidden_states, 'memory_tokens': memory_tokens, 'memory_mask': memory_mask}
    _L0_xattn_all = _L0_xattn_setup()
    _L0_xattn_in = {k: v for k, v in _L0_xattn_all.items() if k in ()}
    del _L0_xattn_all

    def _L0_ffn_setup():
        import jax, jax.numpy as jnp
        import numpy as np
        EPS = 1e-06
        Q_B = 128.0

        def layer_norm(x):
            mean = jnp.mean(x, axis=-1, keepdims=True)
            var = jnp.var(x, axis=-1, keepdims=True)
            return (x - mean) / jnp.sqrt(var + EPS)

        def absmax_quant(x):
            gamma = jnp.max(jnp.abs(x), axis=-1, keepdims=True)
            x_hat = jnp.clip(x * Q_B / gamma, -Q_B + EPS, Q_B - EPS)
            return x_hat * gamma / Q_B

        def ternarize_weights(w):
            gamma = jnp.mean(jnp.abs(w))
            return jnp.sign(jnp.round(w / (gamma + EPS))) * gamma

        def bitlinear(x, w):
            xn = layer_norm(x)
            x_hat = xn + jax.lax.stop_gradient(absmax_quant(xn) - xn)
            w_hat = w + jax.lax.stop_gradient(ternarize_weights(w) - w)
            return jnp.einsum('bsd,od->bso', x_hat, w_hat)
        key = jax.random.key(seed)
        k1, k2, k3 = jax.random.split(key, 3)
        B, S, D = (4, 256, 256)
        x = jax.random.normal(k1, (B, S, D), dtype=jnp.float32)
        w_fc = jax.random.normal(k2, (4 * D, D), dtype=jnp.float32) / np.sqrt(D)
        w_proj = jax.random.normal(k3, (D, 4 * D), dtype=jnp.float32) / np.sqrt(4 * D)
        return {'x': x, 'w_fc': w_fc, 'w_proj': w_proj}
    _L0_ffn_all = _L0_ffn_setup()
    _L0_ffn_in = {k: v for k, v in _L0_ffn_all.items() if k in ('w_fc', 'w_proj')}
    del _L0_ffn_all

    def _L1_attn_setup():
        import jax, jax.numpy as jnp
        import numpy as np
        from jax import lax
        CHUNK = 32
        ROPE_BASE = 10000.0

        def _forward(x, norm_scale, conv_w, conv_b, in_proj_w, dt_bias, head_mix, out_proj_w):
            B, N, D = x.shape
            H = head_mix.shape[0]
            Dh = D // H
            K = conv_w.shape[-1]
            residual = x
            xf = x.astype(jnp.float32)
            rms = lax.rsqrt(jnp.mean(xf * xf, -1, keepdims=True) + 1e-06)
            xn = jnp.clip(norm_scale * xf * rms, -60000.0, 60000.0).astype(x.dtype)
            xc = lax.conv_general_dilated(xn.transpose(0, 2, 1), conv_w, (1,), [(K - 1, 0)], dimension_numbers=('NCH', 'OIH', 'NCH'), feature_group_count=D)
            xc = xc + conv_b[None, :, None]
            xc = jax.nn.silu(xc.transpose(0, 2, 1))
            fused = xc @ in_proj_w.T
            dt_raw, v, gate = jnp.split(fused, 3, axis=-1)
            dt = jnp.clip(jax.nn.softplus(dt_raw.astype(jnp.float32) + dt_bias), 0.001, 2.0)
            gate = jax.nn.sigmoid(gate)
            log_alpha = -dt
            inv_freq = 1.0 / ROPE_BASE ** (jnp.arange(0, Dh, 2, dtype=jnp.float32) / Dh)
            t = jnp.arange(N, dtype=jnp.float32)
            freqs = t[:, None] * inv_freq[None, :]
            cos = jnp.cos(freqs)[None, :, None, :]
            sin = jnp.sin(freqs)[None, :, None, :]
            v4 = v.reshape(B, N, H, Dh)
            v1, v2 = (v4[..., :Dh // 2], v4[..., Dh // 2:])
            v_rot = jnp.concatenate([v1 * cos - v2 * sin, v1 * sin + v2 * cos], -1).reshape(B, N, D)
            v_in = v_rot * dt
            pad = -N % CHUNK
            if pad:
                v_in = jnp.pad(v_in, ((0, 0), (0, pad), (0, 0)))
                log_alpha = jnp.pad(log_alpha, ((0, 0), (0, pad), (0, 0)))
            NC = v_in.shape[1] // CHUNK
            vc = v_in.reshape(B, NC, CHUNK, D)
            la = log_alpha.reshape(B, NC, CHUNK, D)
            L = jnp.clip(jnp.cumsum(la, axis=2), -20.0, 0.0)
            Lmax = jnp.max(L, axis=2, keepdims=True)
            Ls = L - Lmax
            cum = jnp.cumsum(jnp.exp(-Ls) * vc, axis=2)
            chunk_out = jnp.exp(Ls) * cum
            if NC > 1:
                bd = L[:, :, -1, :]
                bo = chunk_out[:, :, -1, :]
                cd = jnp.clip(jnp.cumsum(bd, axis=1), -80.0, 0.0)
                stab = jnp.max(cd, axis=1, keepdims=True)
                ncd = jnp.clip(cd - stab, -20.0, 0.0)
                seeds = bo * jnp.exp(-ncd)
                shifted = jnp.pad(seeds[:, :-1], ((0, 0), (1, 0), (0, 0)))
                carries = jnp.cumsum(shifted, axis=1) * jnp.exp(ncd)
                final = chunk_out + carries[:, :, None, :] * jnp.exp(L)
            else:
                final = chunk_out
            final = final.astype(x.dtype).reshape(B, -1, D)[:, :N, :]
            vm = jnp.einsum('bnhd,hm->bnmd', final.reshape(B, N, H, Dh), head_mix).reshape(B, N, D)
            out = vm * gate @ out_proj_w.T
            return residual + out
        D, H, K = (256, 16, 4)
        Dh = D // H
        key = jax.random.key(seed)
        ks = jax.random.split(key, 8)
        x = jax.random.normal(ks[0], (2, 512, D), dtype=jnp.float32)
        norm_scale = jnp.ones((D,), jnp.float32)
        conv_w = jax.random.normal(ks[1], (D, 1, K), jnp.float32) * 0.1
        conv_b = jnp.zeros((D,), jnp.float32)
        in_proj_w = jax.random.normal(ks[2], (3 * D, D), jnp.float32) * 0.02
        out_proj_w = jax.random.normal(ks[3], (D, D), jnp.float32) * 0.02
        u = jax.random.uniform(ks[4], (H, Dh), jnp.float32)
        dt = jnp.clip(jnp.exp(u * (np.log(0.1) - np.log(10.0)) + np.log(10.0)), 0.001, None)
        dt_bias = (dt + jnp.log(-jnp.expm1(-dt))).reshape(-1)
        head_mix = jnp.eye(H, dtype=jnp.float32)
        return {'x': x, 'norm_scale': norm_scale, 'conv_w': conv_w, 'conv_b': conv_b, 'in_proj_w': in_proj_w, 'dt_bias': dt_bias, 'head_mix': head_mix, 'out_proj_w': out_proj_w}
    _L1_attn_all = _L1_attn_setup()
    _L1_attn_in = {k: v for k, v in _L1_attn_all.items() if k in ('norm_scale', 'conv_w', 'conv_b', 'in_proj_w', 'dt_bias', 'head_mix', 'out_proj_w')}
    del _L1_attn_all

    def _L1_xattn_setup():
        import jax, jax.numpy as jnp
        import numpy as np
        B, CTX, DRAFT, D = (2, 512, 64, 256)
        H, KVH, HD = (16, 4, 128)
        N_REP = H // KVH
        EPS = 1e-06
        THETA = 10000.0
        SCALE = 1.0 / np.sqrt(HD).astype(np.float32)

        def _rms_norm(x, w):
            v = jnp.mean(jnp.square(x.astype(jnp.float32)), axis=-1, keepdims=True)
            return (w * (x.astype(jnp.float32) * jax.lax.rsqrt(v + EPS))).astype(x.dtype)

        def _rotate_half(x):
            x1, x2 = jnp.split(x, 2, axis=-1)
            return jnp.concatenate((-x2, x1), axis=-1)

        def _rope(x, pos):
            inv_freq = 1.0 / THETA ** (jnp.arange(0, HD, 2, dtype=jnp.float32) / HD)
            freqs = pos.astype(jnp.float32)[:, None, :, None] * inv_freq
            emb = jnp.concatenate((freqs, freqs), axis=-1)
            return x * jnp.cos(emb) + _rotate_half(x) * jnp.sin(emb)
        key = jax.random.key(seed)
        ks = jax.random.split(key, 6)
        return {'draft_hidden': jax.random.normal(ks[0], (B, DRAFT, D), jnp.float32), 'context_hidden': jax.random.normal(ks[1], (B, CTX, D), jnp.float32), 'Wq': jax.random.normal(ks[2], (H * HD, D), jnp.float32) * 0.02, 'Wk': jax.random.normal(ks[3], (KVH * HD, D), jnp.float32) * 0.02, 'Wv': jax.random.normal(ks[4], (KVH * HD, D), jnp.float32) * 0.02, 'Wo': jax.random.normal(ks[5], (D, H * HD), jnp.float32) * 0.02, 'q_norm_w': jnp.ones((HD,), jnp.float32), 'k_norm_w': jnp.ones((HD,), jnp.float32), 'context_position_ids': jnp.broadcast_to(jnp.arange(CTX, dtype=jnp.int32), (B, CTX)), 'draft_position_ids': jnp.broadcast_to(CTX + jnp.arange(DRAFT, dtype=jnp.int32), (B, DRAFT))}
    _L1_xattn_all = _L1_xattn_setup()
    _L1_xattn_in = {k: v for k, v in _L1_xattn_all.items() if k in ('Wq', 'Wk', 'Wv', 'Wo', 'q_norm_w', 'k_norm_w')}
    del _L1_xattn_all

    def _L1_ffn_setup():
        import jax, jax.numpy as jnp
        import numpy as np
        B, S, D = (4, 256, 256)
        E, K, M = (8, 2, 128)
        key = jax.random.key(seed)
        k0, k1, k2, k3, k4 = jax.random.split(key, 5)
        d_scale = D ** (-0.5)
        m_scale = M ** (-0.5)
        return {'x': jax.random.normal(k0, (B, S, D), jnp.float32), 'w_gate': jax.random.normal(k1, (D, E), jnp.float32) * d_scale, 'wi_0': jax.random.normal(k2, (E, D, M), jnp.float32) * d_scale, 'wi_1': jax.random.normal(k3, (E, D, M), jnp.float32) * d_scale, 'wo': jax.random.normal(k4, (E, M, D), jnp.float32) * m_scale}
    _L1_ffn_all = _L1_ffn_setup()
    _L1_ffn_in = {k: v for k, v in _L1_ffn_all.items() if k in ('w_gate', 'wi_0', 'wi_1', 'wo')}
    del _L1_ffn_all
    return {'x': x, 'ctx_2048': ctx_2048, 'pos_BxS2': pos_BxS2, 'itok_BxS_4096_4607': itok_BxS_4096_4607, 'mask_BxS2_bk0': mask_BxS2_bk0, 'L0_attn_qn_g': _L0_attn_in['qn_g'], 'L0_attn_qn_b': _L0_attn_in['qn_b'], 'L0_attn_kvn_g': _L0_attn_in['kvn_g'], 'L0_attn_kvn_b': _L0_attn_in['kvn_b'], 'L0_attn_Wq': _L0_attn_in['Wq'], 'L0_attn_bq': _L0_attn_in['bq'], 'L0_attn_Wkv': _L0_attn_in['Wkv'], 'L0_attn_bkv': _L0_attn_in['bkv'], 'L0_attn_Wo': _L0_attn_in['Wo'], 'L0_attn_bo': _L0_attn_in['bo'], 'L0_attn_ln_g': _L0_attn_in['ln_g'], 'L0_attn_ln_b': _L0_attn_in['ln_b'], 'L0_ffn_w_fc': _L0_ffn_in['w_fc'], 'L0_ffn_w_proj': _L0_ffn_in['w_proj'], 'L1_attn_norm_scale': _L1_attn_in['norm_scale'], 'L1_attn_conv_w': _L1_attn_in['conv_w'], 'L1_attn_conv_b': _L1_attn_in['conv_b'], 'L1_attn_in_proj_w': _L1_attn_in['in_proj_w'], 'L1_attn_dt_bias': _L1_attn_in['dt_bias'], 'L1_attn_head_mix': _L1_attn_in['head_mix'], 'L1_attn_out_proj_w': _L1_attn_in['out_proj_w'], 'L1_xattn_Wq': _L1_xattn_in['Wq'], 'L1_xattn_Wk': _L1_xattn_in['Wk'], 'L1_xattn_Wv': _L1_xattn_in['Wv'], 'L1_xattn_Wo': _L1_xattn_in['Wo'], 'L1_xattn_q_norm_w': _L1_xattn_in['q_norm_w'], 'L1_xattn_k_norm_w': _L1_xattn_in['k_norm_w'], 'L1_ffn_w_gate': _L1_ffn_in['w_gate'], 'L1_ffn_wi_0': _L1_ffn_in['wi_0'], 'L1_ffn_wi_1': _L1_ffn_in['wi_1'], 'L1_ffn_wo': _L1_ffn_in['wo']}

def reference(x, ctx_2048, pos_BxS2, itok_BxS_4096_4607, mask_BxS2_bk0, L0_attn_qn_g, L0_attn_qn_b, L0_attn_kvn_g, L0_attn_kvn_b, L0_attn_Wq, L0_attn_bq, L0_attn_Wkv, L0_attn_bkv, L0_attn_Wo, L0_attn_bo, L0_attn_ln_g, L0_attn_ln_b, L0_ffn_w_fc, L0_ffn_w_proj, L1_attn_norm_scale, L1_attn_conv_w, L1_attn_conv_b, L1_attn_in_proj_w, L1_attn_dt_bias, L1_attn_head_mix, L1_attn_out_proj_w, L1_xattn_Wq, L1_xattn_Wk, L1_xattn_Wv, L1_xattn_Wo, L1_xattn_q_norm_w, L1_xattn_k_norm_w, L1_ffn_w_gate, L1_ffn_wi_0, L1_ffn_wi_1, L1_ffn_wo):
    import jax
    import jax.numpy as jnp

    def _L0_attn_ref(x, qn_g, qn_b, kvn_g, kvn_b, Wq, bq, Wkv, bkv, Wo, bo, ln_g, ln_b):
        import jax, jax.numpy as jnp
        import numpy as np
        HEAD = 16
        THETA = 30000.0

        def _layernorm(x, g, b, eps=1e-05):
            mu = jnp.mean(x, axis=-1, keepdims=True)
            var = jnp.mean((x - mu) ** 2, axis=-1, keepdims=True)
            return (x - mu) * jax.lax.rsqrt(var + eps) * g + b

        def _rotary(t, xa):
            B, H, C, D = t.shape
            pos = jnp.arange(C, dtype=t.dtype)
            freqs = jnp.arange(0, D, 2, dtype=t.dtype) / D * jnp.log(jnp.asarray(THETA, t.dtype))
            ang = pos[:, None] * freqs[None, :]
            m = jnp.linalg.norm(xa, axis=-1, keepdims=True)
            fre = (m * jnp.cos(ang))[:, None]
            fim = (m * jnp.sin(ang))[:, None]
            tp = t.reshape(B, H, C, D // 2, 2)
            a, b = (tp[..., 0], tp[..., 1])
            out = jnp.stack([a * fre - b * fim, a * fim + b * fre], axis=-1)
            return out.reshape(B, H, C, D)
        B, C, Dm = x.shape
        H = HEAD
        hd = Dm // H
        scale = hd ** (-0.25)
        q = (_layernorm(x, qn_g, qn_b) @ Wq + bq).reshape(B, C, H, hd).transpose(0, 2, 1, 3)
        kv = (_layernorm(x, kvn_g, kvn_b) @ Wkv + bkv).reshape(B, C, 2, H, hd)
        kv = kv.transpose(2, 0, 3, 1, 4)
        k, v = (kv[0], kv[1])
        q = q * scale
        k = k * scale
        q = _rotary(q, x)
        k = _rotary(k, x)
        qn = _layernorm(q, ln_g, ln_b)
        kn = _layernorm(k, ln_g, ln_b)
        scores = jnp.einsum('bhqd,bhkd->bhqk', qn, kn) / jnp.sqrt(jnp.asarray(hd, x.dtype))
        causal = jnp.tril(jnp.ones((C, C), bool))
        scores = jnp.where(causal, scores, jnp.finfo(scores.dtype).min)
        w = jax.nn.softmax(scores, axis=-1)
        a = jnp.einsum('bhqk,bhkd->bhqd', w, v)
        out = a.transpose(0, 2, 1, 3).reshape(B, C, Dm) @ Wo + bo
        return out

    def _L0_xattn_ref(hidden_states, memory_tokens, memory_mask):
        import jax, jax.numpy as jnp
        import numpy as np
        B, S, D = hidden_states.shape
        scale = 1.0 / jnp.sqrt(jnp.asarray(D, hidden_states.dtype))
        scores = jnp.einsum('bsd,bmd->bsm', hidden_states, memory_tokens) * scale
        neg_inf = jnp.asarray(-1e+30, scores.dtype)
        scores = jnp.where(memory_mask[:, None, :], scores, neg_inf)
        attn = jax.nn.softmax(scores, axis=-1)
        readout = jnp.einsum('bsm,bmd->bsd', attn, memory_tokens)
        valid_b = jnp.any(memory_mask, axis=-1)
        out = jnp.where(valid_b[:, None, None], readout, jnp.zeros_like(readout))
        return out

    def _L0_ffn_ref(x, w_fc, w_proj):
        import jax, jax.numpy as jnp
        import numpy as np
        EPS = 1e-06
        Q_B = 128.0

        def layer_norm(x):
            mean = jnp.mean(x, axis=-1, keepdims=True)
            var = jnp.var(x, axis=-1, keepdims=True)
            return (x - mean) / jnp.sqrt(var + EPS)

        def absmax_quant(x):
            gamma = jnp.max(jnp.abs(x), axis=-1, keepdims=True)
            x_hat = jnp.clip(x * Q_B / gamma, -Q_B + EPS, Q_B - EPS)
            return x_hat * gamma / Q_B

        def ternarize_weights(w):
            gamma = jnp.mean(jnp.abs(w))
            return jnp.sign(jnp.round(w / (gamma + EPS))) * gamma

        def bitlinear(x, w):
            xn = layer_norm(x)
            x_hat = xn + jax.lax.stop_gradient(absmax_quant(xn) - xn)
            w_hat = w + jax.lax.stop_gradient(ternarize_weights(w) - w)
            return jnp.einsum('bsd,od->bso', x_hat, w_hat)
        h = bitlinear(x, w_fc)
        h = jax.nn.gelu(h, approximate=False)
        return bitlinear(h, w_proj)

    def _L1_attn_ref(x, norm_scale, conv_w, conv_b, in_proj_w, dt_bias, head_mix, out_proj_w):
        import jax, jax.numpy as jnp
        import numpy as np
        from jax import lax
        CHUNK = 32
        ROPE_BASE = 10000.0

        def _forward(x, norm_scale, conv_w, conv_b, in_proj_w, dt_bias, head_mix, out_proj_w):
            B, N, D = x.shape
            H = head_mix.shape[0]
            Dh = D // H
            K = conv_w.shape[-1]
            residual = x
            xf = x.astype(jnp.float32)
            rms = lax.rsqrt(jnp.mean(xf * xf, -1, keepdims=True) + 1e-06)
            xn = jnp.clip(norm_scale * xf * rms, -60000.0, 60000.0).astype(x.dtype)
            xc = lax.conv_general_dilated(xn.transpose(0, 2, 1), conv_w, (1,), [(K - 1, 0)], dimension_numbers=('NCH', 'OIH', 'NCH'), feature_group_count=D)
            xc = xc + conv_b[None, :, None]
            xc = jax.nn.silu(xc.transpose(0, 2, 1))
            fused = xc @ in_proj_w.T
            dt_raw, v, gate = jnp.split(fused, 3, axis=-1)
            dt = jnp.clip(jax.nn.softplus(dt_raw.astype(jnp.float32) + dt_bias), 0.001, 2.0)
            gate = jax.nn.sigmoid(gate)
            log_alpha = -dt
            inv_freq = 1.0 / ROPE_BASE ** (jnp.arange(0, Dh, 2, dtype=jnp.float32) / Dh)
            t = jnp.arange(N, dtype=jnp.float32)
            freqs = t[:, None] * inv_freq[None, :]
            cos = jnp.cos(freqs)[None, :, None, :]
            sin = jnp.sin(freqs)[None, :, None, :]
            v4 = v.reshape(B, N, H, Dh)
            v1, v2 = (v4[..., :Dh // 2], v4[..., Dh // 2:])
            v_rot = jnp.concatenate([v1 * cos - v2 * sin, v1 * sin + v2 * cos], -1).reshape(B, N, D)
            v_in = v_rot * dt
            pad = -N % CHUNK
            if pad:
                v_in = jnp.pad(v_in, ((0, 0), (0, pad), (0, 0)))
                log_alpha = jnp.pad(log_alpha, ((0, 0), (0, pad), (0, 0)))
            NC = v_in.shape[1] // CHUNK
            vc = v_in.reshape(B, NC, CHUNK, D)
            la = log_alpha.reshape(B, NC, CHUNK, D)
            L = jnp.clip(jnp.cumsum(la, axis=2), -20.0, 0.0)
            Lmax = jnp.max(L, axis=2, keepdims=True)
            Ls = L - Lmax
            cum = jnp.cumsum(jnp.exp(-Ls) * vc, axis=2)
            chunk_out = jnp.exp(Ls) * cum
            if NC > 1:
                bd = L[:, :, -1, :]
                bo = chunk_out[:, :, -1, :]
                cd = jnp.clip(jnp.cumsum(bd, axis=1), -80.0, 0.0)
                stab = jnp.max(cd, axis=1, keepdims=True)
                ncd = jnp.clip(cd - stab, -20.0, 0.0)
                seeds = bo * jnp.exp(-ncd)
                shifted = jnp.pad(seeds[:, :-1], ((0, 0), (1, 0), (0, 0)))
                carries = jnp.cumsum(shifted, axis=1) * jnp.exp(ncd)
                final = chunk_out + carries[:, :, None, :] * jnp.exp(L)
            else:
                final = chunk_out
            final = final.astype(x.dtype).reshape(B, -1, D)[:, :N, :]
            vm = jnp.einsum('bnhd,hm->bnmd', final.reshape(B, N, H, Dh), head_mix).reshape(B, N, D)
            out = vm * gate @ out_proj_w.T
            return residual + out
        return _forward(x, norm_scale, conv_w, conv_b, in_proj_w, dt_bias, head_mix, out_proj_w)

    def _L1_xattn_ref(draft_hidden, context_hidden, Wq, Wk, Wv, Wo, q_norm_w, k_norm_w, context_position_ids, draft_position_ids):
        import jax, jax.numpy as jnp
        import numpy as np
        B, CTX, DRAFT, D = (2, 512, 64, 256)
        H, KVH, HD = (16, 4, 128)
        N_REP = H // KVH
        EPS = 1e-06
        THETA = 10000.0
        SCALE = 1.0 / np.sqrt(HD).astype(np.float32)

        def _rms_norm(x, w):
            v = jnp.mean(jnp.square(x.astype(jnp.float32)), axis=-1, keepdims=True)
            return (w * (x.astype(jnp.float32) * jax.lax.rsqrt(v + EPS))).astype(x.dtype)

        def _rotate_half(x):
            x1, x2 = jnp.split(x, 2, axis=-1)
            return jnp.concatenate((-x2, x1), axis=-1)

        def _rope(x, pos):
            inv_freq = 1.0 / THETA ** (jnp.arange(0, HD, 2, dtype=jnp.float32) / HD)
            freqs = pos.astype(jnp.float32)[:, None, :, None] * inv_freq
            emb = jnp.concatenate((freqs, freqs), axis=-1)
            return x * jnp.cos(emb) + _rotate_half(x) * jnp.sin(emb)
        bsz, draft_len, _ = draft_hidden.shape
        ctx_len = context_hidden.shape[1]
        total_len = ctx_len + draft_len
        q = (draft_hidden @ Wq.T).reshape(bsz, draft_len, H, HD)
        q = _rms_norm(q, q_norm_w).transpose(0, 2, 1, 3)
        kv_in = jnp.concatenate([context_hidden, draft_hidden], axis=1)
        k = (kv_in @ Wk.T).reshape(bsz, total_len, KVH, HD)
        v = (kv_in @ Wv.T).reshape(bsz, total_len, KVH, HD).transpose(0, 2, 1, 3)
        k = _rms_norm(k, k_norm_w).transpose(0, 2, 1, 3)
        full_position_ids = jnp.concatenate([context_position_ids, draft_position_ids], axis=1)
        q = _rope(q, draft_position_ids)
        k = _rope(k, full_position_ids)
        k = jnp.repeat(k, N_REP, axis=1)
        v = jnp.repeat(v, N_REP, axis=1)
        scores = jnp.einsum('bhqd,bhkd->bhqk', q, k) * SCALE
        probs = jax.nn.softmax(scores, axis=-1)
        attn = jnp.einsum('bhqk,bhkd->bhqd', probs, v)
        attn = attn.transpose(0, 2, 1, 3).reshape(bsz, draft_len, H * HD)
        return attn @ Wo.T

    def _L1_ffn_ref(x, w_gate, wi_0, wi_1, wo):
        import jax, jax.numpy as jnp
        import numpy as np
        B, S, D = (4, 256, 256)
        E, K, M = (8, 2, 128)
        b, s, d = x.shape
        e = w_gate.shape[1]
        xf = x.reshape(-1, d)
        logits = jnp.dot(xf, w_gate)
        top_logits, top_idx = jax.lax.top_k(logits, K)
        weights = jax.nn.softmax(top_logits, axis=-1)
        flat_idx = top_idx.reshape(-1)
        sort_order = jnp.argsort(flat_idx)
        token_ids = sort_order // K
        sorted_x = jnp.take(xf, token_ids, axis=0)
        group_sizes = jnp.bincount(flat_idx, length=E).astype(jnp.int32)
        h0 = jax.lax.ragged_dot(sorted_x, wi_0, group_sizes)
        h1 = jax.lax.ragged_dot(sorted_x, wi_1, group_sizes)
        inter = jax.nn.silu(h0) * h1
        out_sorted = jax.lax.ragged_dot(inter, wo, group_sizes)
        unsort = jnp.argsort(sort_order)
        out = jnp.take(out_sorted, unsort, axis=0).reshape(-1, K, d)
        out = jnp.einsum('tkd,tk->td', out, weights)
        return out.reshape(b, s, d)
    x = x + _L0_attn_ref(_layernorm(x, axis=-1), L0_attn_qn_g, L0_attn_qn_b, L0_attn_kvn_g, L0_attn_kvn_b, L0_attn_Wq, L0_attn_bq, L0_attn_Wkv, L0_attn_bkv, L0_attn_Wo, L0_attn_bo, L0_attn_ln_g, L0_attn_ln_b)
    x = x + _L0_xattn_ref(_layernorm(x, axis=-1), ctx_2048, mask_BxS2_bk0)
    x = x + _L0_ffn_ref(_layernorm(x, axis=-1), L0_ffn_w_fc, L0_ffn_w_proj)
    x = x + _L1_attn_ref(_layernorm(x, axis=-1), L1_attn_norm_scale, L1_attn_conv_w, L1_attn_conv_b, L1_attn_in_proj_w, L1_attn_dt_bias, L1_attn_head_mix, L1_attn_out_proj_w)
    x = x + _L1_xattn_ref(_layernorm(x, axis=-1), ctx_2048, L1_xattn_Wq, L1_xattn_Wk, L1_xattn_Wv, L1_xattn_Wo, L1_xattn_q_norm_w, L1_xattn_k_norm_w, pos_BxS2, itok_BxS_4096_4607)
    x = x + _L1_ffn_ref(_layernorm(x, axis=-1), L1_ffn_w_gate, L1_ffn_wi_0, L1_ffn_wi_1, L1_ffn_wo)
    return x

_drawn_inputs = setup_inputs


def setup_inputs(seed=0):
    import zlib

    import numpy as np

    out = dict(_drawn_inputs(seed))
    spreads = {'L0_attn_qn_g': (1.0, 0.6),
     'L0_attn_qn_b': (0.0, 0.8),
     'L0_attn_kvn_g': (1.0, 0.6),
     'L0_attn_kvn_b': (0.0, 0.497),
     'L0_attn_bq': (0.0, 0.477),
     'L0_attn_bkv': (0.0, 0.1),
     'L0_attn_bo': (0.0, 0.1),
     'L0_attn_ln_g': (1.0, 0.6),
     'L0_attn_ln_b': (0.0, 0.8),
     'L1_attn_norm_scale': (1.0, 0.6),
     'L1_attn_conv_b': (0.0, 0.461),
     'L1_xattn_q_norm_w': (1.0, 0.6),
     'L1_xattn_k_norm_w': (1.0, 0.6)}
    factors = {'L1_attn_conv_w': 2.85,
     'L1_attn_dt_bias': 2.848,
     'L1_xattn_Wq': 3.042,
     'L1_xattn_Wk': 3.336}
    for name, (base, spread) in spreads.items():
        noise = np.random.default_rng([zlib.crc32(name.encode()), seed]).standard_normal(out[name].shape)
        drawn = base * np.exp(spread * noise) if base else spread * noise
        out[name] = jnp.asarray(drawn.astype(out[name].dtype))
    for name, factor in factors.items():
        out[name] = (out[name] * factor).astype(out[name].dtype)
    return out
```

```python
import math
from contextlib import ExitStack

import numpy as np

import concourse.bass as bass
from concourse import mybir

ALU = mybir.AluOpType
ACT = mybir.ActivationFunctionType
F32 = mybir.dt.float32
BF16 = mybir.dt.bfloat16
F16 = mybir.dt.float16
I32 = mybir.dt.int32
U32 = mybir.dt.uint32
U8 = mybir.dt.uint8
AX_X = mybir.AxisListType.X

P = 128
BATCH, SEQ, DM = 4, 256, 256
QT = SEQ // P
TILES = BATCH * QT
TOK = BATCH * SEQ
DC = DM // P
CTX = 1601
HEADS = 16
HD0 = DM // HEADS
FF = 4 * DM
FC = FF // P
MASKED = -1.0e30


class Stage:

    def __init__(self, nc, name):
        self.nc, self.name, self.ctx, self.numbers = nc, name, ExitStack(), []

    def __enter__(self):
        self.ctx.__enter__()
        return self

    def __exit__(self, *a):
        if self.numbers and a[0] is None:
            self.rewind()
        return self.ctx.__exit__(*a)

    def sb(self, name, shape, dt=F32):
        return self.ctx.enter_context(self.nc.sbuf_tensor(f"{self.name}_{name}", shape, dt))

    def banks(self):
        return self.ctx.enter_context(self.nc.psum_tensor(f"{self.name}_banks", [P, 8, 512], F32))

    def sem(self, name):
        s = self.ctx.enter_context(self.nc.semaphore(f"{self.name}_{name}"))
        self.numbers.append(s.num)
        return s

    def rewind(self):
        numbers, runs = sorted(self.numbers), []
        for n in numbers:
            if runs and runs[-1][1] == n:
                runs[-1][1] = n + 1
            else:
                runs.append([n, n + 1])
        for first, end in runs:
            self.nc.all_engine_barrier(sems_to_clear=range(first, end))


def chain(engine, sem):
    done = [0]

    def link(ins):
        done[0] += 1
        ins.then_inc(sem, 1)
        engine.wait_ge(sem, done[0])

    return link


def row_stats(nc, link, x, stats, mean_var):
    for t in range(TILES):
        last = nc.vector.bn_stats(stats[:, t, :], x[:, t, :])
    link(last)
    for t in range(TILES):
        last = nc.vector.bn_aggr(mean_var[:, t, :], stats[:, t, :])
    link(last)


def bcast(ap, axis, n):
    shape = list(ap.shape)
    shape.insert(axis, n)
    return ap.unsqueeze(axis).to_broadcast(shape)


def self_attention(nc, x, const, w):
    with Stage(nc, "self") as st:
        sb, sem = st.sb, st.sem
        ps = st.banks()
        w_qk = sb("w_qk", [P, DC, 2 * DM])
        w_v = sb("w_v", [P, DC, DM])
        w_o = sb("w_o", [P, DC, DM])
        b_qk = sb("b_qk", [P, 2 * DM])
        b_v = sb("b_v", [P, DM])
        b_o = sb("b_o", [P, DM])
        gains = sb("gains", [P, 4, DC])
        ln_g = sb("ln_g", [P, HD0])
        ln_b = sb("ln_b", [P, HD0])
        cos = sb("cos", [P, QT, HD0 // 2])
        sin = sb("sin", [P, QT, HD0 // 2])
        causal = sb("causal", [P, SEQ])
        stats = sb("stats", [P, TILES, 6])
        mean_var = sb("mean_var", [P, TILES, 2])
        rs = sb("rs", [P, 6, TILES])
        half = sb("half", [P, 2, TILES])
        xn = sb("xn", [P, TILES, DM])
        qin_t = sb("qin_t", [P, DC, TOK])
        kvin_t = sb("kvin_t", [P, DC, TOK])
        qk = sb("qk", [P, TILES, 2 * DM])
        v = sb("v", [P, TILES, DM])
        turn = sb("turn", [P, 2, HD0 // 2])
        by_cos = sb("by_cos", [P, 2 * HEADS, HD0 // 2, 2])
        by_sin = sb("by_sin", [P, 2 * HEADS, HD0 // 2, 2])
        rot = sb("rot", [P, 2 * HEADS, HD0])
        hstat = sb("hstat", [P, 4, 2 * HEADS])
        hpow = sb("hpow", [P, 2 * HEADS])
        padded = sb("padded", [P, 2, 2 * HEADS, 32])
        q_t = sb("q_t", [P, 4, TOK])
        k_own = sb("k_own", [P, 4, 4, TOK])
        sm = sb("sm", [P, 2, 4, SEQ])
        mx = sb("mx", [P, 2, 4])
        shift = sb("shift", [P, 2, 4])
        sums = sb("sums", [P, TILES, HEADS])
        inv = sb("inv", [P, TILES, HEADS])
        p_t = sb("p_t", [P, 2, 8, P])
        att = sb("att", [P, TILES, DM])
        att_t = sb("att_t", [P, DC, TOK])

        loaded = sem("weights_loaded")
        dve_step, rs_ready, rs_done = sem("dve_step"), sem("rs_ready"), sem("rs_done")
        xn_ready, xt_ready, qin_ready, kvin_ready = sem("xn_ready"), sem("xt_ready"), sem("qin_ready"), sem("kvin_ready")
        qkv_ready, qkv_taken = sem("qkv_ready"), sem("qkv_taken")
        hvar_ready, hrs_done = sem("hvar_ready"), sem("hrs_done")
        padded_ready, padded_t, qkt_ready = sem("padded_ready"), sem("padded_t"), sem("qkt_ready")
        scores_ready, scores_taken, shift_ready, probs_ready = sem("scores_ready"), sem("scores_taken"), sem("shift_ready"), sem("probs_ready")
        probs_t, pt_ready, att_ready = sem("probs_t"), sem("pt_ready"), sem("att_ready")
        att_tr, attt_ready, out_ready, out_taken = sem("att_tr"), sem("attt_ready"), sem("out_ready"), sem("out_taken")
        pv_done, zeroed = sem("pv_done"), sem("zeroed")

        GROUPS = HEADS // 4
        JOBS = TILES * GROUPS

        def keys(job):
            return P * (job // GROUPS % QT + 1)

        with nc.Block() as block:
            @block.sync
            def _(sp):
                for dst, src in (
                    (gains[:, 0, :], w["qn_g"]),
                    (gains[:, 1, :], w["qn_b"]),
                    (gains[:, 2, :], w["kvn_g"]),
                    (gains[:, 3, :], w["kvn_b"]),
                    (w_qk[:, :, 0:DM], w["Wq"].rearrange("(c p) n -> p c n", p=P)),
                    (w_qk[:, :, DM:2 * DM], w["Wkv"][:, 0:DM].rearrange("(c p) n -> p c n", p=P)),
                    (w_v[:], w["Wkv"][:, DM:2 * DM].rearrange("(c p) n -> p c n", p=P)),
                    (b_qk[:, 0:DM], w["bq"].partition_broadcast(P)),
                    (b_qk[:, DM:2 * DM], w["bkv"][0:DM].partition_broadcast(P)),
                    (b_v[:], w["bkv"][DM:2 * DM].partition_broadcast(P)),
                    (b_o[:], w["bo"].partition_broadcast(P)),
                    (ln_g[:], w["ln_g"].partition_broadcast(P)),
                    (ln_b[:], w["ln_b"].partition_broadcast(P)),
                    (cos[:], w["cos"]), (sin[:], w["sin"]), (causal[:], w["causal"]),
                    (w_o[:], w["Wo"].rearrange("(c p) n -> p c n", p=P)),
                ):
                    sp.dma_start(dst, src).then_inc(loaded, 16)

            @block.gpsimd
            def _(gp):
                nc.gpsimd.memset(k_own[:], 0.0).then_inc(zeroed, 1)
                gp.wait_ge(rs_ready, 1)
                nc.gpsimd.tensor_tensor(rs[:, 1, :], rs[:, 0, :], half[:, 0, :], ALU.pow).then_inc(rs_done, 1)
                gp.wait_ge(rs_ready, 2)
                nc.gpsimd.tensor_tensor(rs[:, 3, :], rs[:, 2, :], half[:, 0, :], ALU.pow).then_inc(rs_done, 1)
                gp.wait_ge(rs_ready, 3)
                nc.gpsimd.tensor_tensor(rs[:, 5, :], rs[:, 4, :], half[:, 1, :], ALU.pow).then_inc(rs_done, 1)
                for t in range(TILES):
                    gp.wait_ge(hvar_ready, t + 1)
                    nc.gpsimd.tensor_tensor(hstat[:, 3, :], hstat[:, 2, :], hpow[:], ALU.pow).then_inc(hrs_done, 1)

            @block.vector
            def _(ve):
                link = chain(ve, dve_step)
                nc.vector.memset(half[:, 0, :], -0.5)
                nc.vector.memset(half[:, 1, :], 0.5)
                nc.vector.memset(hpow[:], -0.5)
                nc.vector.memset(padded[:], 0.0)
                row_stats(nc, link, x, stats, mean_var)
                nc.vector.tensor_scalar(rs[:, 0, :], mean_var[:, :, 1], 1e-5, None, ALU.add).then_inc(rs_ready, 1)
                ve.wait_ge(rs_done, 1)
                link(nc.vector.tensor_tensor(rs[:, 2, :], rs[:, 1, :], rs[:, 1, :], ALU.mult))
                link(nc.vector.tensor_tensor(rs[:, 4, :], rs[:, 2, :], mean_var[:, :, 1], ALU.mult))
                nc.vector.tensor_scalar(rs[:, 2, :], rs[:, 4, :], 1e-5, None, ALU.add).then_inc(rs_ready, 1)
                ve.wait_ge(rs_done, 2)
                nc.vector.tensor_scalar(rs[:, 4, :], rs[:, 4, :], float(DM), None, ALU.mult).then_inc(rs_ready, 1)
                ve.wait_ge(rs_done, 3)
                link(nc.vector.tensor_tensor(rs[:, 2, :], rs[:, 1, :], rs[:, 3, :], ALU.mult))
                link(nc.vector.tensor_scalar(rs[:, 5, :], rs[:, 5, :], float(HD0) ** -0.25, None, ALU.mult))
                for t in range(TILES):
                    nc.vector.tensor_scalar(xn[:, t, :], x[:, t, :], mean_var[:, t, 0:1], rs[:, 2, t:t + 1],
                                            ALU.subtract, ALU.mult).then_inc(xn_ready, 1)
                ve.wait_ge(loaded, 16 * 17)
                for b in range(BATCH):
                    ve.wait_ge(xt_ready, b + 1)
                    for c in range(DC):
                        last = nc.vector.tensor_scalar(kvin_t[:, c, b * SEQ:(b + 1) * SEQ], ps[:, b, c * SEQ:(c + 1) * SEQ],
                                                       gains[:, 2, c:c + 1], gains[:, 3, c:c + 1], ALU.mult, ALU.add)
                    last.then_inc(kvin_ready, 1)

                def take_qkv(t):
                    ve.wait_ge(qkv_ready, t + 1)
                    nc.vector.tensor_tensor(qk[:, t, :], ps[:, 4 + t % 2, :], b_qk[:], ALU.add)
                    ins = nc.vector.tensor_tensor(v[:, t, :], ps[:, 6 + t % 2, 0:DM], b_v[:], ALU.add)
                    ins.then_inc(qkv_taken, 1)
                    ve.wait_ge(qkv_taken, t + 1)

                take_qkv(0)
                for t in range(TILES):
                    if t + 1 < TILES:
                        take_qkv(t + 1)
                    nc.vector.tensor_scalar(turn[:, 0, :], cos[:, t % QT, :], rs[:, 5, t:t + 1], None, ALU.mult)
                    link(nc.vector.tensor_scalar(turn[:, 1, :], sin[:, t % QT, :], rs[:, 5, t:t + 1], None, ALU.mult))
                    qk_v = qk[:, t, :].rearrange("p (h d e) -> p h d e", h=2 * HEADS, e=2)
                    wide = [P, 2 * HEADS, HD0 // 2, 2]
                    nc.vector.tensor_tensor(by_cos[:], qk_v, turn[:, 0, :].unsqueeze(1).unsqueeze(3).to_broadcast(wide), ALU.mult)
                    link(nc.vector.tensor_tensor(by_sin[:], qk_v, turn[:, 1, :].unsqueeze(1).unsqueeze(3).to_broadcast(wide), ALU.mult))
                    rot_v = rot[:].rearrange("p h (d e) -> p h d e", e=2)
                    nc.vector.tensor_tensor(rot_v[:, :, :, 0], by_cos[:, :, :, 0], by_sin[:, :, :, 1], ALU.subtract)
                    link(nc.vector.tensor_tensor(rot_v[:, :, :, 1], by_cos[:, :, :, 1], by_sin[:, :, :, 0], ALU.add))
                    link(nc.vector.tensor_reduce(hstat[:, 0, :], rot[:], AX_X, ALU.add))
                    link(nc.vector.tensor_scalar(hstat[:, 1, :], hstat[:, 0, :], 1.0 / HD0, None, ALU.mult))
                    link(nc.vector.tensor_tensor(rot[:], rot[:], bcast(hstat[:, 1, :], 2, HD0), ALU.subtract))
                    sq = by_cos[:].rearrange("p h d e -> p h (d e)")
                    link(nc.vector.tensor_tensor(sq, rot[:], rot[:], ALU.mult))
                    link(nc.vector.tensor_reduce(hstat[:, 0, :], sq, AX_X, ALU.add))
                    nc.vector.tensor_scalar(hstat[:, 2, :], hstat[:, 0, :], 1.0 / HD0, 1e-5, ALU.mult, ALU.add).then_inc(hvar_ready, 1)
                    link(nc.vector.tensor_tensor(sq, rot[:], bcast(ln_g[:], 1, 2 * HEADS), ALU.mult))
                    ve.wait_ge(hrs_done, t + 1)
                    link(nc.vector.tensor_tensor(rot[:], sq, bcast(hstat[:, 3, :], 2, HD0), ALU.mult))
                    if t >= 2:
                        ve.wait_ge(padded_t, t - 1)
                    ins = nc.vector.tensor_tensor(padded[:, t % 2, :, 0:HD0], rot[:], bcast(ln_b[:], 1, 2 * HEADS), ALU.add)
                    ins.then_inc(padded_ready, 1)
                    ve.wait_ge(padded_ready, t + 1)

                def normalise(t):
                    ve.wait_ge(pv_done, GROUPS * (t + 1))
                    link(nc.vector.reciprocal(inv[:, t, :], sums[:, t, :]))
                    nc.vector.tensor_tensor(att[:, t, :].rearrange("p (h d) -> p h d", h=HEADS),
                                            ps[:, 2 + t % 2, 0:DM].rearrange("p (h d) -> p h d", h=HEADS),
                                            bcast(inv[:, t, :], 2, HD0), ALU.mult).then_inc(att_ready, 1)

                for j in range(JOBS):
                    nk, k = keys(j), j % 2
                    ve.wait_ge(scores_ready, j + 1)
                    if j >= 2:
                        ve.wait_ge(probs_t, j - 1)
                    ins = nc.vector.tensor_tensor(sm[:, k, :, 0:nk],
                                                  ps[:, 4 + 2 * k:6 + 2 * k, :].rearrange("p a (h n) -> p (a h) n", h=2)[:, :, 0:nk],
                                                  bcast(causal[:, SEQ - nk:SEQ], 1, 4), ALU.add)
                    ins.then_inc(scores_taken, 1)
                    ve.wait_ge(scores_taken, j + 1)
                    link(nc.vector.tensor_reduce(mx[:, k, :], sm[:, k, :, 0:nk], AX_X, ALU.max))
                    nc.vector.tensor_scalar(shift[:, k, :], mx[:, k, :], -float(HD0) ** -0.5, None, ALU.mult).then_inc(shift_ready, 1)
                    if j % GROUPS == 2 and j > GROUPS:
                        normalise(j // GROUPS - 1)
                normalise(TILES - 1)
                for t in range(TILES):
                    ve.wait_ge(out_ready, t + 1)
                    ins = nc.vector.tensor_tensor(att[:, t, :], ps[:, 4 + t % 4, 0:DM], b_o[:], ALU.add)
                    ins.then_inc(out_taken, 1)
                    ve.wait_ge(out_taken, t + 1)
                    link(nc.vector.tensor_tensor(x[:, t, :], att[:, t, :], x[:, t, :], ALU.add))

            @block.scalar
            def _(ac):
                ac.wait_ge(loaded, 16 * 17)
                for b in range(BATCH):
                    ac.wait_ge(kvin_ready, b + 1)
                    for c in range(DC):
                        last = nc.scalar.activation(qin_t[:, c, b * SEQ:(b + 1) * SEQ], ps[:, b, c * SEQ:(c + 1) * SEQ],
                                                    ACT.Identity, bias=gains[:, 1, c:c + 1], scale=gains[:, 0, c:c + 1])
                    last.then_inc(qin_ready, 1)
                ac.wait_ge(zeroed, 1)
                for t in range(TILES):
                    ac.wait_ge(padded_t, t + 1)
                    bank = ps[:, 2 * (t % 2):2 * (t % 2) + 2, :].rearrange("p a (g n) -> p a g n", g=4)
                    nc.scalar.copy(q_t[:, :, t * P:(t + 1) * P], bank[:, 0])
                    for i in range(4):
                        rows = slice(32 * i, 32 * i + 32)
                        last = nc.scalar.copy(k_own[rows, :, i, t * P:(t + 1) * P], bank[rows, 1])
                    last.then_inc(qkt_ready, 1)

                def copy_pt(j):
                    ac.wait_ge(probs_t, j + 1)
                    if j >= 2:
                        ac.wait_ge(pv_done, j - 1)
                    n = 4 * keys(j) // P
                    nc.scalar.copy(p_t[:, j % 2, 0:n, :],
                                   ps[:, 0:2, :].rearrange("p a (g n) -> p (a g) n", g=4)[:, 0:n, :]).then_inc(pt_ready, 1)

                for j in range(JOBS):
                    k, nk, t = j % 2, keys(j), j // GROUPS
                    ac.wait_ge(shift_ready, j + 1)
                    for i in range(4):
                        h = j % GROUPS * 4 + i
                        last = nc.scalar.activation(sm[:, k, i, 0:nk], sm[:, k, i, 0:nk], ACT.Exp, bias=shift[:, k, i:i + 1],
                                                    scale=float(HD0) ** -0.5, accum_out=sums[:, t, h:h + 1])
                    last.then_inc(probs_ready, 1)
                    if j >= 1:
                        copy_pt(j - 1)
                copy_pt(JOBS - 1)
                for b in range(BATCH):
                    ac.wait_ge(att_tr, b + 1)
                    nc.scalar.copy(att_t[:, :, b * SEQ:(b + 1) * SEQ],
                                   ps[:, b, :].rearrange("p (c n) -> p c n", c=DC)).then_inc(attt_ready, 1)

            @block.tensor
            def _(pe):
                for b in range(BATCH):
                    pe.wait_ge(xn_ready, 2 * b + 2)
                    for c in range(DC):
                        for q in range(QT):
                            last = nc.tensor.transpose(ps[:, b, c * SEQ + q * P:c * SEQ + (q + 1) * P],
                                                       xn[:, b * QT + q, c * P:(c + 1) * P], const["ident"][:])
                    last.then_inc(xt_ready, 1)
                def project(t):
                    pe.wait_ge(qin_ready, t // QT + 1)
                    pe.wait_ge(kvin_ready, t // QT + 1)
                    if t >= 2:
                        pe.wait_ge(qkv_taken, t - 1)
                    tok = slice(t * P, (t + 1) * P)
                    for dst, src, wt in ((ps[:, 4 + t % 2, 0:DM], qin_t, w_qk[:, :, 0:DM]),
                                         (ps[:, 4 + t % 2, DM:2 * DM], kvin_t, w_qk[:, :, DM:2 * DM]),
                                         (ps[:, 6 + t % 2, 0:DM], kvin_t, w_v)):
                        for c in range(DC):
                            last = nc.tensor.matmul(dst, src[:, c, tok], wt[:, c, :], start=(c == 0), stop=(c == DC - 1))
                    last.then_inc(qkv_ready, 1)

                def turn_heads(t):
                    pe.wait_ge(padded_ready, t + 1)
                    if t >= 2:
                        pe.wait_ge(qkt_ready, t - 1)
                    for g in range(8):
                        last = nc.tensor.transpose(ps[:, 2 * (t % 2) + g // 4, g % 4 * P:(g % 4 + 1) * P],
                                                   padded[:, t % 2, 4 * g:4 * g + 4, :].rearrange("p h d -> p (h d)"),
                                                   const["ident"][:])
                    last.then_inc(padded_t, 1)

                for t in range(TILES):
                    project(t)
                    if t == 2:
                        pe.wait_ge(qin_ready, BATCH)
                    if t >= 2:
                        turn_heads(t - 2)
                turn_heads(TILES - 2)
                turn_heads(TILES - 1)
                pe.wait_ge(qkt_ready, TILES)

                def score(j):
                    t, g, nk = j // GROUPS, j % GROUPS, keys(j)
                    if j >= 2:
                        pe.wait_ge(scores_taken, j - 1)
                    for half_group in range(2):
                        keep = slice(2 * half_group, 2 * half_group + 2)
                        last = nc.tensor.matmul(
                            ps[:, 4 + 2 * (j % 2) + half_group, :].rearrange("p (h n) -> p h n", h=2)[:, :, 0:nk],
                            q_t[:, g, t * P:(t + 1) * P],
                            k_own[:, g, keep, t // QT * SEQ:t // QT * SEQ + nk], start=True, stop=True)
                    last.then_inc(scores_ready, 1)

                def weigh(j):
                    t, g, n = j // GROUPS, j % GROUPS, keys(j) // P
                    pe.wait_ge(probs_ready, j + 1)
                    if j >= 1:
                        pe.wait_ge(pt_ready, j)
                    for i in range(4):
                        for c in range(n):
                            s = i * n + c
                            last = nc.tensor.transpose(ps[:, s // 4, s % 4 * P:(s % 4 + 1) * P],
                                                       sm[:, j % 2, i, c * P:(c + 1) * P], const["ident"][:])
                    last.then_inc(probs_t, 1)
                    pe.wait_ge(pt_ready, j + 1)
                    if g == 0 and t >= 2:
                        pe.wait_ge(att_ready, t - 1)
                    for i in range(4):
                        h = 4 * g + i
                        for c in range(n):
                            last = nc.tensor.matmul(ps[:, 2 + t % 2, h * HD0:(h + 1) * HD0], p_t[:, j % 2, i * n + c, :],
                                                    v[:, t // QT * QT + c, h * HD0:(h + 1) * HD0],
                                                    start=(c == 0), stop=(c == n - 1))
                    last.then_inc(pv_done, 1)

                pe.wait_ge(qkv_taken, TILES)
                score(0)
                for j in range(JOBS):
                    if j + 1 < JOBS:
                        score(j + 1)
                    weigh(j)
                for b in range(BATCH):
                    pe.wait_ge(att_ready, TILES)
                    for c in range(DC):
                        for q in range(QT):
                            last = nc.tensor.transpose(ps[:, b, c * SEQ + q * P:c * SEQ + (q + 1) * P],
                                                       att[:, b * QT + q, c * P:(c + 1) * P], const["ident"][:])
                    last.then_inc(att_tr, 1)
                for t in range(TILES):
                    pe.wait_ge(attt_ready, t // QT + 1)
                    if t >= 4:
                        pe.wait_ge(out_taken, t - 3)
                    for c in range(DC):
                        last = nc.tensor.matmul(ps[:, 4 + t % 4, 0:DM], att_t[:, c, t * P:(t + 1) * P], w_o[:, c, :],
                                                start=(c == 0), stop=(c == DC - 1))
                    last.then_inc(out_ready, 1)


CTX_FULL = CTX // P
CTX_REST = CTX - CTX_FULL * P
CTX_TILES = CTX_FULL + 1


def memory_attention(nc, x, const, a):
    with Stage(nc, "memory") as st:
        sb, sem = st.sb, st.sem
        ps = st.banks()
        ctx_t = sb("ctx_t", [P, BATCH, DC, CTX])
        ctx = sb("ctx", [P, BATCH, CTX_TILES, DM])
        flags = sb("flags", [BATCH, CTX], U8)
        barred = sb("barred", [BATCH, CTX], BF16)
        pick_raw = sb("pick_raw", [BATCH, BATCH, P])
        pick = sb("pick", [BATCH, BATCH, P], BF16)
        stats = sb("stats", [P, TILES, 6])
        mean_var = sb("mean_var", [P, TILES, 2])
        rs = sb("rs", [P, 6, TILES])
        half = sb("half", [P, TILES])
        xn = sb("xn", [P, TILES, DM])
        xn_t = sb("xn_t", [P, DC, TOK])
        mx = sb("mx", [P, TILES])
        shift = sb("shift", [P, TILES])
        sums = sb("sums", [P, TILES])
        seen = sb("seen", [P, TILES])
        gain = sb("gain", [P, TILES])
        probs = sb("probs", [P, 2, CTX])
        p_t = sb("p_t", [P, 2, 4, P])

        loaded = [sem(f"ctx_loaded{b}") for b in range(BATCH)]
        mask_loaded, barred_ready = sem("mask_loaded"), sem("barred_ready")
        dve_step, rs_ready, rs_done = sem("dve_step"), sem("rs_ready"), sem("rs_done")
        xn_ready, xt_ready, xnt_ready = sem("xn_ready"), sem("xt_ready"), sem("xnt_ready")
        scores_ready, shift_ready, probs_ready = sem("scores_ready"), sem("shift_ready"), sem("probs_ready")
        turned, pt_ready, pv_done, added = sem("turned"), sem("pt_ready"), sem("pv_done"), sem("added")
        SCALE = float(DM) ** -0.5
        CHUNKS = [(s, min(512, CTX - s)) for s in range(0, CTX, 512)]

        def scores(t):
            return ps[:, 0:4, :].rearrange("p a n -> p (a n)")[:, 0:CTX]

        with nc.Block() as block:
            @block.sync
            def _(sp):
                sp.dma_start(flags[:], a["mask_BxS2_bk0"]).then_inc(mask_loaded, 16)
                sp.dma_start(pick_raw[:], a["c_pick"]).then_inc(mask_loaded, 16)
                for b in range(BATCH):
                    sp.dma_start(ctx_t[:, b], a["ctx_t"][b].rearrange("(c p) n -> p c n", p=P)).then_inc(loaded[b], 16)
                    sp.dma_start(ctx[:, b, 0:CTX_FULL, :], a["ctx_2048"][b, 0:CTX_FULL * P, :].rearrange("(t p) d -> p t d", p=P))\
                        .then_inc(loaded[b], 16)
                    sp.dma_start(ctx[0:CTX_REST, b, CTX_FULL, :], a["ctx_2048"][b, CTX_FULL * P:CTX, :]).then_inc(loaded[b], 16)

            @block.gpsimd
            def _(gp):
                nc.gpsimd.memset(half[:], -0.5).then_inc(rs_done, 1)
                gp.wait_ge(rs_done, 1)
                gp.wait_ge(rs_ready, 1)
                nc.gpsimd.tensor_tensor(rs[:, 1, :], rs[:, 0, :], half[:], ALU.pow).then_inc(rs_done, 1)

            @block.vector
            def _(ve):
                link = chain(ve, dve_step)
                row_stats(nc, link, x, stats, mean_var)
                nc.vector.tensor_scalar(rs[:, 0, :], mean_var[:, :, 1], 1e-5, None, ALU.add).then_inc(rs_ready, 1)
                ve.wait_ge(rs_done, 2)
                for t in range(TILES):
                    nc.vector.tensor_scalar(xn[:, t, :], x[:, t, :], mean_var[:, t, 0:1], rs[:, 1, t:t + 1],
                                            ALU.subtract, ALU.mult).then_inc(xn_ready, 1)
                ve.wait_ge(mask_loaded, 32)
                nc.vector.tensor_copy(pick[:], pick_raw[:])
                nc.vector.tensor_scalar(barred[:], flags[:], -MASKED, MASKED, ALU.mult, ALU.add).then_inc(barred_ready, 1)

                def add_read(t):
                    ve.wait_ge(probs_ready, t + 1)
                    nc.vector.tensor_scalar(seen[:, t:t + 1], mx[:, t:t + 1], MASKED / 2, None, ALU.is_gt)
                    link(nc.vector.reciprocal(gain[:, t:t + 1], sums[:, t:t + 1]))
                    link(nc.vector.tensor_tensor(gain[:, t:t + 1], gain[:, t:t + 1], seen[:, t:t + 1], ALU.mult))
                    ve.wait_ge(pv_done, 4 * (t + 1))
                    nc.vector.scalar_tensor_tensor(x[:, t, :], ps[:, 6 + t % 2, 0:DM], gain[:, t:t + 1], x[:, t, :],
                                                   ALU.mult, ALU.add).then_inc(added, 1)

                for t in range(TILES):
                    ve.wait_ge(scores_ready, t + 1)
                    link(nc.vector.tensor_reduce(mx[:, t:t + 1], scores(t), AX_X, ALU.max))
                    nc.vector.tensor_scalar(shift[:, t:t + 1], mx[:, t:t + 1], -SCALE, None, ALU.mult).then_inc(shift_ready, 1)
                    if t >= 1:
                        add_read(t - 1)
                add_read(TILES - 1)

            @block.scalar
            def _(ac):
                for b in range(BATCH):
                    ac.wait_ge(xt_ready, b + 1)
                    nc.scalar.copy(xn_t[:, :, b * SEQ:(b + 1) * SEQ],
                                   ps[:, 4 + b, :].rearrange("p (c n) -> p c n", c=DC)).then_inc(xnt_ready, 1)
                for t in range(TILES):
                    ac.wait_ge(shift_ready, t + 1)
                    if t >= 2:
                        ac.wait_ge(turned, 4 * (t - 1))
                    nc.scalar.activation(probs[:, t % 2, :], scores(t), ACT.Exp, bias=shift[:, t:t + 1], scale=SCALE,
                                         accum_out=sums[:, t:t + 1]).then_inc(probs_ready, 1)
                    for g in range(4):
                        n = 4 * t + g
                        ac.wait_ge(turned, n + 1)
                        if n >= 2:
                            ac.wait_ge(pv_done, n - 1)
                        if g < 3:
                            nc.scalar.copy(p_t[:, n % 2], ps[:, 4 + n % 2, :].rearrange("p (c n) -> p c n", c=4)).then_inc(pt_ready, 1)
                        else:
                            nc.scalar.copy(p_t[0:CTX_REST, n % 2, 0, :], ps[0:CTX_REST, 4 + n % 2, 0:P]).then_inc(pt_ready, 1)

            @block.tensor
            def _(pe):
                for b in range(BATCH):
                    pe.wait_ge(xn_ready, 2 * b + 2)
                    for c in range(DC):
                        for q in range(QT):
                            last = nc.tensor.transpose(ps[:, 4 + b, c * SEQ + q * P:c * SEQ + (q + 1) * P],
                                                       xn[:, b * QT + q, c * P:(c + 1) * P], const["ident"][:])
                    last.then_inc(xt_ready, 1)
                pe.wait_ge(barred_ready, 1)
                pe.wait_ge(xnt_ready, BATCH)

                def score(t):
                    b = t // QT
                    if t % QT == 0:
                        pe.wait_ge(loaded[b], 48)
                    if t >= 1:
                        pe.wait_ge(probs_ready, t)
                    for i, (s, n) in enumerate(CHUNKS):
                        for c in range(DC):
                            nc.tensor.matmul(ps[:, i, 0:n], xn_t[:, c, t * P:(t + 1) * P], ctx_t[:, b, c, s:s + n],
                                             start=(c == 0), stop=False)
                        last = nc.tensor.matmul(ps[:, i, 0:n], pick[:, b, :], barred[:, s:s + n], start=False, stop=True)
                    last.then_inc(scores_ready, 1)

                def turn(t, g):
                    n = 4 * t + g
                    if n >= 2:
                        pe.wait_ge(pt_ready, n - 1)
                    for i in range(4 if g < 3 else 1):
                        k = 4 * g + i
                        w = min(P, CTX - k * P)
                        last = nc.tensor.transpose(ps[0:w, 4 + n % 2, i * P:(i + 1) * P], probs[:, t % 2, k * P:k * P + w],
                                                   const["ident"][:])
                    last.then_inc(turned, 1)

                def read(t, g):
                    n = 4 * t + g
                    pe.wait_ge(pt_ready, n + 1)
                    if g == 0 and t >= 2:
                        pe.wait_ge(added, t - 1)
                    for i in range(4 if g < 3 else 1):
                        k = 4 * g + i
                        w = min(P, CTX - k * P)
                        last = nc.tensor.matmul(ps[:, 6 + t % 2, 0:DM], p_t[0:w, n % 2, i, :], ctx[0:w, t // QT, k, :],
                                                start=(k == 0), stop=(k == CTX_TILES - 1))
                    last.then_inc(pv_done, 1)

                score(0)
                for t in range(TILES):
                    pe.wait_ge(probs_ready, t + 1)
                    turn(t, 0)
                    turn(t, 1)
                    if t + 1 < TILES:
                        score(t + 1)
                    read(t, 0)
                    turn(t, 2)
                    read(t, 1)
                    turn(t, 3)
                    read(t, 2)
                    read(t, 3)


def ternary_ffn(nc, x, const, a):
    with Stage(nc, "ffn") as st:
        sb, sem = st.sb, st.sem
        ps = st.banks()
        CLIP = 128.0 - 1e-6
        raw = [sb("raw_fc", [P, DC, FF]), sb("raw_proj", [P, FC, DM])]
        tern = [sb("tern_fc", [P, DC, FF], F16), sb("tern_proj", [P, FC, DM], F16)]
        below = sb("below", [P, DC * FF], F16)
        ones = sb("ones", [P, P])
        size = sb("size", [P, 2])
        mean_size = sb("mean_size", [P, 2])
        per_size = sb("per_size", [P, 2])
        stats = sb("stats", [P, TILES, 6])
        mean_var = sb("mean_var", [P, TILES, 2])
        rs = sb("rs", [P, 6, TILES])
        half = sb("half", [P, TILES])
        rows = sb("rows", [P, TILES, DM])
        top = sb("top", [P, 3, TILES])
        rows_hi = sb("rows_hi", [P, DC, TOK], F16)
        rows_lo = sb("rows_lo", [P, DC, TOK], F16)
        h = sb("h", [P, 2, FF])
        hstats = sb("hstats", [P, TILES, 2, 6])
        hmv = sb("hmv", [P, TILES, 2])
        hvar = sb("hvar", [P, 2, TILES])
        htop = sb("htop", [P, 3, TILES])
        h_hi = sb("h_hi", [P, 2, FC, P], F16)
        h_lo = sb("h_lo", [P, 2, FC, P], F16)

        loaded = sem("weights_loaded")
        dve_step, rs_ready, rs_done = sem("dve_step"), sem("rs_ready"), sem("rs_done")
        ones_ready, sizes_ready, size_spread, size_ready, tern_ready = sem("ones_ready"), sem("sizes_ready"), sem("size_spread"), sem("size_ready"), sem("tern_ready")
        rows_ready, rows_t, hi_ready, lo_ready = sem("rows_ready"), sem("rows_t"), sem("hi_ready"), sem("lo_ready")
        up_ready, h_ready, hvar_ready, hvar_done = sem("up_ready"), sem("h_ready"), sem("hvar_ready"), sem("hvar_done")
        h_clipped, h_t, hhi_ready, hlo_ready = sem("h_clipped"), sem("h_t"), sem("hhi_ready"), sem("hlo_ready")
        down_ready, added = sem("down_ready"), sem("added")

        with nc.Block() as block:
            @block.sync
            def _(sp):
                sp.dma_start(raw[0][:], a["L0_ffn_w_fc"].rearrange("(c p) n -> p c n", p=P)).then_inc(loaded, 16)
                sp.dma_start(raw[1][:], a["L0_ffn_w_proj"].rearrange("(c p) n -> p c n", p=P)).then_inc(loaded, 16)

            @block.gpsimd
            def _(gp):
                nc.gpsimd.memset(half[:], -0.5)
                nc.gpsimd.memset(ones[:], 1.0).then_inc(ones_ready, 1)
                gp.wait_ge(ones_ready, 1)
                for i in range(2):
                    gp.wait_ge(rs_ready, i + 1)
                    nc.gpsimd.tensor_tensor(rs[:, 2 * i + 1, :], rs[:, 2 * i, :], half[:], ALU.pow).then_inc(rs_done, 1)
                for t in range(TILES):
                    gp.wait_ge(hvar_ready, t + 1)
                    nc.gpsimd.tensor_tensor(hvar[:, 1, t:t + 1], hvar[:, 0, t:t + 1], half[:, 0:1], ALU.pow).then_inc(hvar_done, 1)

            @block.vector
            def _(ve):
                link = chain(ve, dve_step)
                row_stats(nc, link, x, stats, mean_var)
                nc.vector.tensor_scalar(rs[:, 0, :], mean_var[:, :, 1], 1e-5, None, ALU.add).then_inc(rs_ready, 1)
                ve.wait_ge(rs_done, 1)
                link(nc.vector.tensor_tensor(rs[:, 4, :], rs[:, 1, :], rs[:, 1, :], ALU.mult))
                link(nc.vector.tensor_tensor(rs[:, 5, :], rs[:, 4, :], mean_var[:, :, 1], ALU.mult))
                nc.vector.tensor_scalar(rs[:, 2, :], rs[:, 5, :], 1e-6, None, ALU.add).then_inc(rs_ready, 1)
                ve.wait_ge(loaded, 32)
                nc.vector.tensor_reduce(size[:, 0:1], raw[0][:].rearrange("p c n -> p (c n)"), AX_X, ALU.add, apply_absolute_value=True)
                nc.vector.tensor_reduce(size[:, 1:2], raw[1][:].rearrange("p c n -> p (c n)"), AX_X, ALU.add,
                                        apply_absolute_value=True).then_inc(sizes_ready, 1)
                ve.wait_ge(rs_done, 2)
                link(nc.vector.tensor_tensor(rs[:, 4, :], rs[:, 1, :], rs[:, 3, :], ALU.mult))

                def clip(dst, src, marks, t):
                    link(nc.vector.tensor_reduce(marks[:, 0, t:t + 1], src, AX_X, ALU.max, apply_absolute_value=True))
                    link(nc.vector.reciprocal(marks[:, 1, t:t + 1], marks[:, 0, t:t + 1]))
                    nc.vector.tensor_scalar(marks[:, 2, t:t + 1], marks[:, 0, t:t + 1], 1.0 / 128.0, None, ALU.mult)
                    link(nc.vector.tensor_scalar(marks[:, 1, t:t + 1], marks[:, 1, t:t + 1], 128.0, None, ALU.mult))
                    link(nc.vector.tensor_scalar(dst, src, marks[:, 1, t:t + 1], CLIP, ALU.mult, ALU.min))
                    return nc.vector.tensor_scalar(dst, dst, -CLIP, marks[:, 2, t:t + 1], ALU.max, ALU.mult)

                def rest(b):
                    ve.wait_ge(hi_ready, b + 1)
                    tok = slice(b * SEQ, (b + 1) * SEQ)
                    nc.vector.tensor_tensor(rows_lo[:, :, tok], ps[:, b % 2, :].rearrange("p (c n) -> p c n", c=DC),
                                            rows_hi[:, :, tok], ALU.subtract).then_inc(lo_ready, 1)

                for t in range(TILES):
                    link(nc.vector.tensor_scalar(rows[:, t, :], x[:, t, :], mean_var[:, t, 0:1], rs[:, 4, t:t + 1],
                                                 ALU.subtract, ALU.mult))
                    clip(rows[:, t, :], rows[:, t, :], top, t).then_inc(rows_ready, 1)
                    if t % 2 == 1 and t > 2:
                        rest(t // 2 - 1)
                rest(BATCH - 1)
                ve.wait_ge(size_spread, 1)
                link(nc.vector.tensor_scalar(mean_size[:], ps[:, 7, 0:2], 1.0 / (FF * DM), None, ALU.mult))
                link(nc.vector.tensor_scalar(per_size[:], mean_size[:], 1e-6, None, ALU.add))
                link(nc.vector.reciprocal(per_size[:], per_size[:]))
                for i in range(2):
                    flat = [r[:].rearrange("p c n -> p (c n)") for r in (raw[i], tern[i])]
                    nc.vector.tensor_scalar(below[:], flat[0], per_size[:, i:i + 1], -0.5, ALU.mult, ALU.is_lt)
                    link(nc.vector.tensor_scalar(flat[1], flat[0], per_size[:, i:i + 1], 0.5, ALU.mult, ALU.is_gt))
                    ins = nc.vector.tensor_tensor(flat[1], flat[1], below[:], ALU.subtract)
                    ins.then_inc(tern_ready, 1)
                    ve.wait_ge(tern_ready, i + 1)

                def quantise(t):
                    hb = h[:, t % 2, :]
                    ve.wait_ge(h_ready, t + 1)
                    for k in range(2):
                        last = nc.vector.bn_stats(hstats[:, t, k, :], h[:, t % 2, k * 512:(k + 1) * 512])
                    link(last)
                    link(nc.vector.bn_aggr(hmv[:, t, :], hstats[:, t, :, :].rearrange("p k n -> p (k n)")))
                    nc.vector.tensor_scalar(hvar[:, 0, t:t + 1], hmv[:, t, 1:2], 1e-6, None, ALU.add).then_inc(hvar_ready, 1)
                    ve.wait_ge(hvar_done, t + 1)
                    link(nc.vector.tensor_scalar(hb, hb, hmv[:, t, 0:1], hvar[:, 1, t:t + 1], ALU.subtract, ALU.mult))
                    clip(hb, hb, htop, t).then_inc(h_clipped, 1)

                def h_rest(t):
                    ve.wait_ge(hhi_ready, t + 1)
                    nc.vector.tensor_tensor(h_lo[:, t % 2], ps[:, 4:6, :].rearrange("p a (c n) -> p (a c) n", n=P),
                                            h_hi[:, t % 2], ALU.subtract).then_inc(hlo_ready, 1)

                def add(t):
                    ve.wait_ge(down_ready, t + 1)
                    nc.vector.scalar_tensor_tensor(x[:, t, :], ps[:, 6 + t % 2, 0:DM], mean_size[:, 1:2], x[:, t, :],
                                                   ALU.mult, ALU.add).then_inc(added, 1)

                for t in range(TILES):
                    quantise(t)
                    if t >= 1:
                        add(t - 1)
                    h_rest(t)
                add(TILES - 1)

            @block.scalar
            def _(ac):
                for b in range(BATCH):
                    ac.wait_ge(rows_t, b + 1)
                    nc.scalar.copy(rows_hi[:, :, b * SEQ:(b + 1) * SEQ],
                                   ps[:, b % 2, :].rearrange("p (c n) -> p c n", c=DC)).then_inc(hi_ready, 1)

                def gelu(t):
                    ac.wait_ge(up_ready, t + 1)
                    if t >= 2:
                        ac.wait_ge(h_t, t - 1)
                    nc.scalar.activation(h[:, t % 2, :], ps[:, 2:4, :].rearrange("p a n -> p (a n)"), ACT.Gelu,
                                         scale=mean_size[:, 0:1]).then_inc(h_ready, 1)

                def high(t):
                    ac.wait_ge(h_t, t + 1)
                    if t >= 2:
                        ac.wait_ge(down_ready, t - 1)
                    nc.scalar.copy(h_hi[:, t % 2], ps[:, 4:6, :].rearrange("p a (c n) -> p (a c) n", n=P)).then_inc(hhi_ready, 1)

                gelu(0)
                for t in range(TILES):
                    if t + 1 < TILES:
                        gelu(t + 1)
                    high(t)

            @block.tensor
            def _(pe):
                pe.wait_ge(ones_ready, 1)
                pe.wait_ge(sizes_ready, 1)
                nc.tensor.matmul(ps[:, 7, 0:2], ones[:], size[:], start=True, stop=True).then_inc(size_spread, 1)
                for b in range(BATCH):
                    pe.wait_ge(rows_ready, 2 * b + 2)
                    if b >= 2:
                        pe.wait_ge(lo_ready, b - 1)
                    for c in range(DC):
                        for q in range(QT):
                            last = nc.tensor.transpose(ps[:, b % 2, c * SEQ + q * P:c * SEQ + (q + 1) * P],
                                                       rows[:, b * QT + q, c * P:(c + 1) * P], const["ident"][:])
                    last.then_inc(rows_t, 1)
                pe.wait_ge(lo_ready, BATCH)
                pe.wait_ge(tern_ready, 1)

                def up(t):
                    if t >= 1:
                        pe.wait_ge(h_ready, t)
                    tok = slice(t * P, (t + 1) * P)
                    for n in range(2):
                        for k, (part, c) in enumerate((part, c) for part in (rows_hi, rows_lo) for c in range(DC)):
                            last = nc.tensor.matmul(ps[:, 2 + n, :], part[:, c, tok], tern[0][:, c, n * 512:(n + 1) * 512],
                                                    start=(k == 0), stop=(k == 3))
                    last.then_inc(up_ready, 1)

                def turn(t):
                    pe.wait_ge(h_clipped, t + 1)
                    if t >= 1:
                        pe.wait_ge(hlo_ready, t)
                    for c in range(FC):
                        last = nc.tensor.transpose(ps[:, 4 + c // 4, c % 4 * P:(c % 4 + 1) * P],
                                                   h[:, t % 2, c * P:(c + 1) * P], const["ident"][:])
                    last.then_inc(h_t, 1)

                def down(t):
                    pe.wait_ge(hhi_ready, t + 1)
                    pe.wait_ge(hlo_ready, t + 1)
                    if t >= 2:
                        pe.wait_ge(added, t - 1)
                    for k, (part, c) in enumerate((part, c) for part in (h_hi, h_lo) for c in range(FC)):
                        last = nc.tensor.matmul(ps[:, 6 + t % 2, 0:DM], part[:, t % 2, c, :], tern[1][:, c, :],
                                                start=(k == 0), stop=(k == 2 * FC - 1))
                    last.then_inc(down_ready, 1)

                up(0)
                pe.wait_ge(tern_ready, 2)
                for t in range(TILES):
                    if t + 1 < TILES:
                        up(t + 1)
                    turn(t)
                    down(t)


def gated_scan(nc, x, const, a, w):
    with Stage(nc, "scan") as st:
        sb, sem = st.sb, st.sem
        ps = st.banks()
        CHUNK, TAPS = 32, 4
        NC = SEQ // CHUNK
        RUNS = BATCH * NC
        w_in = sb("w_in", [P, DC, 3 * DM])
        w_swap = sb("w_swap", [P, DC, DM])
        w_out = sb("w_out", [P, DC, DM])
        mix = sb("mix", [P, DC, HEADS])
        same = sb("same", [P, HEADS])
        mixer = sb("mixer", [P, DC, DM])
        norm_scale, conv_b, dt_bias = sb("norm_scale", [P, DC]), sb("conv_b", [P, DC]), sb("dt_bias", [P, DC])
        conv_w = sb("conv_w", [P, DC, TAPS])
        cos, sin = sb("cos", [P, SEQ]), sb("sin", [P, SEQ])
        stats = sb("stats", [P, TILES, 6])
        mean_var = sb("mean_var", [P, TILES, 2])
        rs = sb("rs", [P, 6, TILES])
        half = sb("half", [P, TILES])
        xn = sb("xn", [P, TILES, DM])
        xr = sb("xr", [P, TILES, DM])
        conv_in = sb("conv_in", [P, DC, BATCH, TAPS - 1 + SEQ])
        acc = sb("acc", [P, DC, BATCH, SEQ])
        xs = sb("xs", [P, DC, TOK])
        keep_chunk = sb("keep_chunk", [P, TOK])
        keep_row = sb("keep_row", [P, RUNS])
        dt = sb("dt", [P, DC, TOK])
        v_in = sb("v_in", [P, DC, TOK])
        v_sin = sb("v_sin", [P, TOK])
        gate = sb("gate", [P, DC, TOK])
        decay = sb("decay", [P, DC, TOK])
        since = sb("since", [P, DC, TOK])
        grow = sb("grow", [P, TOK])
        local = sb("local", [P, DC, TOK])
        shrink = sb("shrink", [P, TOK])
        runs = sb("runs", [P, 8, RUNS])
        final = sb("final", [P, DC, TOK])
        y = sb("y", [P, DC, TOK])

        loaded = sem("weights_loaded")
        dve_step, rs_ready, rs_done, masks_ready = sem("dve_step"), sem("rs_ready"), sem("rs_done"), sem("masks_ready")
        xr_ready, xt_ready, xt_taken, conv_done, xs_ready = sem("xr_ready"), sem("xt_ready"), sem("xt_taken"), sem("conv_done"), sem("xs_ready")
        swap_ready, proj_ready, dt_in, dt_ln, act_step = sem("swap_ready"), sem("proj_ready"), sem("dt_in"), sem("dt_ln"), sem("act_step")
        proj_taken, gate_ready = sem("proj_taken"), sem("gate_ready")
        since_ready, grow_ready, shrink_ready, runs_ready, runs_exp = sem("since_ready"), sem("grow_ready"), sem("shrink_ready"), sem("runs_ready"), sem("runs_exp")
        decay_used, decay_ready, decay_exp, final_ready = sem("decay_used"), sem("decay_ready"), sem("decay_exp"), sem("final_ready")
        mixed, y_ready, out_ready, out_taken = sem("mixed"), sem("y_ready"), sem("out_ready"), sem("out_taken")

        def pair(j):
            return ps[:, 2 * (j % 4):2 * (j % 4) + 2, :].rearrange("p a n -> p (a n)")

        def chunks(ap):
            return ap.rearrange("p (k n) -> p k n", n=CHUNK)

        with nc.Block() as block:
            @block.sync
            def _(sp):
                for dst, src in (
                    (norm_scale[:], w["norm_scale"]), (conv_w[:], w["conv_w"]), (conv_b[:], w["conv_b"]), (dt_bias[:], w["dt_bias"]),
                    (w_in[:], w["in_proj_w"].rearrange("(c p) n -> p c n", p=P)),
                    (cos[:], a["c_scan_cos"]), (sin[:], a["c_scan_sin"]), (same[:], a["c_scan_same"]),
                    (mix[:], a["mix_rows"]),
                    (w_out[:], w["out_proj_w"].rearrange("(c p) n -> p c n", p=P)),
                ):
                    sp.dma_start(dst, src).then_inc(loaded, 16)

            @block.gpsimd
            def _(gp):
                nc.gpsimd.memset(half[:], -0.5)
                nc.gpsimd.memset(keep_chunk[:], 1.0)
                nc.gpsimd.memset(keep_row[:], 1.0)
                nc.gpsimd.memset(conv_in[:, :, :, 0:TAPS - 1], 0.0).then_inc(masks_ready, 1)
                gp.wait_ge(masks_ready, 1)
                nc.gpsimd.memset(chunks(keep_chunk[:])[:, :, 0:1], 0.0)
                nc.gpsimd.memset(keep_row[:].rearrange("p (b k) -> p b k", b=BATCH)[:, :, 0:1], 0.0).then_inc(masks_ready, 1)
                for i in range(2):
                    gp.wait_ge(rs_ready, i + 1)
                    nc.gpsimd.tensor_tensor(rs[:, 2 * i + 1, :], rs[:, 2 * i, :], half[:], ALU.pow).then_inc(rs_done, 1)
                gp.wait_ge(loaded, 160)
                for c in range(DC):
                    v = w_in[:, c, DM:2 * DM].rearrange("p (h s d) -> p h s d", s=2, d=HEADS // 2)
                    s = w_swap[:, c, :].rearrange("p (h s d) -> p h s d", s=2, d=HEADS // 2)
                    nc.gpsimd.tensor_copy(s[:, :, 0, :], v[:, :, 1, :])
                    last = nc.gpsimd.tensor_copy(s[:, :, 1, :], v[:, :, 0, :])
                last.then_inc(swap_ready, 1)
                for c in range(DC):
                    last = nc.gpsimd.tensor_tensor(mixer[:, c, :].rearrange("p (m d) -> p m d", m=HEADS),
                                                   bcast(mix[:, c, :], 2, HEADS), bcast(same[:], 1, HEADS), ALU.mult)
                last.then_inc(swap_ready, 1)

            @block.vector
            def _(ve):
                link = chain(ve, dve_step)
                row_stats(nc, link, x, stats, mean_var)
                nc.vector.tensor_scalar(rs[:, 0, :], mean_var[:, :, 1], 1e-5, None, ALU.add).then_inc(rs_ready, 1)
                ve.wait_ge(rs_done, 1)
                link(nc.vector.tensor_tensor(rs[:, 4, :], rs[:, 1, :], rs[:, 1, :], ALU.mult))
                link(nc.vector.tensor_tensor(rs[:, 5, :], rs[:, 4, :], mean_var[:, :, 1], ALU.mult))
                nc.vector.tensor_scalar(rs[:, 2, :], rs[:, 5, :], 1e-6, None, ALU.add).then_inc(rs_ready, 1)
                for t in range(TILES):
                    last = nc.vector.tensor_scalar(xn[:, t, :], x[:, t, :], mean_var[:, t, 0:1], rs[:, 1, t:t + 1],
                                                   ALU.subtract, ALU.mult)
                link(last)
                ve.wait_ge(rs_done, 2)
                for t in range(TILES):
                    nc.vector.tensor_scalar(xr[:, t, :], xn[:, t, :], rs[:, 3, t:t + 1], None, ALU.mult).then_inc(xr_ready, 1)
                ve.wait_ge(loaded, 160)
                ve.wait_ge(masks_ready, 2)
                for b in range(BATCH):
                    ve.wait_ge(xt_ready, b + 1)
                    for c in range(DC):
                        last = nc.vector.tensor_scalar(conv_in[:, c, b, TAPS - 1:], ps[:, b, c * SEQ:(c + 1) * SEQ],
                                                       norm_scale[:, c:c + 1], 60000.0, ALU.mult, ALU.min)
                    last.then_inc(xt_taken, 1)
                ve.wait_ge(xt_taken, BATCH)
                link(nc.vector.tensor_scalar(conv_in[:], conv_in[:], -60000.0, None, ALU.max))
                for c in range(DC):
                    link(nc.vector.tensor_scalar(acc[:, c], conv_in[:, c, :, 0:SEQ], conv_w[:, c, 0:1], None, ALU.mult))
                    for k in range(1, TAPS):
                        ins = nc.vector.scalar_tensor_tensor(acc[:, c], conv_in[:, c, :, k:k + SEQ], conv_w[:, c, k:k + 1], acc[:, c],
                                                             ALU.mult, ALU.add)
                        if k < TAPS - 1:
                            link(ins)
                    ins.then_inc(conv_done, 1)
                rows = [P, BATCH, SEQ]
                for c in range(DC):
                    ve.wait_ge(proj_ready, 4 * c + 1)
                    ins = nc.vector.tensor_scalar(dt[:, c, :], pair(4 * c), dt_bias[:, c:c + 1], 20.0, ALU.add, ALU.min)
                    ins.then_inc(dt_in, 1)
                    by_row = lambda ap: ap.rearrange("p (b n) -> p b n", b=BATCH)
                    ve.wait_ge(proj_ready, 4 * c + 2)
                    nc.vector.tensor_tensor(by_row(v_in[:, c, :]), by_row(pair(4 * c + 1)), bcast(cos[:], 1, BATCH), ALU.mult)
                    ve.wait_ge(proj_ready, 4 * c + 3)
                    ins = nc.vector.tensor_tensor(by_row(v_sin[:]), by_row(pair(4 * c + 2)), bcast(sin[:], 1, BATCH), ALU.mult)
                    ins.then_inc(proj_taken, 1)
                    ve.wait_ge(proj_taken, c + 1)
                    link(nc.vector.tensor_tensor(v_in[:, c, :], v_in[:, c, :], v_sin[:], ALU.add))
                    ve.wait_ge(dt_ln, c + 1)
                    link(nc.vector.tensor_scalar(dt[:, c, :], dt[:, c, :], 0.001, 2.0, ALU.max, ALU.min))
                    link(nc.vector.tensor_tensor(v_in[:, c, :], v_in[:, c, :], dt[:, c, :], ALU.mult))
                    link(nc.vector.tensor_tensor_scan(decay[:, c, :], keep_chunk[:], dt[:, c, :], 0.0, ALU.mult, ALU.add))
                    link(nc.vector.tensor_scalar(decay[:, c, :], decay[:, c, :], 20.0, None, ALU.min))
                    nc.vector.tensor_tensor(chunks(since[:, c, :]), chunks(decay[:, c, :]),
                                            chunks(decay[:, c, :])[:, :, 0:1].to_broadcast([P, RUNS, CHUNK]),
                                            ALU.subtract).then_inc(since_ready, 1)
                    ve.wait_ge(grow_ready, c + 1)
                    link(nc.vector.tensor_tensor(v_in[:, c, :], v_in[:, c, :], grow[:], ALU.mult))
                    link(nc.vector.tensor_tensor_scan(local[:, c, :], keep_chunk[:], v_in[:, c, :], 0.0, ALU.mult, ALU.add))
                    ve.wait_ge(shrink_ready, c + 1)
                    ins = nc.vector.tensor_tensor(local[:, c, :], local[:, c, :], shrink[:], ALU.mult)
                    ins.then_inc(decay_used, 1)
                    ve.wait_ge(decay_used, c + 1)
                    total, seed = runs[:, 0, :], runs[:, 1, :]
                    first = lambda ap: ap.rearrange("p (b k) -> p b k", b=BATCH)
                    link(nc.vector.tensor_copy(runs[:, 2, :], chunks(decay[:, c, :])[:, :, CHUNK - 1]))
                    link(nc.vector.tensor_tensor_scan(total, keep_row[:], runs[:, 2, :], 0.0, ALU.mult, ALU.add))
                    link(nc.vector.tensor_scalar(total, total, 80.0, None, ALU.min))
                    link(nc.vector.tensor_tensor(first(runs[:, 3, :]), first(total), first(total)[:, :, 0:1].to_broadcast([P, BATCH, NC]),
                                                 ALU.subtract))
                    nc.vector.tensor_scalar(runs[:, 3, :], runs[:, 3, :], 20.0, None, ALU.min).then_inc(runs_ready, 1)
                    ve.wait_ge(runs_exp, c + 1)
                    link(nc.vector.tensor_tensor(seed, chunks(local[:, c, :])[:, :, CHUNK - 1], runs[:, 4, :], ALU.mult))
                    link(nc.vector.memset(runs[:, 6, :], 0.0))
                    link(nc.vector.tensor_copy(first(runs[:, 6, :])[:, :, 1:NC], first(seed)[:, :, 0:NC - 1]))
                    link(nc.vector.tensor_tensor_scan(runs[:, 7, :], keep_row[:], runs[:, 6, :], 0.0, ALU.mult, ALU.add))
                    link(nc.vector.tensor_tensor(runs[:, 7, :], runs[:, 7, :], runs[:, 5, :], ALU.mult))
                    ve.wait_ge(decay_exp, c + 1)
                    link(nc.vector.tensor_tensor(chunks(final[:, c, :]), chunks(since[:, c, :]), bcast(runs[:, 7, :], 2, CHUNK), ALU.mult))
                    nc.vector.tensor_tensor(final[:, c, :], final[:, c, :], local[:, c, :], ALU.add).then_inc(final_ready, 1)
                for c in range(DC):
                    ve.wait_ge(mixed, c + 1)
                    ve.wait_ge(gate_ready, c + 1)
                    nc.vector.tensor_tensor(y[:, c, :], pair(8 + c), gate[:, c, :], ALU.mult).then_inc(y_ready, 1)
                for t in range(TILES):
                    last = nc.vector.tensor_tensor(x[:, t, :], x[:, t, :], xn[:, t, :], ALU.add)
                link(last)
                for t in range(TILES):
                    ve.wait_ge(out_ready, t + 1)
                    nc.vector.tensor_tensor(x[:, t, :], x[:, t, :], ps[:, 4 + t % 4, 0:DM], ALU.add).then_inc(out_taken, 1)

            @block.scalar
            def _(ac):
                for c in range(DC):
                    ac.wait_ge(conv_done, c + 1)
                    nc.scalar.activation(xs[:, c, :], acc[:, c].rearrange("p b n -> p (b n)"), ACT.Silu,
                                         bias=conv_b[:, c:c + 1]).then_inc(xs_ready, 1)
                step = chain(ac, act_step)
                for c in range(DC):
                    ac.wait_ge(dt_in, c + 1)
                    step(nc.scalar.activation(dt[:, c, :], dt[:, c, :], ACT.Exp))
                    nc.scalar.activation(dt[:, c, :], dt[:, c, :], ACT.Ln, bias=1.0).then_inc(dt_ln, 1)
                    ac.wait_ge(since_ready, c + 1)
                    if c >= 1:
                        ac.wait_ge(decay_used, c)
                    nc.scalar.activation(grow[:], since[:, c, :], ACT.Exp).then_inc(grow_ready, 1)
                    ins = nc.scalar.activation(shrink[:], since[:, c, :], ACT.Exp, scale=-1.0)
                    ins.then_inc(shrink_ready, 1)
                    ac.wait_ge(shrink_ready, c + 1)
                    nc.scalar.activation(since[:, c, :], decay[:, c, :], ACT.Exp, scale=-1.0).then_inc(decay_exp, 1)
                    ac.wait_ge(runs_ready, c + 1)
                    nc.scalar.activation(runs[:, 4, :], runs[:, 3, :], ACT.Exp)
                    nc.scalar.activation(runs[:, 5, :], runs[:, 3, :], ACT.Exp, scale=-1.0).then_inc(runs_exp, 1)
                    ac.wait_ge(proj_ready, 4 * c + 4)
                    nc.scalar.activation(gate[:, c, :], pair(4 * c + 3), ACT.Sigmoid).then_inc(gate_ready, 1)

            @block.tensor
            def _(pe):
                for b in range(BATCH):
                    pe.wait_ge(xr_ready, 2 * b + 2)
                    for c in range(DC):
                        for q in range(QT):
                            last = nc.tensor.transpose(ps[:, b, c * SEQ + q * P:c * SEQ + (q + 1) * P],
                                                       xr[:, b * QT + q, c * P:(c + 1) * P], const["ident"][:])
                    last.then_inc(xt_ready, 1)
                pe.wait_ge(xs_ready, DC)
                pe.wait_ge(swap_ready, 1)
                for c in range(DC):
                    for k, (wt, col) in enumerate(((w_in, 0), (w_in, DM), (w_swap, 0), (w_in, 2 * DM))):
                        if c == 1:
                            if k == 0:
                                pe.wait_ge(dt_in, 1)
                            elif k < 3:
                                pe.wait_ge(proj_taken, 1)
                            else:
                                pe.wait_ge(gate_ready, 1)
                        for n in range(2):
                            for d in range(DC):
                                last = nc.tensor.matmul(ps[:, 2 * k + n, :], wt[:, d, col + c * P:col + (c + 1) * P],
                                                        xs[:, d, n * 512:(n + 1) * 512], start=(d == 0), stop=(d == DC - 1))
                        last.then_inc(proj_ready, 1)
                pe.wait_ge(final_ready, DC)
                pe.wait_ge(swap_ready, 2)
                pe.wait_ge(gate_ready, DC)
                for c in range(DC):
                    for n in range(2):
                        for d in range(DC):
                            last = nc.tensor.matmul(ps[:, 2 * c + n, :], mixer[:, d, c * P:(c + 1) * P],
                                                    final[:, d, n * 512:(n + 1) * 512], start=(d == 0), stop=(d == DC - 1))
                    last.then_inc(mixed, 1)
                pe.wait_ge(y_ready, DC)
                for t in range(TILES):
                    if t >= 4:
                        pe.wait_ge(out_taken, t - 3)
                    for d in range(DC):
                        last = nc.tensor.matmul(ps[:, 4 + t % 4, 0:DM], y[:, d, t * P:(t + 1) * P], w_out[:, d, :],
                                                start=(d == 0), stop=(d == DC - 1))
                    last.then_inc(out_ready, 1)


QH, KVH, HD = 16, 4, 128
REP = QH // KVH
KEYS = SEQ + CTX
KT = QT + CTX_TILES
QCOLS = REP * SEQ
ROUND = 1.5 * 2.0 ** 23
TWO_PI = (6.28125, 0.0019353071693331003, 1.0253131677018246e-11)


def rows_of(tile):
    return P if tile < KT - 1 else CTX_REST


def cross_attention(nc, x, const, a, w):
    with Stage(nc, "cross") as keep:
        sb = keep.sb
        names = (("q", DC, QH * HD), ("k", DC, KVH * HD), ("v", DC, KVH * HD), ("o", QH, DM))
        W = {n: [sb(f"w_{n}_{part}", [P, c, m], BF16) for part in ("hi", "lo")] for n, c, m in names}
        k_t = [sb(f"k_t_{part}", [P, KVH, KEYS], BF16) for part in ("hi", "lo")]
        q_t = [sb(f"q_t_{part}", [P, QH, SEQ], BF16) for part in ("hi", "lo")]
        v = [sb(f"v_{part}", [P, KT, KVH * HD], BF16) for part in ("hi", "lo")]
        k_gain = sb("k_gain", [P, 2, HD])
        q_gain = sb("q_gain", [P, 2, HD])
        freq = sb("freq", [P, HD // 2])
        ones = sb("ones", [P, P])
        ones_own = sb("ones_own", [8, P], BF16)
        own8 = sb("own8", [8, 8])

        with Stage(nc, "cross_w") as st:
            raw = {n: st.sb(f"raw_{n}", [P, c, m]) for n, c, m in names}
            loaded, high_done, low_done, set_up, signed = (st.sem(s) for s in ("loaded", "high_done", "low_done", "set_up", "signed"))
            with nc.Block() as block:
                @block.sync
                def _(sp):
                    for n, src in (("k", "Wk"), ("v", "Wv"), ("q", "Wq"), ("o", "Wo")):
                        sp.dma_start(raw[n][:], w[src].rearrange("(c p) n -> p c n", p=P)).then_inc(loaded, 16)
                    for gain, src in ((k_gain, "k_norm_w"), (q_gain, "q_norm_w")):
                        sp.dma_start(gain[:, 0, :], w[src].partition_broadcast(P)).then_inc(loaded, 16)
                        sp.dma_start(gain[:, 1, 0:HD // 2], w[src][HD // 2:HD].partition_broadcast(P)).then_inc(loaded, 16)
                        sp.dma_start(gain[:, 1, HD // 2:HD], w[src][0:HD // 2].partition_broadcast(P)).then_inc(loaded, 16)
                    sp.dma_start(freq[:], a["c_cross_freq"].partition_broadcast(P)).then_inc(loaded, 16)
                    sp.dma_start(own8[:], a["c_cross_own"]).then_inc(loaded, 16)

                @block.gpsimd
                def _(gp):
                    nc.gpsimd.memset(ones[:], 1.0)
                    nc.gpsimd.memset(ones_own[:], 1.0)

                @block.scalar
                def _(ac):
                    ac.wait_ge(loaded, 16 * 12)
                    for n in "kvqo":
                        nc.scalar.copy(W[n][0][:], raw[n][:]).then_inc(high_done, 1)

                @block.vector
                def _(ve):
                    ve.wait_ge(loaded, 16 * 12)
                    for gain in (k_gain, q_gain):
                        last = nc.vector.tensor_scalar(gain[:, 1, 0:HD // 2], gain[:, 1, 0:HD // 2], -1.0, None, ALU.mult)
                    for i, n in enumerate("kvqo"):
                        ve.wait_ge(high_done, i + 1)
                        nc.vector.tensor_tensor(W[n][1][:], raw[n][:], W[n][0][:], ALU.subtract)

        with nc.Fori(0, BATCH) as b:
            project_row(nc, x, const, a, b, W, k_t, q_t, v, k_gain, q_gain, freq)
            attend_row(nc, x, const, b, W["o"], k_t, q_t, v, ones, ones_own, own8)


def project_row(nc, x, const, a, b, W, k_t, q_t, v, k_gain, q_gain, freq):
    with Stage(nc, "project") as st:
        sb, sem = st.sb, st.sem
        ps = st.banks()
        H2 = HD // 2
        row = sb("row", [P, QT, DM])
        stats = sb("stats", [P, QT, 6])
        mean_var = sb("mean_var", [P, QT, 2])
        rs = sb("rs", [P, 2, QT])
        half = sb("half", [P, 8])
        ctx_t = sb("ctx_t", [P, DC, CTX])
        in_t = [sb(f"in_t_{part}", [P, DC, KEYS], BF16) for part in ("hi", "lo")]
        where = sb("where", [P, KT], I32)
        where_f = sb("where_f", [P, KT])
        angle = sb("angle", [P, KT, H2])
        turns = sb("turns", [P, KT, H2])
        sin = sb("sin", [P, KT, H2])
        cos = angle
        k_tab = [sb(f"k_tab_{f}", [P, KT, HD]) for f in ("cos", "sin")]
        q_tab = [sb(f"q_tab_{f}", [P, QT, HD]) for f in ("cos", "sin")]
        squares = sb("squares", [P, 2, 4, HD])
        ss = sb("ss", [P, 2, 4])
        ms = sb("ms", [P, 2, 4])
        rms = sb("rms", [P, 2, 4])
        by_cos = sb("by_cos", [P, 2, 4, HD])
        by_sin = sb("by_sin", [P, 2, 4, HD])
        summed = sb("summed", [P, 2, 4, HD])
        normed = sb("normed", [P, 2, 4, HD])

        loaded, dve_step, rs_ready, rs_done = sem("loaded"), sem("dve_step"), sem("rs_ready"), sem("rs_done")
        act_step, pool_step = sem("act_step"), sem("pool_step")
        row_ready, row_t, own_hi, own_ready = sem("row_ready"), sem("row_t"), sem("own_hi"), sem("own_ready")
        ctx_hi, ctx_ready, angle_ready, waves_ready, mag_ready = sem("ctx_hi"), sem("ctx_ready"), sem("angle_ready"), sem("waves_ready"), sem("mag_ready")
        projected, v_hi, v_taken, squared = sem("projected"), sem("v_hi"), sem("v_taken"), sem("squared")
        taken, summed_done, normed_ready, turned, hi_ready, lo_ready = (sem(s) for s in ("taken", "summed_done", "normed_ready", "turned", "hi_ready", "lo_ready"))

        units = [("k", k, 0) for k in range(KT)] + [("q", q, g) for q in range(QT) for g in range(QH // 4)]

        def place(u):
            kind, tile, g = units[u]
            if kind == "k":
                return [part[:, :, tile * P:tile * P + rows_of(tile)] for part in k_t]
            return [part[:, 4 * g:4 * g + 4, tile * P:(tile + 1) * P] for part in q_t]

        with nc.Block() as block:
            @block.sync
            def _(sp):
                sp.dma_start(ctx_t[:], a["ctx_t"].rearrange("b (c p) n -> p b c n", p=P)[:, bass.ds(b, 1)]
                             .rearrange("p b c n -> p (b c) n")).then_inc(loaded, 16)
                sp.dma_start(where[:], a["positions"][bass.ds(b, 1)].rearrange("b p k -> (b p) k")).then_inc(loaded, 16)

            @block.gpsimd
            def _(gp):
                link = chain(gp, pool_step)
                link(nc.gpsimd.memset(half[:], -0.5))
                gp.wait_ge(rs_ready, 1)
                nc.gpsimd.tensor_tensor(rs[:, 1, :], rs[:, 0, :], half[:, 0:QT], ALU.pow).then_inc(rs_done, 1)
                for u, (kind, tile, g) in enumerate(units):
                    r, k = rows_of(tile) if kind == "k" else P, u % 2
                    gp.wait_ge(squared, u + 1)
                    link(nc.gpsimd.tensor_scalar(ms[0:r, k, :], ss[0:r, k, :], 1.0 / HD, 1e-6, ALU.mult, ALU.add))
                    link(nc.gpsimd.tensor_tensor(rms[0:r, k, :], ms[0:r, k, :], half[0:r, 0:4], ALU.pow))
                    gp.wait_ge(summed_done, u + 1)
                    if u >= 2:
                        gp.wait_ge(turned, u - 1)
                    nc.gpsimd.tensor_tensor(normed[0:r, k], summed[0:r, k], bcast(rms[0:r, k, :], 2, HD),
                                            ALU.mult).then_inc(normed_ready, 1)

            @block.vector
            def _(ve):
                link = chain(ve, dve_step)
                link(nc.vector.tensor_copy(row[:], x[:, bass.ds(b * QT, QT), :]))
                for q in range(QT):
                    last = nc.vector.bn_stats(stats[:, q, :], row[:, q, :])
                link(last)
                for q in range(QT):
                    last = nc.vector.bn_aggr(mean_var[:, q, :], stats[:, q, :])
                link(last)
                nc.vector.tensor_scalar(rs[:, 0, :], mean_var[:, :, 1], 1e-5, None, ALU.add).then_inc(rs_ready, 1)
                ve.wait_ge(rs_done, 1)
                for q in range(QT):
                    last = nc.vector.tensor_scalar(row[:, q, :], row[:, q, :], mean_var[:, q, 0:1], rs[:, 1, q:q + 1],
                                                   ALU.subtract, ALU.mult)
                last.then_inc(row_ready, 1)
                ve.wait_ge(loaded, 32)
                link(nc.vector.tensor_copy(where_f[:], where[:]))
                link(nc.vector.tensor_tensor(angle[:], bcast(where_f[:], 2, H2), bcast(freq[:], 1, KT), ALU.mult))
                link(nc.vector.tensor_scalar(turns[:], angle[:], 1.0 / (2.0 * math.pi), ROUND, ALU.mult, ALU.add))
                link(nc.vector.tensor_scalar(turns[:], turns[:], ROUND, None, ALU.subtract))
                for part in TWO_PI:
                    link(nc.vector.scalar_tensor_tensor(angle[:], turns[:], -part, angle[:], ALU.mult, ALU.add))
                nc.vector.tensor_scalar(angle[:], angle[:], 3.1415925, -3.1415925, ALU.min, ALU.max).then_inc(angle_ready, 1)
                ve.wait_ge(row_t, 1)
                ve.wait_ge(own_hi, 1)
                nc.vector.tensor_tensor(in_t[1][:, :, 0:SEQ], ps[:, 7, :].rearrange("p (c n) -> p c n", c=DC),
                                        in_t[0][:, :, 0:SEQ], ALU.subtract).then_inc(own_ready, 1)
                for c in range(DC):
                    ve.wait_ge(ctx_hi, c + 1)
                    nc.vector.tensor_tensor(in_t[1][:, c, SEQ:KEYS], ctx_t[:, c, :], in_t[0][:, c, SEQ:KEYS],
                                            ALU.subtract).then_inc(ctx_ready, 1)
                ve.wait_ge(waves_ready, 1)
                for tab, gain, n in ((k_tab, k_gain, KT), (q_tab, q_gain, QT)):
                    for s in range(2):
                        cols = slice(s * H2, (s + 1) * H2)
                        nc.vector.tensor_tensor(tab[0][:, :, cols], cos[:, 0:n, :], bcast(gain[:, 0, cols], 1, n), ALU.mult)
                        last = nc.vector.tensor_tensor(tab[1][:, :, cols], sin[:, 0:n, :], bcast(gain[:, 1, cols], 1, n), ALU.mult)
                link(last)

                def rotate(u):
                    kind, tile, g = units[u]
                    r, k = rows_of(tile) if kind == "k" else P, u % 2
                    tab = k_tab if kind == "k" else q_tab
                    bank = ps[0:r, 2 * k, :].rearrange("p (h n) -> p h n", h=4)
                    if kind == "k":
                        ve.wait_ge(v_hi, u + 1)
                        nc.vector.tensor_tensor(v[1][0:r, tile, :], ps[0:r, 2 * k + 1, :], v[0][0:r, tile, :],
                                                ALU.subtract).then_inc(v_taken, 1)
                    ve.wait_ge(squared, u + 1)
                    if u >= 2:
                        ve.wait_ge(summed_done, u - 1)
                    nc.vector.tensor_tensor(by_cos[0:r, k], bank, bcast(tab[0][0:r, tile, :], 1, 4), ALU.mult)
                    for s in range(2):
                        to, of = slice(s * H2, (s + 1) * H2), slice((1 - s) * H2, (2 - s) * H2)
                        last = nc.vector.tensor_tensor(by_sin[0:r, k, :, to], bank[:, :, of], bcast(tab[1][0:r, tile, to], 1, 4), ALU.mult)
                    last.then_inc(taken, 1)
                    ve.wait_ge(taken, u + 1)
                    if u >= 2:
                        ve.wait_ge(normed_ready, u - 1)
                    nc.vector.tensor_tensor(summed[0:r, k], by_cos[0:r, k], by_sin[0:r, k], ALU.add).then_inc(summed_done, 1)

                def low(u):
                    kind, tile, g = units[u]
                    r, k = rows_of(tile) if kind == "k" else P, u % 2
                    hi, lo = place(u)
                    ve.wait_ge(hi_ready, u + 1)
                    nc.vector.tensor_tensor(lo, ps[:, 4 + k, :].rearrange("p (h n) -> p h n", h=4)[:, :, 0:r], hi,
                                            ALU.subtract).then_inc(lo_ready, 1)

                for u in range(len(units)):
                    rotate(u)
                    if u >= 1:
                        low(u - 1)
                low(len(units) - 1)

            @block.scalar
            def _(ac):
                step = chain(ac, act_step)
                ac.wait_ge(loaded, 32)
                for c in range(DC):
                    nc.scalar.copy(in_t[0][:, c, SEQ:KEYS], ctx_t[:, c, :]).then_inc(ctx_hi, 1)
                ac.wait_ge(row_t, 1)
                nc.scalar.copy(in_t[0][:, :, 0:SEQ], ps[:, 7, :].rearrange("p (c n) -> p c n", c=DC)).then_inc(own_hi, 1)
                ac.wait_ge(angle_ready, 1)
                nc.scalar.activation(sin[:], angle[:], ACT.Sin)
                step(nc.scalar.activation(turns[:], angle[:], ACT.Abs))
                nc.scalar.activation(cos[:], turns[:], ACT.Sin, scale=-1.0, bias=const["half_pi"][:]).then_inc(waves_ready, 1)

                def square(u):
                    kind, tile, g = units[u]
                    r, k = rows_of(tile) if kind == "k" else P, u % 2
                    ac.wait_ge(projected, u + 1)
                    if kind == "k":
                        nc.scalar.copy(v[0][0:r, tile, :], ps[0:r, 2 * k + 1, :]).then_inc(v_hi, 1)
                    if u >= 2:
                        ac.wait_ge(normed_ready, u - 1)
                        ac.wait_ge(squared, u - 1)
                    for h in range(4):
                        last = nc.scalar.activation(squares[0:r, k, h, :], ps[0:r, 2 * k, h * HD:(h + 1) * HD], ACT.Square,
                                                    accum_out=ss[0:r, k, h:h + 1])
                    last.then_inc(squared, 1)

                def high(u):
                    kind, tile, g = units[u]
                    r, k = rows_of(tile) if kind == "k" else P, u % 2
                    ac.wait_ge(turned, u + 1)
                    nc.scalar.copy(place(u)[0], ps[:, 4 + k, :].rearrange("p (h n) -> p h n", h=4)[:, :, 0:r]).then_inc(hi_ready, 1)

                for u in range(len(units)):
                    square(u)
                    if u >= 1:
                        high(u - 1)
                high(len(units) - 1)

            @block.tensor
            def _(pe):
                pe.wait_ge(row_ready, 1)
                for c in range(DC):
                    for q in range(QT):
                        last = nc.tensor.transpose(ps[:, 7, c * SEQ + q * P:c * SEQ + (q + 1) * P], row[:, q, c * P:(c + 1) * P],
                                                   const["ident"][:])
                last.then_inc(row_t, 1)
                pe.wait_ge(own_ready, 1)
                pe.wait_ge(ctx_ready, DC)

                def project(u):
                    kind, tile, g = units[u]
                    r, k = rows_of(tile) if kind == "k" else P, u % 2
                    if u >= 2:
                        pe.wait_ge(taken, u - 1)
                        if kind == "k":
                            pe.wait_ge(v_taken, u - 1)
                    todo = ((0, "k", 0), (1, "v", 0)) if kind == "k" else ((0, "q", g),)
                    for i, name, group in todo:
                        for n, (one, two, c) in enumerate((one, two, c) for one, two in ((0, 0), (0, 1), (1, 0)) for c in range(DC)):
                            last = nc.tensor.matmul(ps[0:r, 2 * k + i, :], in_t[one][:, c, tile * P:tile * P + r],
                                                    W[name][two][:, c, group * 512:(group + 1) * 512],
                                                    start=(n == 0), stop=(n == 3 * DC - 1))
                    last.then_inc(projected, 1)

                def turn(u):
                    kind, tile, g = units[u]
                    r, k = rows_of(tile) if kind == "k" else P, u % 2
                    pe.wait_ge(normed_ready, u + 1)
                    if u >= 2:
                        pe.wait_ge(lo_ready, u - 1)
                    for h in range(4):
                        last = nc.tensor.transpose(ps[:, 4 + k, h * P:h * P + r], normed[0:r, k, h, :], const["ident"][0:r, 0:r])
                    last.then_inc(turned, 1)

                for u in range(len(units)):
                    project(u)
                    if u >= 1:
                        turn(u - 1)
                turn(len(units) - 1)


def attend_row(nc, x, const, b, w_o, k_t, q_t, v, ones, ones_own, own8):
    with Stage(nc, "attend") as st:
        sb, sem = st.sb, st.sem
        ps = st.banks()
        SCALE = float(HD) ** -0.5
        STEPS = KVH * KT
        CHUNKS = [(s, min(512, KEYS - s)) for s in range(0, KEYS, 512)]
        NCH = len(CHUNKS)
        PIECES = REP * QT * NCH
        p32 = sb("p32", [P, 2, QCOLS])
        p_hi = sb("p_hi", [P, 2, QCOLS], F16)
        p_lo = sb("p_lo", [P, 2, QCOLS], F16)
        acc = sb("acc", [P, 2, QCOLS])
        tops = sb("tops", [P, REP * QT, NCH])
        top = sb("top", [P, REP * QT])
        shift = sb("shift", [P, REP * QT], BF16)
        own = sb("own", [8, 2, 8, P], BF16)
        raw = sb("raw", [P, QCOLS])
        inv = sb("inv", [P, QCOLS])
        scaled = sb("scaled", [P, QCOLS])
        att = [sb(f"att_{part}", [P, QH, SEQ], BF16) for part in ("hi", "lo")]
        row = sb("row", [P, QT, DM])

        dve_step = sem("dve_step")
        side_ready, side_taken, shift_ready = sem("side_ready"), sem("side_taken"), sem("shift_ready")
        scored, p32_ready, hi_ready, lo_ready, summed = sem("scored"), sem("p32_ready"), sem("hi_ready"), sem("lo_ready"), sem("summed")
        weighed, raw_ready, scaled_ready, att_hi, att_lo = sem("weighed"), sem("raw_ready"), sem("scaled_ready"), sem("att_hi"), sem("att_lo")
        out_ready = sem("out_ready")

        def side_work(step):
            k, t = divmod(step, KT)
            work = []
            if t == 1 and k >= 1:
                work.append(("sum", k - 1, 0))
            if k + 1 < KVH and 2 <= t < 13:
                work += [("piece", k + 1, n) for n in range(3 * (t - 2), min(3 * (t - 1), PIECES))]
            if k + 1 < KVH and t == 13:
                work.append(("turn", k + 1, 0))
            return work

        before = [("piece", 0, n) for n in range(PIECES)] + [("turn", 0, 0)]
        order = before + [i for s in range(STEPS) for i in side_work(s)] + [("sum", KVH - 1, 0)]
        at = {item: n for n, item in enumerate(order)}

        with nc.Block() as block:
            @block.tensor
            def _(pe):
                def side(item):
                    kind, k, n = item
                    if kind == "piece":
                        prior = order[at[item] - 1][0] if at[item] else None
                        done = at[item] - 1 if prior == "piece" else at[item]
                        if done >= 1:
                            pe.wait_ge(side_taken, done)
                        c, (s, m) = n // NCH, CHUNKS[n % NCH]
                        nc.tensor.matmul(ps[:, 6 + n % 2, 0:m], q_t[0][:, REP * k + c // QT, c % QT * P:(c % QT + 1) * P],
                                         k_t[0][:, k, s:s + m], start=True, stop=True).then_inc(side_ready, 1)
                    elif kind == "turn":
                        pe.wait_ge(side_taken, at[item])
                        pe.wait_ge(shift_ready, k + 1)
                        nc.tensor.matmul(ps[0:8, 6, 0:P], shift[:], const["ident_b"][:], start=True, stop=True).then_inc(side_ready, 1)
                    else:
                        pe.wait_ge(side_taken, at[item])
                        pe.wait_ge(summed, KT * (k + 1))
                        for n in range(2):
                            last = nc.tensor.matmul(ps[:, 6 + n, :], ones[:], acc[:, k % 2, n * 512:(n + 1) * 512], start=True, stop=True)
                        last.then_inc(side_ready, 1)

                def score(step):
                    k, t = divmod(step, KT)
                    r, keys = rows_of(t), slice(t * P, t * P + rows_of(t))
                    if t == 0:
                        pe.wait_ge(side_taken, at[("turn", k, 0)] + 1)
                    if step >= 2:
                        pe.wait_ge(hi_ready, step - 1)
                    for n in range(2):
                        cols = slice(REP * k + 2 * n, REP * k + 2 * n + 2)
                        out = ps[0:r, 2 * (step % 2) + n, :]
                        nc.tensor.matmul(out, ones_own[:, 0:r], own[:, k % 2, 4 * n:4 * n + 4, :], start=True, stop=False)
                        for one, two in ((0, 0), (0, 1), (1, 0)):
                            last = nc.tensor.matmul(out, k_t[one][:, k, keys], q_t[two][:, cols, :], start=False, stop=(one == 1))
                    last.then_inc(scored, 1)

                def weigh(step):
                    k, t = divmod(step, KT)
                    r, head = rows_of(t), slice(k * HD, (k + 1) * HD)
                    pe.wait_ge(lo_ready, step + 1)
                    if t == 0 and k >= 1:
                        pe.wait_ge(raw_ready, k)
                    for one, p in ((0, p_hi), (0, p_lo), (1, p_hi)):
                        for n in range(2):
                            last = nc.tensor.matmul(ps[:, 4 + n, :], v[one][0:r, t, head], p[0:r, step % 2, n * 512:(n + 1) * 512],
                                                    start=(t == 0 and one == 0 and p is p_hi), stop=(t == KT - 1 and one == 1))
                    last.then_inc(weighed, 1)

                for item in before:
                    side(item)
                for step in range(STEPS):
                    score(step)
                    for item in side_work(step):
                        side(item)
                    if step >= 1:
                        weigh(step - 1)
                weigh(STEPS - 1)
                side(("sum", KVH - 1, 0))
                pe.wait_ge(att_lo, KVH)
                for q in range(QT):
                    for n, (one, two, h) in enumerate((one, two, h) for one, two in ((0, 0), (0, 1), (1, 0)) for h in range(QH)):
                        last = nc.tensor.matmul(ps[:, 6 + q, 0:DM], att[one][:, h, q * P:(q + 1) * P], w_o[two][:, h, :],
                                                start=(n == 0), stop=(n == 3 * QH - 1))
                    last.then_inc(out_ready, 1)

            @block.scalar
            def _(ac):
                def copy_out(k):
                    ac.wait_ge(weighed, KT * (k + 1))
                    if k >= 1:
                        ac.wait_ge(scaled_ready, k)
                    nc.scalar.copy(raw[:], ps[:, 4:6, :].rearrange("p a n -> p (a n)")).then_inc(raw_ready, 1)

                def high(k):
                    ac.wait_ge(scaled_ready, k + 1)
                    nc.scalar.copy(att[0][:, REP * k:REP * (k + 1), :], scaled[:].rearrange("p (h n) -> p h n", h=REP)).then_inc(att_hi, 1)

                for step in range(STEPS):
                    k, t = divmod(step, KT)
                    r, i = rows_of(t), step % 2
                    src = ps[0:r, 2 * i:2 * i + 2, :].rearrange("p a n -> p (a n)")
                    ac.wait_ge(scored, step + 1)
                    if step >= 2:
                        ac.wait_ge(lo_ready, step - 1)
                        ac.wait_ge(summed, step - 1)
                    nc.scalar.activation(p32[0:r, i, :], src, ACT.Exp, scale=SCALE).then_inc(p32_ready, 1)
                    if step >= 2:
                        ac.wait_ge(weighed, step - 1)
                    nc.scalar.activation(p_hi[0:r, i, :], src, ACT.Exp, scale=SCALE).then_inc(hi_ready, 1)
                    if t == 0 and k >= 1:
                        copy_out(k - 1)
                    if t == 3 and k >= 1:
                        high(k - 1)
                copy_out(KVH - 1)
                high(KVH - 1)

            @block.gpsimd
            def _(gp):
                for step in range(STEPS):
                    k, t = divmod(step, KT)
                    r, i = rows_of(t), step % 2
                    gp.wait_ge(p32_ready, step + 1)
                    if t == 0:
                        if k >= 2:
                            gp.wait_ge(side_taken, at[("sum", k - 2, 0)] + 1)
                        nc.gpsimd.tensor_copy(acc[:, k % 2, :], p32[:, i, :]).then_inc(summed, 1)
                    else:
                        gp.wait_ge(summed, step)
                        nc.gpsimd.tensor_tensor(acc[0:r, k % 2, :], acc[0:r, k % 2, :], p32[0:r, i, :], ALU.add).then_inc(summed, 1)

            @block.vector
            def _(ve):
                link = chain(ve, dve_step)

                def side(item):
                    kind, k, n = item
                    ve.wait_ge(side_ready, at[item] + 1)
                    if kind == "piece":
                        c, m = n // NCH, CHUNKS[n % NCH][1]
                        nc.vector.tensor_reduce(tops[:, c, n % NCH:n % NCH + 1], ps[:, 6 + n % 2, 0:m], AX_X, ALU.max)\
                            .then_inc(side_taken, 1)
                        if n == PIECES - 1:
                            ve.wait_ge(side_taken, at[item] + 1)
                            link(nc.vector.tensor_reduce(top[:], tops[:], AX_X, ALU.max))
                            nc.vector.tensor_scalar(shift[:], top[:], -1.0, None, ALU.mult).then_inc(shift_ready, 1)
                    elif kind == "turn":
                        if k >= 2:
                            ve.wait_ge(scored, KT * (k - 1))
                        nc.vector.tensor_tensor(own[:, k % 2], bcast(ps[0:8, 6, 0:P], 1, 8), bcast(own8[:], 2, P),
                                                ALU.mult).then_inc(side_taken, 1)
                    else:
                        if k >= 1:
                            ve.wait_ge(att_lo, k)
                        nc.vector.reciprocal(inv[:], ps[:, 6:8, :].rearrange("p a n -> p (a n)")).then_inc(side_taken, 1)
                        ve.wait_ge(side_taken, at[item] + 1)

                def scale(k):
                    ve.wait_ge(raw_ready, k + 1)
                    if k >= 1:
                        ve.wait_ge(att_lo, k)
                        ve.wait_ge(att_hi, k)
                    nc.vector.tensor_tensor(scaled[:], raw[:], inv[:], ALU.mult).then_inc(scaled_ready, 1)

                def rest(k):
                    ve.wait_ge(att_hi, k + 1)
                    heads = slice(REP * k, REP * (k + 1))
                    nc.vector.tensor_tensor(att[1][:, heads, :], scaled[:].rearrange("p (h n) -> p h n", h=REP), att[0][:, heads, :],
                                            ALU.subtract).then_inc(att_lo, 1)

                for item in before:
                    side(item)
                for step in range(STEPS):
                    k, t = divmod(step, KT)
                    r, i = rows_of(t), step % 2
                    for item in side_work(step):
                        side(item)
                    ve.wait_ge(hi_ready, step + 1)
                    if step >= 2:
                        ve.wait_ge(weighed, step - 1)
                    nc.vector.tensor_tensor(p_lo[0:r, i, :], p32[0:r, i, :], p_hi[0:r, i, :], ALU.subtract).then_inc(lo_ready, 1)
                    if t == 1 and k >= 1:
                        scale(k - 1)
                    if t == 4 and k >= 1:
                        rest(k - 1)
                side(("sum", KVH - 1, 0))
                scale(KVH - 1)
                rest(KVH - 1)
                link(nc.vector.tensor_copy(row[:], x[:, bass.ds(b * QT, QT), :]))
                ve.wait_ge(out_ready, QT)
                link(nc.vector.tensor_tensor(row[:], row[:], ps[:, 6:8, 0:DM], ALU.add))
                link(nc.vector.tensor_copy(x[:, bass.ds(b * QT, QT), :], row[:]))


def expert_ffn(nc, x, const, a, w):
    with Stage(nc, "moe") as st:
        sb, sem = st.sb, st.sem
        ps = st.banks()
        E, M = 8, 128
        w_gate = sb("w_gate", [P, DC, E])
        w_up = [sb(f"w_up{i}", [P, E, DC, M]) for i in range(2)]
        w_down = sb("w_down", [P, E, DM])
        number = sb("number", [P, E])
        stats = sb("stats", [P, TILES, 6])
        mean_var = sb("mean_var", [P, TILES, 2])
        rs = sb("rs", [P, 6, TILES])
        half = sb("half", [P, TILES])
        xn = sb("xn", [P, TILES, DM])
        xn_t = sb("xn_t", [P, DC, TOK])
        logits = sb("logits", [P, TILES, E])
        best = sb("best", [P, TILES, E])
        which = sb("which", [P, TILES, E], U32)
        which_f = sb("which_f", [P, TILES, E])
        two = sb("two", [P, 3, TILES])
        hit = sb("hit", [P, 2, TILES, E])
        share = sb("share", [P, TILES, E])
        act = sb("act", [P, 2, 512])
        inner = sb("inner", [P, 2, TOK])

        loaded = sem("weights_loaded")
        dve_step, rs_ready, rs_done = sem("dve_step"), sem("rs_ready"), sem("rs_done")
        xn_ready, xt_ready, xnt_ready = sem("xn_ready"), sem("xt_ready"), sem("xnt_ready")
        logits_ready, diff_ready, exp_ready = sem("logits_ready"), sem("diff_ready"), sem("exp_ready")
        up_ready, act_ready, inner_ready, down_ready, added = sem("up_ready"), sem("act_ready"), sem("inner_ready"), sem("down_ready"), sem("added")

        with nc.Block() as block:
            @block.sync
            def _(sp):
                sp.dma_start(w_gate[:], w["w_gate"].rearrange("(c p) n -> p c n", p=P)).then_inc(loaded, 16)
                sp.dma_start(number[:], a["c_number"].partition_broadcast(P)).then_inc(loaded, 16)
                for i in range(2):
                    sp.dma_start(w_up[i][:], w[f"wi_{i}"].rearrange("e (c p) m -> p e c m", p=P)).then_inc(loaded, 16)
                sp.dma_start(w_down[:], w["wo"].rearrange("e p n -> p e n")).then_inc(loaded, 16)

            @block.gpsimd
            def _(gp):
                nc.gpsimd.memset(half[:], -0.5).then_inc(rs_done, 1)
                gp.wait_ge(rs_done, 1)
                gp.wait_ge(rs_ready, 1)
                nc.gpsimd.tensor_tensor(rs[:, 1, :], rs[:, 0, :], half[:], ALU.pow).then_inc(rs_done, 1)

            @block.vector
            def _(ve):
                link = chain(ve, dve_step)
                row_stats(nc, link, x, stats, mean_var)
                nc.vector.tensor_scalar(rs[:, 0, :], mean_var[:, :, 1], 1e-5, None, ALU.add).then_inc(rs_ready, 1)
                ve.wait_ge(rs_done, 2)
                for t in range(TILES):
                    nc.vector.tensor_scalar(xn[:, t, :], x[:, t, :], mean_var[:, t, 0:1], rs[:, 1, t:t + 1],
                                            ALU.subtract, ALU.mult).then_inc(xn_ready, 1)
                ve.wait_ge(loaded, 80)
                ve.wait_ge(logits_ready, 1)
                link(nc.vector.tensor_copy(logits[:].rearrange("p t e -> p (t e)"), ps[:, 4, 0:TILES * E]))
                for t in range(TILES):
                    last = nc.vector.max(best[:, t, :], logits[:, t, :])
                link(last)
                for t in range(TILES):
                    last = nc.vector.max_index(which[:, t, :], best[:, t, :], logits[:, t, :])
                nc.vector.tensor_tensor(two[:, 0, :], best[:, :, 1], best[:, :, 0], ALU.subtract).then_inc(diff_ready, 1)
                ve.wait_ge(diff_ready, 1)
                link(nc.vector.tensor_copy(which_f[:], which[:]))
                ve.wait_ge(exp_ready, 1)
                link(nc.vector.tensor_scalar(two[:, 1, :], two[:, 0, :], 1.0, None, ALU.add))
                link(nc.vector.reciprocal(two[:, 1, :], two[:, 1, :]))
                link(nc.vector.tensor_tensor(two[:, 2, :], two[:, 0, :], two[:, 1, :], ALU.mult))
                for i in range(2):
                    last = nc.vector.tensor_tensor(hit[:, i], bcast(number[:], 1, TILES), bcast(which_f[:, :, i], 2, E), ALU.is_equal)
                link(last)
                for i in range(2):
                    last = nc.vector.tensor_tensor(hit[:, i], hit[:, i], bcast(two[:, 1 + i, :], 2, E), ALU.mult)
                link(last)
                link(nc.vector.tensor_tensor(share[:], hit[:, 0], hit[:, 1], ALU.add))

                def multiply(e):
                    for n in range(2):
                        j = 2 * e + n
                        ve.wait_ge(act_ready, j + 1)
                        nc.vector.tensor_tensor(inner[:, e % 2, n * 512:(n + 1) * 512], act[:, n, :], ps[:, 2 * n + 1, :],
                                                ALU.mult).then_inc(inner_ready, 1)

                multiply(0)
                for e in range(E):
                    if e + 1 < E:
                        multiply(e + 1)
                    for t in range(TILES):
                        j = TILES * e + t
                        ve.wait_ge(down_ready, j + 1)
                        if e >= 1:
                            ve.wait_ge(added, j + 1 - TILES)
                        nc.vector.scalar_tensor_tensor(x[:, t, :], ps[:, 4 + t % 4, 0:DM], share[:, t, e:e + 1], x[:, t, :],
                                                       ALU.mult, ALU.add).then_inc(added, 1)

            @block.scalar
            def _(ac):
                for b in range(BATCH):
                    ac.wait_ge(xt_ready, b + 1)
                    nc.scalar.copy(xn_t[:, :, b * SEQ:(b + 1) * SEQ],
                                   ps[:, b, :].rearrange("p (c n) -> p c n", c=DC)).then_inc(xnt_ready, 1)
                ac.wait_ge(diff_ready, 1)
                nc.scalar.activation(two[:, 0, :], two[:, 0, :], ACT.Exp).then_inc(exp_ready, 1)
                for j in range(2 * E):
                    ac.wait_ge(up_ready, j + 1)
                    if j >= 2:
                        ac.wait_ge(inner_ready, j - 1)
                    nc.scalar.activation(act[:, j % 2, :], ps[:, 2 * (j % 2), :], ACT.Silu).then_inc(act_ready, 1)

            @block.tensor
            def _(pe):
                for b in range(BATCH):
                    pe.wait_ge(xn_ready, 2 * b + 2)
                    for c in range(DC):
                        for q in range(QT):
                            last = nc.tensor.transpose(ps[:, b, c * SEQ + q * P:c * SEQ + (q + 1) * P],
                                                       xn[:, b * QT + q, c * P:(c + 1) * P], const["ident"][:])
                    last.then_inc(xt_ready, 1)
                pe.wait_ge(xnt_ready, BATCH)
                pe.wait_ge(loaded, 80)
                for t in range(TILES):
                    for c in range(DC):
                        last = nc.tensor.matmul(ps[:, 4, t * E:(t + 1) * E], xn_t[:, c, t * P:(t + 1) * P], w_gate[:, c, :],
                                                start=(c == 0), stop=(c == DC - 1))
                last.then_inc(logits_ready, 1)

                def up(e):
                    for n in range(2):
                        if e >= 1:
                            pe.wait_ge(inner_ready, 2 * e - 1 + n)
                        for i in range(2):
                            for c in range(DC):
                                last = nc.tensor.matmul(ps[:, 2 * n + i, :], w_up[i][:, e, c, :], xn_t[:, c, n * 512:(n + 1) * 512],
                                                        start=(c == 0), stop=(c == DC - 1))
                        last.then_inc(up_ready, 1)

                up(0)
                pe.wait_ge(diff_ready, 1)
                for e in range(E):
                    if e + 1 < E:
                        up(e + 1)
                    pe.wait_ge(inner_ready, 2 * e + 2)
                    for t in range(TILES):
                        j = TILES * e + t
                        if j >= 4:
                            pe.wait_ge(added, j - 3)
                        nc.tensor.matmul(ps[:, 4 + t % 4, 0:DM], inner[:, e % 2, t * P:(t + 1) * P], w_down[:, e, :],
                                         start=True, stop=True).then_inc(down_ready, 1)



def run_self(nc, x, const, a, layer):
    w = layer("L0_attn_")
    w.update(cos=a["c_self_cos"], sin=a["c_self_sin"], causal=a["c_self_causal"])
    self_attention(nc, x, const, w)


def run_memory(nc, x, const, a, layer):
    memory_attention(nc, x, const, a)


def run_ffn(nc, x, const, a, layer):
    ternary_ffn(nc, x, const, a)


def run_scan(nc, x, const, a, layer):
    gated_scan(nc, x, const, a, layer("L1_attn_"))


def run_cross(nc, x, const, a, layer):
    cross_attention(nc, x, const, a, layer("L1_xattn_"))


def run_experts(nc, x, const, a, layer):
    expert_ffn(nc, x, const, a, layer("L1_ffn_"))


STAGES = [run_self, run_memory, run_ffn, run_scan, run_cross, run_experts]


def decoder(nc, a, out):
    with Stage(nc, "model") as st:
        x = st.sb("x", [P, TILES, DM])
        ident = st.sb("ident", [P, P])
        ident_b = st.sb("ident_b", [P, P], BF16)
        half_pi = st.sb("half_pi", [P, 1])
        const = {"ident": ident, "ident_b": ident_b, "half_pi": half_pi}
        x_loaded, x_stored = st.sem("x_loaded"), st.sem("x_stored")
        with nc.Block() as block:
            @block.sync
            def _(sp):
                sp.dma_start(x[:], a["x"].rearrange("b (t p) d -> p (b t) d", p=P)).then_inc(x_loaded, 16)
                sp.dma_start(ident[:], a["c_ident"]).then_inc(x_loaded, 16)
                sp.wait_ge(x_loaded, 32)

            @block.vector
            def _(ve):
                nc.vector.memset(half_pi[:], math.pi / 2)
                ve.wait_ge(x_loaded, 32)
                nc.vector.tensor_copy(ident_b[:], ident[:])

        def layer(prefix):
            return {k[len(prefix):]: v for k, v in a.items() if k.startswith(prefix)}

        for n, stage in enumerate(STAGES):
            stage(nc, x, const, a, layer)
        with nc.Block() as block:
            @block.sync
            def _(sp):
                sp.dma_start(out.rearrange("b (t p) d -> p (b t) d", p=P), x[:]).then_inc(x_stored, 16)
                sp.wait_ge(x_stored, 16)


def constants():
    c = {}
    c["c_ident"] = np.eye(P, dtype=np.float32)
    c["c_number"] = np.arange(8, dtype=np.float32)
    pick = np.zeros((BATCH, BATCH, P), np.float32)
    for b in range(BATCH):
        pick[b, b] = 1.0
    c["c_pick"] = pick
    pos = np.arange(SEQ, dtype=np.float32)
    f0 = np.arange(0, HD0, 2, dtype=np.float32) / np.float32(HD0) * np.log(np.float32(30000.0))
    ang = (pos[:, None] * f0[None, :]).astype(np.float32)
    for n, f in (("cos", np.cos), ("sin", np.sin)):
        c["c_self_" + n] = f(ang).astype(np.float32).reshape(QT, P, HD0 // 2).transpose(1, 0, 2).copy()
    causal = np.zeros((P, SEQ), np.float32)
    causal[:, P:] = np.where(np.tril(np.ones((P, P), bool)), 0.0, MASKED)
    c["c_self_causal"] = causal
    f1 = 1.0 / np.float32(10000.0) ** (np.arange(0, 16, 2, dtype=np.float32) / np.float32(16))
    ang = (pos[:, None] * f1[None, :].astype(np.float32)).astype(np.float32)
    ch = np.arange(P)
    c["c_scan_cos"] = np.cos(ang).astype(np.float32)[:, ch % 8].T.copy()
    c["c_scan_sin"] = (np.sin(ang).astype(np.float32)[:, ch % 8].T * np.where(ch % 16 < 8, -1.0, 1.0)[:, None]).astype(np.float32)
    c["c_scan_same"] = (ch[:, None] % 16 == np.arange(16)[None, :]).astype(np.float32)
    c["c_cross_freq"] = (1.0 / np.float32(10000.0) ** (np.arange(0, P, 2, dtype=np.float32) / np.float32(P))).astype(np.float32)
    c["c_cross_own"] = np.eye(8, dtype=np.float32)
    return c


def layouts(i):
    def column(v):
        return v.reshape(-1, P).T
    o = {k: i[k] for k in ("x", "ctx_2048", "L0_attn_Wq", "L0_attn_bq", "L0_attn_Wkv", "L0_attn_bkv", "L0_attn_Wo", "L0_attn_bo",
                           "L0_attn_ln_g", "L0_attn_ln_b", "L1_xattn_q_norm_w", "L1_xattn_k_norm_w",
                           "L1_ffn_w_gate", "L1_ffn_wi_0", "L1_ffn_wi_1", "L1_ffn_wo")}
    for k in ("L0_attn_qn_g", "L0_attn_qn_b", "L0_attn_kvn_g", "L0_attn_kvn_b", "L1_attn_norm_scale", "L1_attn_conv_b",
              "L1_attn_dt_bias"):
        o[k] = column(i[k])
    o["L1_attn_conv_w"] = i["L1_attn_conv_w"].reshape(DC, P, 4).transpose(1, 0, 2)
    for k in ("L0_ffn_w_fc", "L0_ffn_w_proj", "L1_attn_in_proj_w", "L1_attn_out_proj_w", "L1_xattn_Wq", "L1_xattn_Wk",
              "L1_xattn_Wv", "L1_xattn_Wo"):
        o[k] = i[k].T
    o["mix_rows"] = np.repeat(i["L1_attn_head_mix"], HD0, axis=0).reshape(DC, P, HEADS).transpose(1, 0, 2)
    place = np.zeros((BATCH, KT * P), i["pos_BxS2"].dtype)
    place[:, 0:SEQ] = i["itok_BxS_4096_4607"]
    place[:, SEQ:KEYS] = i["pos_BxS2"]
    o["positions"] = place.reshape(BATCH, KT, P).transpose(0, 2, 1)
    o["ctx_t"] = i["ctx_2048"].transpose(0, 2, 1)
    o["mask_BxS2_bk0"] = i["mask_BxS2_bk0"]
    return o


def kernel(**inputs):
    import concourse.bacc as _bacc
    from concourse.bass_utils import run_bass_kernel_spmd as _run

    nc = _bacc.Bacc("TRN2", target_bir_lowering=False, num_devices=1)
    arrays, args = {}, {}
    inputs = {k: np.asarray(v) for k, v in inputs.items()}
    for name, value in {**layouts(inputs), **constants()}.items():
        v = np.ascontiguousarray(value)
        arrays[f"in_{name}"] = v
        args[name] = nc.dram_tensor(f"in_{name}", v.shape, mybir.dt.from_np(v.dtype), kind="ExternalInput").ap()
    out = nc.dram_tensor("out_0", (BATCH, SEQ, DM), F32, kind="ExternalOutput").ap()
    decoder(nc, args, out)
    r = _run(nc, [arrays], core_ids=[0])
    return r.results[0]["out_0"]
```

```python
import math
from contextlib import ExitStack

import numpy as np

import concourse.bass as bass
from concourse import mybir

ALU = mybir.AluOpType
ACT = mybir.ActivationFunctionType
F32 = mybir.dt.float32
BF16 = mybir.dt.bfloat16
F16 = mybir.dt.float16
I32 = mybir.dt.int32
U32 = mybir.dt.uint32
U8 = mybir.dt.uint8
AX_X = mybir.AxisListType.X

P = 128
BATCH, SEQ, DM = 4, 256, 256
QT = SEQ // P
TILES = BATCH * QT
TOK = BATCH * SEQ
DC = DM // P
CTX = 1601
HEADS = 16
HD0 = DM // HEADS
FF = 4 * DM
FC = FF // P
MASKED = -1.0e30


class Stage:

    def __init__(self, nc, name):
        self.nc, self.name, self.ctx, self.numbers = nc, name, ExitStack(), []

    def __enter__(self):
        self.ctx.__enter__()
        return self

    def __exit__(self, *a):
        if self.numbers and a[0] is None:
            self.rewind()
        return self.ctx.__exit__(*a)

    def sb(self, name, shape, dt=F32):
        return self.ctx.enter_context(self.nc.sbuf_tensor(f"{self.name}_{name}", shape, dt))

    def banks(self):
        return self.ctx.enter_context(self.nc.psum_tensor(f"{self.name}_banks", [P, 8, 512], F32))

    def sem(self, name):
        s = self.ctx.enter_context(self.nc.semaphore(f"{self.name}_{name}"))
        self.numbers.append(s.num)
        return s

    def rewind(self):
        numbers, runs = sorted(self.numbers), []
        for n in numbers:
            if runs and runs[-1][1] == n:
                runs[-1][1] = n + 1
            else:
                runs.append([n, n + 1])
        for first, end in runs:
            self.nc.all_engine_barrier(sems_to_clear=range(first, end))


def chain(engine, sem):
    done = [0]

    def link(ins):
        done[0] += 1
        ins.then_inc(sem, 1)
        engine.wait_ge(sem, done[0])

    return link


def row_stats(nc, link, x, stats, mean_var):
    for t in range(TILES):
        last = nc.vector.bn_stats(stats[:, t, :], x[:, t, :])
    link(last)
    for t in range(TILES):
        last = nc.vector.bn_aggr(mean_var[:, t, :], stats[:, t, :])
    link(last)


def bcast(ap, axis, n):
    shape = list(ap.shape)
    shape.insert(axis, n)
    return ap.unsqueeze(axis).to_broadcast(shape)


def self_attention(nc, x, const, w):
    with Stage(nc, "self") as st:
        sb, sem = st.sb, st.sem
        ps = st.banks()
        w_qk = sb("w_qk", [P, DC, 2 * DM])
        w_v = sb("w_v", [P, DC, DM])
        w_o = sb("w_o", [P, DC, DM])
        b_qk = sb("b_qk", [P, 2 * DM])
        b_v = sb("b_v", [P, DM])
        b_o = sb("b_o", [P, DM])
        gains = sb("gains", [P, 4, DC])
        ln_g = sb("ln_g", [P, HD0])
        ln_b = sb("ln_b", [P, HD0])
        cos = sb("cos", [P, QT, HD0 // 2])
        sin = sb("sin", [P, QT, HD0 // 2])
        causal = sb("causal", [P, SEQ])
        stats = sb("stats", [P, TILES, 6])
        mean_var = sb("mean_var", [P, TILES, 2])
        rs = sb("rs", [P, 6, TILES])
        xn = sb("xn", [P, TILES, DM])
        qin_t = sb("qin_t", [P, DC, TOK])
        kvin_t = sb("kvin_t", [P, DC, TOK])
        qk = sb("qk", [P, TILES, 2 * DM])
        v = sb("v", [P, TILES, DM])
        turn = sb("turn", [P, 2, HD0 // 2])
        by_cos = sb("by_cos", [P, 2 * HEADS, HD0 // 2, 2])
        by_sin = sb("by_sin", [P, 2 * HEADS, HD0 // 2, 2])
        rot = sb("rot", [P, 2 * HEADS, HD0])
        hstat = sb("hstat", [P, 4, 2 * HEADS])
        gained = sb("gained", [P, 2, 2 * HEADS, HD0])
        hinv = sb("hinv", [P, 2, 2 * HEADS])
        padded = sb("padded", [P, 2, 2 * HEADS, 32])
        q_t = sb("q_t", [P, 4, TOK])
        k_own = sb("k_own", [P, 4, 4, TOK])
        sm = sb("sm", [P, 3, 4, SEQ])
        mx = sb("mx", [P, 2, 4])
        shift = sb("shift", [P, 2, 4])
        sums = sb("sums", [P, TILES, HEADS])
        inv = sb("inv", [P, TILES, HEADS])
        p_t = sb("p_t", [P, 2, 8, P])
        att = sb("att", [P, TILES, DM])
        att_t = sb("att_t", [P, DC, TOK])

        loaded, bias_added = sem("weights_loaded"), sem("bias_added")
        dve_step, rs_ready, rs_done = sem("dve_step"), sem("rs_ready"), sem("rs_done")
        xn_ready, xt_ready, qin_ready, kvin_ready = sem("xn_ready"), sem("xt_ready"), sem("qin_ready"), sem("kvin_ready")
        qkv_ready, qkv_taken = sem("qkv_ready"), sem("qkv_taken")
        hvar_ready, hrs_done, centred, divided = sem("hvar_ready"), sem("hrs_done"), sem("centred"), sem("divided")
        padded_ready, padded_t, qkt_ready = sem("padded_ready"), sem("padded_t"), sem("qkt_ready")
        scores_ready, scores_taken, shift_ready, probs_ready = sem("scores_ready"), sem("scores_taken"), sem("shift_ready"), sem("probs_ready")
        probs_t, pt_ready, att_ready = sem("probs_t"), sem("pt_ready"), sem("att_ready")
        att_tr, attt_ready, out_ready, out_taken = sem("att_tr"), sem("attt_ready"), sem("out_ready"), sem("out_taken")
        pv_done, zeroed = sem("pv_done"), sem("zeroed")

        GROUPS = HEADS // 4
        JOBS = TILES * GROUPS

        def keys(job):
            return P * (job // GROUPS % QT + 1)

        with nc.Block() as block:
            @block.sync
            def _(sp):
                for dst, src in (
                    (gains[:, 0, :], w["qn_g"]),
                    (gains[:, 1, :], w["qn_b"]),
                    (gains[:, 2, :], w["kvn_g"]),
                    (gains[:, 3, :], w["kvn_b"]),
                    (w_qk[:, :, 0:DM], w["Wq"].rearrange("(c p) n -> p c n", p=P)),
                    (w_qk[:, :, DM:2 * DM], w["Wkv"][:, 0:DM].rearrange("(c p) n -> p c n", p=P)),
                    (w_v[:], w["Wkv"][:, DM:2 * DM].rearrange("(c p) n -> p c n", p=P)),
                    (b_qk[:, 0:DM], w["bq"].partition_broadcast(P)),
                    (b_qk[:, DM:2 * DM], w["bkv"][0:DM].partition_broadcast(P)),
                    (b_v[:], w["bkv"][DM:2 * DM].partition_broadcast(P)),
                    (b_o[:], w["bo"].partition_broadcast(P)),
                    (ln_g[:], w["ln_g"].partition_broadcast(P)),
                    (ln_b[:], w["ln_b"].partition_broadcast(P)),
                    (cos[:], w["cos"]), (sin[:], w["sin"]), (causal[:], w["causal"]),
                    (w_o[:], w["Wo"].rearrange("(c p) n -> p c n", p=P)),
                ):
                    sp.dma_start(dst, src).then_inc(loaded, 16)

            @block.gpsimd
            def _(gp):
                nc.gpsimd.memset(k_own[:], 0.0).then_inc(zeroed, 1)
                gp.wait_ge(xn_ready, TILES)
                gp.wait_ge(loaded, 16 * 17)
                nc.gpsimd.tensor_tensor(x[:], x[:], bcast(b_o[:], 1, TILES), ALU.add).then_inc(bias_added, 1)
                for t in range(TILES):
                    gp.wait_ge(centred, t + 1)
                    nc.gpsimd.tensor_tensor(gained[:, t % 2], gained[:, t % 2], bcast(hinv[:, t % 2, :], 2, HD0), ALU.mult).then_inc(divided, 1)
                    gp.wait_ge(divided, t + 1)
                    if t >= 2:
                        gp.wait_ge(padded_t, t - 1)
                    nc.gpsimd.tensor_tensor(padded[:, t % 2, :, 0:HD0], gained[:, t % 2], bcast(ln_b[:], 1, 2 * HEADS),
                                            ALU.add).then_inc(padded_ready, 1)

            @block.vector
            def _(ve):
                link = chain(ve, dve_step)
                nc.vector.memset(padded[:], 0.0)
                row_stats(nc, link, x, stats, mean_var)
                nc.vector.tensor_scalar(rs[:, 0, :], mean_var[:, :, 1], 1e-5, None, ALU.add).then_inc(rs_ready, 1)
                ve.wait_ge(rs_done, 1)
                link(nc.vector.reciprocal(rs[:, 1, :], rs[:, 1, :]))
                link(nc.vector.tensor_tensor(rs[:, 2, :], rs[:, 1, :], rs[:, 1, :], ALU.mult))
                link(nc.vector.tensor_tensor(rs[:, 4, :], rs[:, 2, :], mean_var[:, :, 1], ALU.mult))
                nc.vector.tensor_scalar(rs[:, 2, :], rs[:, 4, :], 1e-5, None, ALU.add).then_inc(rs_ready, 1)
                ve.wait_ge(rs_done, 2)
                nc.vector.tensor_scalar(rs[:, 4, :], rs[:, 4, :], float(DM), None, ALU.mult).then_inc(rs_ready, 1)
                link(nc.vector.reciprocal(rs[:, 3, :], rs[:, 3, :]))
                ve.wait_ge(rs_done, 3)
                link(nc.vector.tensor_tensor(rs[:, 2, :], rs[:, 1, :], rs[:, 3, :], ALU.mult))
                link(nc.vector.tensor_scalar(rs[:, 5, :], rs[:, 5, :], float(HD0) ** -0.25, None, ALU.mult))
                for t in range(TILES):
                    nc.vector.tensor_scalar(xn[:, t, :], x[:, t, :], mean_var[:, t, 0:1], rs[:, 2, t:t + 1],
                                            ALU.subtract, ALU.mult).then_inc(xn_ready, 1)
                ve.wait_ge(loaded, 16 * 17)
                for b in range(BATCH):
                    ve.wait_ge(xt_ready, b + 1)
                    for c in range(DC):
                        last = nc.vector.tensor_scalar(kvin_t[:, c, b * SEQ:(b + 1) * SEQ], ps[:, b, c * SEQ:(c + 1) * SEQ],
                                                       gains[:, 2, c:c + 1], gains[:, 3, c:c + 1], ALU.mult, ALU.add)
                    last.then_inc(kvin_ready, 1)

                def take_qkv(t):
                    ve.wait_ge(qkv_ready, t + 1)
                    nc.vector.tensor_tensor(qk[:, t, :], ps[:, 4 + t % 2, :], b_qk[:], ALU.add)
                    ins = nc.vector.tensor_tensor(v[:, t, :], ps[:, 6 + t % 2, 0:DM], b_v[:], ALU.add)
                    ins.then_inc(qkv_taken, 1)
                    ve.wait_ge(qkv_taken, t + 1)

                take_qkv(0)
                for t in range(TILES):
                    if t + 1 < TILES:
                        take_qkv(t + 1)
                    nc.vector.tensor_scalar(turn[:, 0, :], cos[:, t % QT, :], rs[:, 5, t:t + 1], None, ALU.mult)
                    link(nc.vector.tensor_scalar(turn[:, 1, :], sin[:, t % QT, :], rs[:, 5, t:t + 1], None, ALU.mult))
                    qk_v = qk[:, t, :].rearrange("p (h d e) -> p h d e", h=2 * HEADS, e=2)
                    wide = [P, 2 * HEADS, HD0 // 2, 2]
                    nc.vector.tensor_tensor(by_cos[:], qk_v, turn[:, 0, :].unsqueeze(1).unsqueeze(3).to_broadcast(wide), ALU.mult)
                    link(nc.vector.tensor_tensor(by_sin[:], qk_v, turn[:, 1, :].unsqueeze(1).unsqueeze(3).to_broadcast(wide), ALU.mult))
                    rot_v = rot[:].rearrange("p h (d e) -> p h d e", e=2)
                    nc.vector.tensor_tensor(rot_v[:, :, :, 0], by_cos[:, :, :, 0], by_sin[:, :, :, 1], ALU.subtract)
                    link(nc.vector.tensor_tensor(rot_v[:, :, :, 1], by_cos[:, :, :, 1], by_sin[:, :, :, 0], ALU.add))
                    link(nc.vector.tensor_reduce(hstat[:, 0, :], rot[:], AX_X, ALU.add))
                    link(nc.vector.tensor_scalar(hstat[:, 1, :], hstat[:, 0, :], 1.0 / HD0, None, ALU.mult))
                    link(nc.vector.tensor_tensor(rot[:], rot[:], bcast(hstat[:, 1, :], 2, HD0), ALU.subtract))
                    sq = by_cos[:].rearrange("p h d e -> p h (d e)")
                    link(nc.vector.tensor_tensor(sq, rot[:], rot[:], ALU.mult))
                    link(nc.vector.tensor_reduce(hstat[:, 0, :], sq, AX_X, ALU.add))
                    nc.vector.tensor_scalar(hstat[:, 2, :], hstat[:, 0, :], 1.0 / HD0, 1e-5, ALU.mult, ALU.add).then_inc(hvar_ready, 1)
                    if t >= 2:
                        ve.wait_ge(padded_ready, t - 1)
                    link(nc.vector.tensor_tensor(gained[:, t % 2], rot[:], bcast(ln_g[:], 1, 2 * HEADS), ALU.mult))
                    ve.wait_ge(hrs_done, t + 1)
                    nc.vector.reciprocal(hinv[:, t % 2, :], hstat[:, 3, :]).then_inc(centred, 1)
                    ve.wait_ge(centred, t + 1)

                def normalise(t):
                    ve.wait_ge(pv_done, GROUPS * (t + 1))
                    link(nc.vector.reciprocal(inv[:, t, :], sums[:, t, :]))
                    nc.vector.tensor_tensor(att[:, t, :].rearrange("p (h d) -> p h d", h=HEADS),
                                            ps[:, 2 + t % 2, 0:DM].rearrange("p (h d) -> p h d", h=HEADS),
                                            bcast(inv[:, t, :], 2, HD0), ALU.mult).then_inc(att_ready, 1)

                for j in range(JOBS):
                    nk, k, m = keys(j), j % 2, j % 3
                    ve.wait_ge(scores_ready, j + 1)
                    if j >= 3:
                        ve.wait_ge(probs_t, j - 2)
                    ins = nc.vector.tensor_tensor(sm[:, m, :, 0:nk],
                                                  ps[:, 4 + 2 * k:6 + 2 * k, :].rearrange("p a (h n) -> p (a h) n", h=2)[:, :, 0:nk],
                                                  bcast(causal[:, SEQ - nk:SEQ], 1, 4), ALU.add)
                    ins.then_inc(scores_taken, 1)
                    ve.wait_ge(scores_taken, j + 1)
                    link(nc.vector.tensor_reduce(mx[:, k, :], sm[:, m, :, 0:nk], AX_X, ALU.max))
                    nc.vector.tensor_scalar(shift[:, k, :], mx[:, k, :], -float(HD0) ** -0.5, None, ALU.mult).then_inc(shift_ready, 1)
                    if j % GROUPS == 2 and j > GROUPS:
                        normalise(j // GROUPS - 1)
                normalise(TILES - 1)
                for t in range(TILES):
                    ve.wait_ge(out_ready, t + 1)
                    if t == 0:
                        ve.wait_ge(bias_added, 1)
                    nc.vector.tensor_tensor(x[:, t, :], x[:, t, :], ps[:, 4 + t % 4, 0:DM], ALU.add).then_inc(out_taken, 1)

            @block.scalar
            def _(ac):
                for n, (src, dst) in enumerate(((0, 1), (2, 3), (4, 5))):
                    ac.wait_ge(rs_ready, n + 1)
                    nc.scalar.activation(rs[:, dst, :], rs[:, src, :], ACT.Sqrt).then_inc(rs_done, 1)
                ac.wait_ge(loaded, 16 * 17)
                for b in range(BATCH):
                    ac.wait_ge(kvin_ready, b + 1)
                    for c in range(DC):
                        last = nc.scalar.activation(qin_t[:, c, b * SEQ:(b + 1) * SEQ], ps[:, b, c * SEQ:(c + 1) * SEQ],
                                                    ACT.Identity, bias=gains[:, 1, c:c + 1], scale=gains[:, 0, c:c + 1])
                    last.then_inc(qin_ready, 1)
                ac.wait_ge(zeroed, 1)

                def deviate(t):
                    ac.wait_ge(hvar_ready, t + 1)
                    nc.scalar.activation(hstat[:, 3, :], hstat[:, 2, :], ACT.Sqrt).then_inc(hrs_done, 1)

                deviate(0)
                for t in range(TILES):
                    if t + 1 < TILES:
                        deviate(t + 1)
                    ac.wait_ge(padded_t, t + 1)
                    bank = ps[:, 2 * (t % 2):2 * (t % 2) + 2, :].rearrange("p a (g n) -> p a g n", g=4)
                    nc.scalar.copy(q_t[:, :, t * P:(t + 1) * P], bank[:, 0])
                    for i in range(4):
                        rows = slice(32 * i, 32 * i + 32)
                        last = nc.scalar.copy(k_own[rows, :, i, t * P:(t + 1) * P], bank[rows, 1])
                    last.then_inc(qkt_ready, 1)

                def copy_pt(j):
                    ac.wait_ge(probs_t, j + 1)
                    if j >= 2:
                        ac.wait_ge(pv_done, j - 1)
                    n = 4 * keys(j) // P
                    nc.scalar.copy(p_t[:, j % 2, 0:n, :],
                                   ps[:, 0:2, :].rearrange("p a (g n) -> p (a g) n", g=4)[:, 0:n, :]).then_inc(pt_ready, 1)

                for j in range(JOBS):
                    k, m, nk, t = j % 2, j % 3, keys(j), j // GROUPS
                    ac.wait_ge(shift_ready, j + 1)
                    for i in range(4):
                        h = j % GROUPS * 4 + i
                        last = nc.scalar.activation(sm[:, m, i, 0:nk], sm[:, m, i, 0:nk], ACT.Exp, bias=shift[:, k, i:i + 1],
                                                    scale=float(HD0) ** -0.5, accum_out=sums[:, t, h:h + 1])
                    last.then_inc(probs_ready, 1)
                    if j >= 1:
                        copy_pt(j - 1)
                copy_pt(JOBS - 1)
                for b in range(BATCH):
                    ac.wait_ge(att_tr, b + 1)
                    nc.scalar.copy(att_t[:, :, b * SEQ:(b + 1) * SEQ],
                                   ps[:, b, :].rearrange("p (c n) -> p c n", c=DC)).then_inc(attt_ready, 1)

            @block.tensor
            def _(pe):
                for b in range(BATCH):
                    pe.wait_ge(xn_ready, 2 * b + 2)
                    for c in range(DC):
                        for q in range(QT):
                            last = nc.tensor.transpose(ps[:, b, c * SEQ + q * P:c * SEQ + (q + 1) * P],
                                                       xn[:, b * QT + q, c * P:(c + 1) * P], const["ident"][:])
                    last.then_inc(xt_ready, 1)
                def project(t):
                    pe.wait_ge(qin_ready, t // QT + 1)
                    pe.wait_ge(kvin_ready, t // QT + 1)
                    if t >= 2:
                        pe.wait_ge(qkv_taken, t - 1)
                    tok = slice(t * P, (t + 1) * P)
                    for dst, src, wt in ((ps[:, 4 + t % 2, 0:DM], qin_t, w_qk[:, :, 0:DM]),
                                         (ps[:, 4 + t % 2, DM:2 * DM], kvin_t, w_qk[:, :, DM:2 * DM]),
                                         (ps[:, 6 + t % 2, 0:DM], kvin_t, w_v)):
                        for c in range(DC):
                            last = nc.tensor.matmul(dst, src[:, c, tok], wt[:, c, :], start=(c == 0), stop=(c == DC - 1))
                    last.then_inc(qkv_ready, 1)

                def turn_heads(t):
                    pe.wait_ge(padded_ready, t + 1)
                    if t >= 2:
                        pe.wait_ge(qkt_ready, t - 1)
                    for g in range(8):
                        last = nc.tensor.transpose(ps[:, 2 * (t % 2) + g // 4, g % 4 * P:(g % 4 + 1) * P],
                                                   padded[:, t % 2, 4 * g:4 * g + 4, :].rearrange("p h d -> p (h d)"),
                                                   const["ident"][:])
                    last.then_inc(padded_t, 1)

                for t in range(TILES):
                    project(t)
                    if t == 2:
                        pe.wait_ge(qin_ready, BATCH)
                    if t >= 2:
                        turn_heads(t - 2)
                turn_heads(TILES - 2)
                turn_heads(TILES - 1)
                pe.wait_ge(qkt_ready, TILES)

                def score(j):
                    t, g, nk = j // GROUPS, j % GROUPS, keys(j)
                    if j >= 2:
                        pe.wait_ge(scores_taken, j - 1)
                    for half_group in range(2):
                        keep = slice(2 * half_group, 2 * half_group + 2)
                        last = nc.tensor.matmul(
                            ps[:, 4 + 2 * (j % 2) + half_group, :].rearrange("p (h n) -> p h n", h=2)[:, :, 0:nk],
                            q_t[:, g, t * P:(t + 1) * P],
                            k_own[:, g, keep, t // QT * SEQ:t // QT * SEQ + nk], start=True, stop=True)
                    last.then_inc(scores_ready, 1)

                def turn_probs(j):
                    n = keys(j) // P
                    pe.wait_ge(probs_ready, j + 1)
                    if j >= 1:
                        pe.wait_ge(pt_ready, j)
                    for i in range(4):
                        for c in range(n):
                            s = i * n + c
                            last = nc.tensor.transpose(ps[:, s // 4, s % 4 * P:(s % 4 + 1) * P],
                                                       sm[:, j % 3, i, c * P:(c + 1) * P], const["ident"][:])
                    last.then_inc(probs_t, 1)

                def weigh(j):
                    t, g, n = j // GROUPS, j % GROUPS, keys(j) // P
                    pe.wait_ge(pt_ready, j + 1)
                    if g == 0 and t >= 2:
                        pe.wait_ge(att_ready, t - 1)
                    for i in range(4):
                        h = 4 * g + i
                        for c in range(n):
                            last = nc.tensor.matmul(ps[:, 2 + t % 2, h * HD0:(h + 1) * HD0], p_t[:, j % 2, i * n + c, :],
                                                    v[:, t // QT * QT + c, h * HD0:(h + 1) * HD0],
                                                    start=(c == 0), stop=(c == n - 1))
                    last.then_inc(pv_done, 1)

                pe.wait_ge(qkv_taken, TILES)
                score(0)
                for j in range(JOBS):
                    if j + 1 < JOBS:
                        score(j + 1)
                    turn_probs(j)
                    if j >= 1:
                        weigh(j - 1)
                weigh(JOBS - 1)
                for b in range(BATCH):
                    pe.wait_ge(att_ready, TILES)
                    for c in range(DC):
                        for q in range(QT):
                            last = nc.tensor.transpose(ps[:, b, c * SEQ + q * P:c * SEQ + (q + 1) * P],
                                                       att[:, b * QT + q, c * P:(c + 1) * P], const["ident"][:])
                    last.then_inc(att_tr, 1)
                for t in range(TILES):
                    pe.wait_ge(attt_ready, t // QT + 1)
                    if t >= 4:
                        pe.wait_ge(out_taken, t - 3)
                    for c in range(DC):
                        last = nc.tensor.matmul(ps[:, 4 + t % 4, 0:DM], att_t[:, c, t * P:(t + 1) * P], w_o[:, c, :],
                                                start=(c == 0), stop=(c == DC - 1))
                    last.then_inc(out_ready, 1)


CTX_FULL = CTX // P
CTX_REST = CTX - CTX_FULL * P
CTX_TILES = CTX_FULL + 1


def memory_attention(nc, x, const, a):
    with Stage(nc, "memory") as st:
        sb, sem = st.sb, st.sem
        ps = st.banks()
        ctx_t = sb("ctx_t", [P, BATCH, DC, CTX])
        ctx = sb("ctx", [P, BATCH, CTX_TILES, DM])
        flags = sb("flags", [BATCH, CTX], U8)
        barred = sb("barred", [BATCH, CTX], BF16)
        pick_raw = sb("pick_raw", [BATCH, BATCH, P])
        pick = sb("pick", [BATCH, BATCH, P], BF16)
        stats = sb("stats", [P, TILES, 6])
        mean_var = sb("mean_var", [P, TILES, 2])
        rs = sb("rs", [P, 6, TILES])
        half = sb("half", [P, TILES])
        xn = sb("xn", [P, TILES, DM])
        xn_t = sb("xn_t", [P, DC, TOK])
        mx = sb("mx", [P, TILES])
        shift = sb("shift", [P, TILES])
        sums = sb("sums", [P, TILES])
        seen = sb("seen", [P, TILES])
        gain = sb("gain", [P, TILES])
        probs = sb("probs", [P, 2, CTX])
        p_t = sb("p_t", [P, 2, 4, P])

        loaded = [sem(f"ctx_loaded{b}") for b in range(BATCH)]
        mask_loaded, barred_ready = sem("mask_loaded"), sem("barred_ready")
        dve_step, rs_ready, rs_done = sem("dve_step"), sem("rs_ready"), sem("rs_done")
        xn_ready, xt_ready, xnt_ready = sem("xn_ready"), sem("xt_ready"), sem("xnt_ready")
        scores_ready, shift_ready, probs_ready = sem("scores_ready"), sem("shift_ready"), sem("probs_ready")
        turned, pt_ready, pv_done, added = sem("turned"), sem("pt_ready"), sem("pv_done"), sem("added")
        SCALE = float(DM) ** -0.5
        CHUNKS = [(s, min(512, CTX - s)) for s in range(0, CTX, 512)]

        def scores(t):
            return ps[:, 0:4, :].rearrange("p a n -> p (a n)")[:, 0:CTX]

        with nc.Block() as block:
            @block.sync
            def _(sp):
                sp.dma_start(flags[:], a["mask_BxS2_bk0"]).then_inc(mask_loaded, 16)
                sp.dma_start(pick_raw[:], a["c_pick"]).then_inc(mask_loaded, 16)
                for b in range(BATCH):
                    sp.dma_start(ctx_t[:, b], a["ctx_t"][b].rearrange("(c p) n -> p c n", p=P)).then_inc(loaded[b], 16)
                    sp.dma_start(ctx[:, b, 0:CTX_FULL, :], a["ctx_2048"][b, 0:CTX_FULL * P, :].rearrange("(t p) d -> p t d", p=P))\
                        .then_inc(loaded[b], 16)
                    sp.dma_start(ctx[0:CTX_REST, b, CTX_FULL, :], a["ctx_2048"][b, CTX_FULL * P:CTX, :]).then_inc(loaded[b], 16)

            @block.gpsimd
            def _(gp):
                nc.gpsimd.memset(half[:], -0.5).then_inc(rs_done, 1)
                gp.wait_ge(rs_done, 1)
                gp.wait_ge(rs_ready, 1)
                nc.gpsimd.tensor_tensor(rs[:, 1, :], rs[:, 0, :], half[:], ALU.pow).then_inc(rs_done, 1)

            @block.vector
            def _(ve):
                link = chain(ve, dve_step)
                row_stats(nc, link, x, stats, mean_var)
                nc.vector.tensor_scalar(rs[:, 0, :], mean_var[:, :, 1], 1e-5, None, ALU.add).then_inc(rs_ready, 1)
                ve.wait_ge(rs_done, 2)
                for t in range(TILES):
                    nc.vector.tensor_scalar(xn[:, t, :], x[:, t, :], mean_var[:, t, 0:1], rs[:, 1, t:t + 1],
                                            ALU.subtract, ALU.mult).then_inc(xn_ready, 1)
                ve.wait_ge(mask_loaded, 32)
                nc.vector.tensor_copy(pick[:], pick_raw[:])
                nc.vector.tensor_scalar(barred[:], flags[:], -MASKED, MASKED, ALU.mult, ALU.add).then_inc(barred_ready, 1)

                def add_read(t):
                    ve.wait_ge(probs_ready, t + 1)
                    nc.vector.tensor_scalar(seen[:, t:t + 1], mx[:, t:t + 1], MASKED / 2, None, ALU.is_gt)
                    link(nc.vector.reciprocal(gain[:, t:t + 1], sums[:, t:t + 1]))
                    link(nc.vector.tensor_tensor(gain[:, t:t + 1], gain[:, t:t + 1], seen[:, t:t + 1], ALU.mult))
                    ve.wait_ge(pv_done, 4 * (t + 1))
                    nc.vector.scalar_tensor_tensor(x[:, t, :], ps[:, 6 + t % 2, 0:DM], gain[:, t:t + 1], x[:, t, :],
                                                   ALU.mult, ALU.add).then_inc(added, 1)

                for t in range(TILES):
                    ve.wait_ge(scores_ready, t + 1)
                    link(nc.vector.tensor_reduce(mx[:, t:t + 1], scores(t), AX_X, ALU.max))
                    nc.vector.tensor_scalar(shift[:, t:t + 1], mx[:, t:t + 1], -SCALE, None, ALU.mult).then_inc(shift_ready, 1)
                    if t >= 1:
                        add_read(t - 1)
                add_read(TILES - 1)

            @block.scalar
            def _(ac):
                for b in range(BATCH):
                    ac.wait_ge(xt_ready, b + 1)
                    nc.scalar.copy(xn_t[:, :, b * SEQ:(b + 1) * SEQ],
                                   ps[:, 4 + b, :].rearrange("p (c n) -> p c n", c=DC)).then_inc(xnt_ready, 1)
                for t in range(TILES):
                    ac.wait_ge(shift_ready, t + 1)
                    if t >= 2:
                        ac.wait_ge(turned, 4 * (t - 1))
                    nc.scalar.activation(probs[:, t % 2, :], scores(t), ACT.Exp, bias=shift[:, t:t + 1], scale=SCALE,
                                         accum_out=sums[:, t:t + 1]).then_inc(probs_ready, 1)
                    for g in range(4):
                        n = 4 * t + g
                        ac.wait_ge(turned, n + 1)
                        if n >= 2:
                            ac.wait_ge(pv_done, n - 1)
                        if g < 3:
                            nc.scalar.copy(p_t[:, n % 2], ps[:, 4 + n % 2, :].rearrange("p (c n) -> p c n", c=4)).then_inc(pt_ready, 1)
                        else:
                            nc.scalar.copy(p_t[0:CTX_REST, n % 2, 0, :], ps[0:CTX_REST, 4 + n % 2, 0:P]).then_inc(pt_ready, 1)

            @block.tensor
            def _(pe):
                for b in range(BATCH):
                    pe.wait_ge(xn_ready, 2 * b + 2)
                    for c in range(DC):
                        for q in range(QT):
                            last = nc.tensor.transpose(ps[:, 4 + b, c * SEQ + q * P:c * SEQ + (q + 1) * P],
                                                       xn[:, b * QT + q, c * P:(c + 1) * P], const["ident"][:])
                    last.then_inc(xt_ready, 1)
                pe.wait_ge(barred_ready, 1)
                pe.wait_ge(xnt_ready, BATCH)

                def score(t):
                    b = t // QT
                    if t % QT == 0:
                        pe.wait_ge(loaded[b], 48)
                    if t >= 1:
                        pe.wait_ge(probs_ready, t)
                    for i, (s, n) in enumerate(CHUNKS):
                        for c in range(DC):
                            nc.tensor.matmul(ps[:, i, 0:n], xn_t[:, c, t * P:(t + 1) * P], ctx_t[:, b, c, s:s + n],
                                             start=(c == 0), stop=False)
                        last = nc.tensor.matmul(ps[:, i, 0:n], pick[:, b, :], barred[:, s:s + n], start=False, stop=True)
                    last.then_inc(scores_ready, 1)

                def turn(t, g):
                    n = 4 * t + g
                    if n >= 2:
                        pe.wait_ge(pt_ready, n - 1)
                    for i in range(4 if g < 3 else 1):
                        k = 4 * g + i
                        w = min(P, CTX - k * P)
                        last = nc.tensor.transpose(ps[0:w, 4 + n % 2, i * P:(i + 1) * P], probs[:, t % 2, k * P:k * P + w],
                                                   const["ident"][:])
                    last.then_inc(turned, 1)

                def read(t, g):
                    n = 4 * t + g
                    pe.wait_ge(pt_ready, n + 1)
                    if g == 0 and t >= 2:
                        pe.wait_ge(added, t - 1)
                    for i in range(4 if g < 3 else 1):
                        k = 4 * g + i
                        w = min(P, CTX - k * P)
                        last = nc.tensor.matmul(ps[:, 6 + t % 2, 0:DM], p_t[0:w, n % 2, i, :], ctx[0:w, t // QT, k, :],
                                                start=(k == 0), stop=(k == CTX_TILES - 1))
                    last.then_inc(pv_done, 1)

                score(0)
                for t in range(TILES):
                    pe.wait_ge(probs_ready, t + 1)
                    turn(t, 0)
                    turn(t, 1)
                    if t + 1 < TILES:
                        score(t + 1)
                    read(t, 0)
                    turn(t, 2)
                    read(t, 1)
                    turn(t, 3)
                    read(t, 2)
                    read(t, 3)


def ternary_ffn(nc, x, const, a):
    with Stage(nc, "ffn") as st:
        sb, sem = st.sb, st.sem
        ps = st.banks()
        CLIP = 128.0 - 1e-6
        raw = [sb("raw_fc", [P, DC, FF]), sb("raw_proj", [P, FC, DM])]
        tern = [sb("tern_fc", [P, DC, FF], F16), sb("tern_proj", [P, FC, DM], F16)]
        below = sb("below", [P, DC * FF], F16)
        ones = sb("ones", [P, P])
        size = sb("size", [P, 2])
        mean_size = sb("mean_size", [P, 2])
        per_size = sb("per_size", [P, 2])
        stats = sb("stats", [P, TILES, 6])
        mean_var = sb("mean_var", [P, TILES, 2])
        rs = sb("rs", [P, 6, TILES])
        half = sb("half", [P, TILES])
        rows = sb("rows", [P, TILES, DM])
        top = sb("top", [P, 3, TILES])
        rows_hi = sb("rows_hi", [P, DC, TOK], F16)
        rows_lo = sb("rows_lo", [P, DC, TOK], F16)
        h = sb("h", [P, 2, FF])
        hstats = sb("hstats", [P, TILES, 2, 6])
        hmv = sb("hmv", [P, TILES, 2])
        hvar = sb("hvar", [P, 2, TILES])
        htop = sb("htop", [P, 3, TILES])
        h_hi = sb("h_hi", [P, 2, FC, P], F16)
        h_lo = sb("h_lo", [P, 2, FC, P], F16)

        loaded = sem("weights_loaded")
        dve_step, rs_ready, rs_done = sem("dve_step"), sem("rs_ready"), sem("rs_done")
        ones_ready, sizes_ready, size_spread, tern_ready = sem("ones_ready"), sem("sizes_ready"), sem("size_spread"), sem("tern_ready")
        rows_ready, rows_t, hi_ready, lo_ready = sem("rows_ready"), sem("rows_t"), sem("hi_ready"), sem("lo_ready")
        up_ready, h_ready, hvar_ready, hvar_done = sem("up_ready"), sem("h_ready"), sem("hvar_ready"), sem("hvar_done")
        h_clipped, h_t, hhi_ready, hlo_ready = sem("h_clipped"), sem("h_t"), sem("hhi_ready"), sem("hlo_ready")
        down_ready, added = sem("down_ready"), sem("added")

        with nc.Block() as block:
            @block.sync
            def _(sp):
                sp.dma_start(raw[0][:], a["L0_ffn_w_fc"].rearrange("(c p) n -> p c n", p=P)).then_inc(loaded, 16)
                sp.dma_start(raw[1][:], a["L0_ffn_w_proj"].rearrange("(c p) n -> p c n", p=P)).then_inc(loaded, 16)

            @block.gpsimd
            def _(gp):
                nc.gpsimd.memset(half[:], -0.5)
                nc.gpsimd.memset(ones[:], 1.0).then_inc(ones_ready, 1)
                gp.wait_ge(ones_ready, 1)
                for i in range(2):
                    gp.wait_ge(rs_ready, i + 1)
                    nc.gpsimd.tensor_tensor(rs[:, 2 * i + 1, :], rs[:, 2 * i, :], half[:], ALU.pow).then_inc(rs_done, 1)
                for t in range(TILES):
                    gp.wait_ge(hvar_ready, t + 1)
                    nc.gpsimd.tensor_tensor(hvar[:, 1, t:t + 1], hvar[:, 0, t:t + 1], half[:, 0:1], ALU.pow).then_inc(hvar_done, 1)

            @block.vector
            def _(ve):
                link = chain(ve, dve_step)
                row_stats(nc, link, x, stats, mean_var)
                nc.vector.tensor_scalar(rs[:, 0, :], mean_var[:, :, 1], 1e-5, None, ALU.add).then_inc(rs_ready, 1)
                ve.wait_ge(rs_done, 1)
                link(nc.vector.tensor_tensor(rs[:, 4, :], rs[:, 1, :], rs[:, 1, :], ALU.mult))
                link(nc.vector.tensor_tensor(rs[:, 5, :], rs[:, 4, :], mean_var[:, :, 1], ALU.mult))
                nc.vector.tensor_scalar(rs[:, 2, :], rs[:, 5, :], 1e-6, None, ALU.add).then_inc(rs_ready, 1)
                ve.wait_ge(loaded, 32)
                nc.vector.tensor_reduce(size[:, 0:1], raw[0][:].rearrange("p c n -> p (c n)"), AX_X, ALU.add, apply_absolute_value=True)
                nc.vector.tensor_reduce(size[:, 1:2], raw[1][:].rearrange("p c n -> p (c n)"), AX_X, ALU.add,
                                        apply_absolute_value=True).then_inc(sizes_ready, 1)
                ve.wait_ge(rs_done, 2)
                link(nc.vector.tensor_tensor(rs[:, 4, :], rs[:, 1, :], rs[:, 3, :], ALU.mult))

                def clip(dst, src, marks, t):
                    link(nc.vector.tensor_reduce(marks[:, 0, t:t + 1], src, AX_X, ALU.max, apply_absolute_value=True))
                    link(nc.vector.reciprocal(marks[:, 1, t:t + 1], marks[:, 0, t:t + 1]))
                    nc.vector.tensor_scalar(marks[:, 2, t:t + 1], marks[:, 0, t:t + 1], 1.0 / 128.0, None, ALU.mult)
                    link(nc.vector.tensor_scalar(marks[:, 1, t:t + 1], marks[:, 1, t:t + 1], 128.0, None, ALU.mult))
                    link(nc.vector.tensor_scalar(dst, src, marks[:, 1, t:t + 1], CLIP, ALU.mult, ALU.min))
                    return nc.vector.tensor_scalar(dst, dst, -CLIP, marks[:, 2, t:t + 1], ALU.max, ALU.mult)

                def rest(b):
                    ve.wait_ge(hi_ready, b + 1)
                    tok = slice(b * SEQ, (b + 1) * SEQ)
                    nc.vector.tensor_tensor(rows_lo[:, :, tok], ps[:, b % 2, :].rearrange("p (c n) -> p c n", c=DC),
                                            rows_hi[:, :, tok], ALU.subtract).then_inc(lo_ready, 1)

                for t in range(TILES):
                    link(nc.vector.tensor_scalar(rows[:, t, :], x[:, t, :], mean_var[:, t, 0:1], rs[:, 4, t:t + 1],
                                                 ALU.subtract, ALU.mult))
                    clip(rows[:, t, :], rows[:, t, :], top, t).then_inc(rows_ready, 1)
                    if t % 2 == 1 and t > 2:
                        rest(t // 2 - 1)
                rest(BATCH - 1)
                ve.wait_ge(size_spread, 1)
                link(nc.vector.tensor_scalar(mean_size[:], ps[:, 7, 0:2], 1.0 / (FF * DM), None, ALU.mult))
                link(nc.vector.tensor_scalar(per_size[:], mean_size[:], 1e-6, None, ALU.add))
                link(nc.vector.reciprocal(per_size[:], per_size[:]))
                for i in range(2):
                    flat = [r[:].rearrange("p c n -> p (c n)") for r in (raw[i], tern[i])]
                    nc.vector.tensor_scalar(below[:], flat[0], per_size[:, i:i + 1], -0.5, ALU.mult, ALU.is_lt)
                    link(nc.vector.tensor_scalar(flat[1], flat[0], per_size[:, i:i + 1], 0.5, ALU.mult, ALU.is_gt))
                    ins = nc.vector.tensor_tensor(flat[1], flat[1], below[:], ALU.subtract)
                    ins.then_inc(tern_ready, 1)
                    ve.wait_ge(tern_ready, i + 1)

                def quantise(t):
                    hb = h[:, t % 2, :]
                    ve.wait_ge(h_ready, t + 1)
                    for k in range(2):
                        last = nc.vector.bn_stats(hstats[:, t, k, :], h[:, t % 2, k * 512:(k + 1) * 512])
                    link(last)
                    link(nc.vector.bn_aggr(hmv[:, t, :], hstats[:, t, :, :].rearrange("p k n -> p (k n)")))
                    nc.vector.tensor_scalar(hvar[:, 0, t:t + 1], hmv[:, t, 1:2], 1e-6, None, ALU.add).then_inc(hvar_ready, 1)
                    ve.wait_ge(hvar_done, t + 1)
                    link(nc.vector.tensor_scalar(hb, hb, hmv[:, t, 0:1], hvar[:, 1, t:t + 1], ALU.subtract, ALU.mult))
                    clip(hb, hb, htop, t).then_inc(h_clipped, 1)

                def h_rest(t):
                    ve.wait_ge(hhi_ready, t + 1)
                    nc.vector.tensor_tensor(h_lo[:, t % 2], ps[:, 4:6, :].rearrange("p a (c n) -> p (a c) n", n=P),
                                            h_hi[:, t % 2], ALU.subtract).then_inc(hlo_ready, 1)

                def add(t):
                    ve.wait_ge(down_ready, t + 1)
                    nc.vector.scalar_tensor_tensor(x[:, t, :], ps[:, 6 + t % 2, 0:DM], mean_size[:, 1:2], x[:, t, :],
                                                   ALU.mult, ALU.add).then_inc(added, 1)

                for t in range(TILES):
                    quantise(t)
                    if t >= 1:
                        h_rest(t - 1)
                    if t >= 2:
                        add(t - 2)
                h_rest(TILES - 1)
                add(TILES - 2)
                add(TILES - 1)

            @block.scalar
            def _(ac):
                for b in range(BATCH):
                    ac.wait_ge(rows_t, b + 1)
                    nc.scalar.copy(rows_hi[:, :, b * SEQ:(b + 1) * SEQ],
                                   ps[:, b % 2, :].rearrange("p (c n) -> p c n", c=DC)).then_inc(hi_ready, 1)

                def gelu(t):
                    ac.wait_ge(up_ready, t + 1)
                    if t >= 2:
                        ac.wait_ge(h_t, t - 1)
                    nc.scalar.activation(h[:, t % 2, :], ps[:, 2:4, :].rearrange("p a n -> p (a n)"), ACT.Gelu,
                                         scale=mean_size[:, 0:1]).then_inc(h_ready, 1)

                def high(t):
                    ac.wait_ge(h_t, t + 1)
                    if t >= 2:
                        ac.wait_ge(down_ready, t - 1)
                    nc.scalar.copy(h_hi[:, t % 2], ps[:, 4:6, :].rearrange("p a (c n) -> p (a c) n", n=P)).then_inc(hhi_ready, 1)

                gelu(0)
                for t in range(TILES):
                    if t + 1 < TILES:
                        gelu(t + 1)
                    high(t)

            @block.tensor
            def _(pe):
                pe.wait_ge(ones_ready, 1)
                pe.wait_ge(sizes_ready, 1)
                nc.tensor.matmul(ps[:, 7, 0:2], ones[:], size[:], start=True, stop=True).then_inc(size_spread, 1)
                for b in range(BATCH):
                    pe.wait_ge(rows_ready, 2 * b + 2)
                    if b >= 2:
                        pe.wait_ge(lo_ready, b - 1)
                    for c in range(DC):
                        for q in range(QT):
                            last = nc.tensor.transpose(ps[:, b % 2, c * SEQ + q * P:c * SEQ + (q + 1) * P],
                                                       rows[:, b * QT + q, c * P:(c + 1) * P], const["ident"][:])
                    last.then_inc(rows_t, 1)
                pe.wait_ge(lo_ready, BATCH)
                pe.wait_ge(tern_ready, 1)

                def up(t):
                    if t >= 1:
                        pe.wait_ge(h_ready, t)
                    tok = slice(t * P, (t + 1) * P)
                    for n in range(2):
                        for k, (part, c) in enumerate((part, c) for part in (rows_hi, rows_lo) for c in range(DC)):
                            last = nc.tensor.matmul(ps[:, 2 + n, :], part[:, c, tok], tern[0][:, c, n * 512:(n + 1) * 512],
                                                    start=(k == 0), stop=(k == 3))
                    last.then_inc(up_ready, 1)

                def turn(t):
                    pe.wait_ge(h_clipped, t + 1)
                    if t >= 1:
                        pe.wait_ge(hlo_ready, t)
                    for c in range(FC):
                        last = nc.tensor.transpose(ps[:, 4 + c // 4, c % 4 * P:(c % 4 + 1) * P],
                                                   h[:, t % 2, c * P:(c + 1) * P], const["ident"][:])
                    last.then_inc(h_t, 1)

                def down(t):
                    pe.wait_ge(hhi_ready, t + 1)
                    pe.wait_ge(hlo_ready, t + 1)
                    if t >= 2:
                        pe.wait_ge(added, t - 1)
                    for k, (part, c) in enumerate((part, c) for part in (h_hi, h_lo) for c in range(FC)):
                        last = nc.tensor.matmul(ps[:, 6 + t % 2, 0:DM], part[:, t % 2, c, :], tern[1][:, c, :],
                                                start=(k == 0), stop=(k == 2 * FC - 1))
                    last.then_inc(down_ready, 1)

                up(0)
                pe.wait_ge(tern_ready, 2)
                for t in range(TILES):
                    if t + 1 < TILES:
                        up(t + 1)
                    if t >= 1:
                        down(t - 1)
                    turn(t)
                down(TILES - 1)


def gated_scan(nc, x, const, a, w):
    with Stage(nc, "scan") as st:
        sb, sem = st.sb, st.sem
        ps = st.banks()
        CHUNK, TAPS = 32, 4
        NC = SEQ // CHUNK
        RUNS = BATCH * NC
        w_in = sb("w_in", [P, DC, 3 * DM])
        w_swap = sb("w_swap", [P, DC, DM])
        w_out = sb("w_out", [P, DC, DM])
        mix = sb("mix", [P, DC, HEADS])
        same = sb("same", [P, HEADS])
        mixer = sb("mixer", [P, DC, DM])
        norm_scale, conv_b, dt_bias = sb("norm_scale", [P, DC]), sb("conv_b", [P, DC]), sb("dt_bias", [P, DC])
        conv_w = sb("conv_w", [P, DC, TAPS])
        cos, sin = sb("cos", [P, SEQ]), sb("sin", [P, SEQ])
        stats = sb("stats", [P, TILES, 6])
        mean_var = sb("mean_var", [P, TILES, 2])
        rs = sb("rs", [P, 6, TILES])
        half = sb("half", [P, TILES])
        xn = sb("xn", [P, TILES, DM])
        xr = sb("xr", [P, TILES, DM])
        conv_in = sb("conv_in", [P, DC, BATCH, TAPS - 1 + SEQ])
        acc = sb("acc", [P, DC, BATCH, SEQ])
        xs = sb("xs", [P, DC, TOK])
        keep_chunk = sb("keep_chunk", [P, TOK])
        keep_row = sb("keep_row", [P, RUNS])
        dt = sb("dt", [P, DC, TOK])
        v_in = sb("v_in", [P, DC, TOK])
        v_sin = sb("v_sin", [P, TOK])
        gate = sb("gate", [P, DC, TOK])
        decay = sb("decay", [P, DC, TOK])
        since = sb("since", [P, DC, TOK])
        grow = sb("grow", [P, TOK])
        local = sb("local", [P, DC, TOK])
        shrink = sb("shrink", [P, TOK])
        runs = sb("runs", [P, 8, RUNS])
        final = sb("final", [P, DC, TOK])
        y = sb("y", [P, DC, TOK])

        loaded = sem("weights_loaded")
        dve_step, rs_ready, rs_done, masks_ready = sem("dve_step"), sem("rs_ready"), sem("rs_done"), sem("masks_ready")
        xr_ready, xt_ready, xt_taken, conv_done, xs_ready = sem("xr_ready"), sem("xt_ready"), sem("xt_taken"), sem("conv_done"), sem("xs_ready")
        swap_ready, proj_ready, dt_in, dt_ln, act_step = sem("swap_ready"), sem("proj_ready"), sem("dt_in"), sem("dt_ln"), sem("act_step")
        proj_taken, gate_ready = sem("proj_taken"), sem("gate_ready")
        since_ready, grow_ready, shrink_ready, runs_ready, runs_exp = sem("since_ready"), sem("grow_ready"), sem("shrink_ready"), sem("runs_ready"), sem("runs_exp")
        decay_used, decay_exp, final_ready = sem("decay_used"), sem("decay_exp"), sem("final_ready")
        normed_added = sem("normed_added")
        mixed, y_ready, out_ready, out_taken = sem("mixed"), sem("y_ready"), sem("out_ready"), sem("out_taken")

        def pair(j):
            return ps[:, 2 * (j % 4):2 * (j % 4) + 2, :].rearrange("p a n -> p (a n)")

        def chunks(ap):
            return ap.rearrange("p (k n) -> p k n", n=CHUNK)

        with nc.Block() as block:
            @block.sync
            def _(sp):
                for dst, src in (
                    (norm_scale[:], w["norm_scale"]), (conv_w[:], w["conv_w"]), (conv_b[:], w["conv_b"]), (dt_bias[:], w["dt_bias"]),
                    (w_in[:], w["in_proj_w"].rearrange("(c p) n -> p c n", p=P)),
                    (cos[:], a["c_scan_cos"]), (sin[:], a["c_scan_sin"]), (same[:], a["c_scan_same"]),
                    (mix[:], a["mix_rows"]),
                    (w_out[:], w["out_proj_w"].rearrange("(c p) n -> p c n", p=P)),
                ):
                    sp.dma_start(dst, src).then_inc(loaded, 16)

            @block.gpsimd
            def _(gp):
                nc.gpsimd.memset(half[:], -0.5)
                nc.gpsimd.memset(keep_chunk[:], 1.0)
                nc.gpsimd.memset(keep_row[:], 1.0)
                nc.gpsimd.memset(conv_in[:, :, :, 0:TAPS - 1], 0.0).then_inc(masks_ready, 1)
                gp.wait_ge(masks_ready, 1)
                nc.gpsimd.memset(chunks(keep_chunk[:])[:, :, 0:1], 0.0)
                nc.gpsimd.memset(keep_row[:].rearrange("p (b k) -> p b k", b=BATCH)[:, :, 0:1], 0.0).then_inc(masks_ready, 1)
                for i in range(2):
                    gp.wait_ge(rs_ready, i + 1)
                    nc.gpsimd.tensor_tensor(rs[:, 2 * i + 1, :], rs[:, 2 * i, :], half[:], ALU.pow).then_inc(rs_done, 1)
                gp.wait_ge(xr_ready, TILES)
                nc.gpsimd.tensor_tensor(x[:], x[:], xn[:], ALU.add).then_inc(normed_added, 1)
                gp.wait_ge(loaded, 160)
                for c in range(DC):
                    v = w_in[:, c, DM:2 * DM].rearrange("p (h s d) -> p h s d", s=2, d=HEADS // 2)
                    s = w_swap[:, c, :].rearrange("p (h s d) -> p h s d", s=2, d=HEADS // 2)
                    nc.gpsimd.tensor_copy(s[:, :, 0, :], v[:, :, 1, :])
                    last = nc.gpsimd.tensor_copy(s[:, :, 1, :], v[:, :, 0, :])
                last.then_inc(swap_ready, 1)
                for c in range(DC):
                    last = nc.gpsimd.tensor_tensor(mixer[:, c, :].rearrange("p (m d) -> p m d", m=HEADS),
                                                   bcast(mix[:, c, :], 2, HEADS), bcast(same[:], 1, HEADS), ALU.mult)
                last.then_inc(swap_ready, 1)

            @block.vector
            def _(ve):
                link = chain(ve, dve_step)
                row_stats(nc, link, x, stats, mean_var)
                nc.vector.tensor_scalar(rs[:, 0, :], mean_var[:, :, 1], 1e-5, None, ALU.add).then_inc(rs_ready, 1)
                ve.wait_ge(rs_done, 1)
                link(nc.vector.tensor_tensor(rs[:, 4, :], rs[:, 1, :], rs[:, 1, :], ALU.mult))
                link(nc.vector.tensor_tensor(rs[:, 5, :], rs[:, 4, :], mean_var[:, :, 1], ALU.mult))
                nc.vector.tensor_scalar(rs[:, 2, :], rs[:, 5, :], 1e-6, None, ALU.add).then_inc(rs_ready, 1)
                for t in range(TILES):
                    last = nc.vector.tensor_scalar(xn[:, t, :], x[:, t, :], mean_var[:, t, 0:1], rs[:, 1, t:t + 1],
                                                   ALU.subtract, ALU.mult)
                link(last)
                ve.wait_ge(rs_done, 2)
                for t in range(TILES):
                    nc.vector.tensor_scalar(xr[:, t, :], xn[:, t, :], rs[:, 3, t:t + 1], None, ALU.mult).then_inc(xr_ready, 1)
                ve.wait_ge(loaded, 160)
                ve.wait_ge(masks_ready, 2)
                for b in range(BATCH):
                    ve.wait_ge(xt_ready, b + 1)
                    for c in range(DC):
                        last = nc.vector.tensor_scalar(conv_in[:, c, b, TAPS - 1:], ps[:, b, c * SEQ:(c + 1) * SEQ],
                                                       norm_scale[:, c:c + 1], 60000.0, ALU.mult, ALU.min)
                    last.then_inc(xt_taken, 1)
                ve.wait_ge(xt_taken, BATCH)
                link(nc.vector.tensor_scalar(conv_in[:], conv_in[:], -60000.0, None, ALU.max))
                for c in range(DC):
                    link(nc.vector.tensor_scalar(acc[:, c], conv_in[:, c, :, 0:SEQ], conv_w[:, c, 0:1], None, ALU.mult))
                    for k in range(1, TAPS):
                        ins = nc.vector.scalar_tensor_tensor(acc[:, c], conv_in[:, c, :, k:k + SEQ], conv_w[:, c, k:k + 1], acc[:, c],
                                                             ALU.mult, ALU.add)
                        if k < TAPS - 1:
                            link(ins)
                    ins.then_inc(conv_done, 1)
                rows = [P, BATCH, SEQ]
                for c in range(DC):
                    ve.wait_ge(proj_ready, 4 * c + 1)
                    ins = nc.vector.tensor_scalar(dt[:, c, :], pair(4 * c), dt_bias[:, c:c + 1], 20.0, ALU.add, ALU.min)
                    ins.then_inc(dt_in, 1)
                    by_row = lambda ap: ap.rearrange("p (b n) -> p b n", b=BATCH)
                    ve.wait_ge(proj_ready, 4 * c + 2)
                    nc.vector.tensor_tensor(by_row(v_in[:, c, :]), by_row(pair(4 * c + 1)), bcast(cos[:], 1, BATCH), ALU.mult)
                    ve.wait_ge(proj_ready, 4 * c + 3)
                    ins = nc.vector.tensor_tensor(by_row(v_sin[:]), by_row(pair(4 * c + 2)), bcast(sin[:], 1, BATCH), ALU.mult)
                    ins.then_inc(proj_taken, 1)
                    ve.wait_ge(proj_taken, c + 1)
                    link(nc.vector.tensor_tensor(v_in[:, c, :], v_in[:, c, :], v_sin[:], ALU.add))
                    ve.wait_ge(dt_ln, c + 1)
                    link(nc.vector.tensor_scalar(dt[:, c, :], dt[:, c, :], 0.001, 2.0, ALU.max, ALU.min))
                    link(nc.vector.tensor_tensor(v_in[:, c, :], v_in[:, c, :], dt[:, c, :], ALU.mult))
                    link(nc.vector.tensor_tensor_scan(decay[:, c, :], keep_chunk[:], dt[:, c, :], 0.0, ALU.mult, ALU.add))
                    link(nc.vector.tensor_scalar(decay[:, c, :], decay[:, c, :], 20.0, None, ALU.min))
                    nc.vector.tensor_tensor(chunks(since[:, c, :]), chunks(decay[:, c, :]),
                                            chunks(decay[:, c, :])[:, :, 0:1].to_broadcast([P, RUNS, CHUNK]),
                                            ALU.subtract).then_inc(since_ready, 1)
                    ve.wait_ge(grow_ready, c + 1)
                    link(nc.vector.tensor_tensor(v_in[:, c, :], v_in[:, c, :], grow[:], ALU.mult))
                    link(nc.vector.tensor_tensor_scan(local[:, c, :], keep_chunk[:], v_in[:, c, :], 0.0, ALU.mult, ALU.add))
                    ve.wait_ge(shrink_ready, c + 1)
                    ins = nc.vector.tensor_tensor(local[:, c, :], local[:, c, :], shrink[:], ALU.mult)
                    ins.then_inc(decay_used, 1)
                    ve.wait_ge(decay_used, c + 1)
                    total, seed = runs[:, 0, :], runs[:, 1, :]
                    first = lambda ap: ap.rearrange("p (b k) -> p b k", b=BATCH)
                    link(nc.vector.tensor_copy(runs[:, 2, :], chunks(decay[:, c, :])[:, :, CHUNK - 1]))
                    link(nc.vector.tensor_tensor_scan(total, keep_row[:], runs[:, 2, :], 0.0, ALU.mult, ALU.add))
                    link(nc.vector.tensor_scalar(total, total, 80.0, None, ALU.min))
                    link(nc.vector.tensor_tensor(first(runs[:, 3, :]), first(total), first(total)[:, :, 0:1].to_broadcast([P, BATCH, NC]),
                                                 ALU.subtract))
                    nc.vector.tensor_scalar(runs[:, 3, :], runs[:, 3, :], 20.0, None, ALU.min).then_inc(runs_ready, 1)
                    ve.wait_ge(runs_exp, c + 1)
                    link(nc.vector.tensor_tensor(seed, chunks(local[:, c, :])[:, :, CHUNK - 1], runs[:, 4, :], ALU.mult))
                    link(nc.vector.memset(runs[:, 6, :], 0.0))
                    link(nc.vector.tensor_copy(first(runs[:, 6, :])[:, :, 1:NC], first(seed)[:, :, 0:NC - 1]))
                    link(nc.vector.tensor_tensor_scan(runs[:, 7, :], keep_row[:], runs[:, 6, :], 0.0, ALU.mult, ALU.add))
                    link(nc.vector.tensor_tensor(runs[:, 7, :], runs[:, 7, :], runs[:, 5, :], ALU.mult))
                    ve.wait_ge(decay_exp, c + 1)
                    link(nc.vector.tensor_tensor(chunks(final[:, c, :]), chunks(since[:, c, :]), bcast(runs[:, 7, :], 2, CHUNK), ALU.mult))
                    nc.vector.tensor_tensor(final[:, c, :], final[:, c, :], local[:, c, :], ALU.add).then_inc(final_ready, 1)
                for c in range(DC):
                    ve.wait_ge(mixed, c + 1)
                    ve.wait_ge(gate_ready, c + 1)
                    nc.vector.tensor_tensor(y[:, c, :], pair(8 + c), gate[:, c, :], ALU.mult).then_inc(y_ready, 1)
                ve.wait_ge(normed_added, 1)
                for t in range(TILES):
                    ve.wait_ge(out_ready, t + 1)
                    nc.vector.tensor_tensor(x[:, t, :], x[:, t, :], ps[:, 4 + t % 4, 0:DM], ALU.add).then_inc(out_taken, 1)

            @block.scalar
            def _(ac):
                for c in range(DC):
                    ac.wait_ge(conv_done, c + 1)
                    nc.scalar.activation(xs[:, c, :], acc[:, c].rearrange("p b n -> p (b n)"), ACT.Silu,
                                         bias=conv_b[:, c:c + 1]).then_inc(xs_ready, 1)
                step = chain(ac, act_step)
                for c in range(DC):
                    ac.wait_ge(dt_in, c + 1)
                    step(nc.scalar.activation(dt[:, c, :], dt[:, c, :], ACT.Exp))
                    nc.scalar.activation(dt[:, c, :], dt[:, c, :], ACT.Ln, bias=1.0).then_inc(dt_ln, 1)
                    ac.wait_ge(since_ready, c + 1)
                    if c >= 1:
                        ac.wait_ge(decay_used, c)
                    nc.scalar.activation(grow[:], since[:, c, :], ACT.Exp).then_inc(grow_ready, 1)
                    ins = nc.scalar.activation(shrink[:], since[:, c, :], ACT.Exp, scale=-1.0)
                    ins.then_inc(shrink_ready, 1)
                    ac.wait_ge(shrink_ready, c + 1)
                    nc.scalar.activation(since[:, c, :], decay[:, c, :], ACT.Exp, scale=-1.0).then_inc(decay_exp, 1)
                    ac.wait_ge(runs_ready, c + 1)
                    nc.scalar.activation(runs[:, 4, :], runs[:, 3, :], ACT.Exp)
                    nc.scalar.activation(runs[:, 5, :], runs[:, 3, :], ACT.Exp, scale=-1.0).then_inc(runs_exp, 1)
                    ac.wait_ge(proj_ready, 4 * c + 4)
                    nc.scalar.activation(gate[:, c, :], pair(4 * c + 3), ACT.Sigmoid).then_inc(gate_ready, 1)

            @block.tensor
            def _(pe):
                for b in range(BATCH):
                    pe.wait_ge(xr_ready, 2 * b + 2)
                    for c in range(DC):
                        for q in range(QT):
                            last = nc.tensor.transpose(ps[:, b, c * SEQ + q * P:c * SEQ + (q + 1) * P],
                                                       xr[:, b * QT + q, c * P:(c + 1) * P], const["ident"][:])
                    last.then_inc(xt_ready, 1)
                pe.wait_ge(xs_ready, DC)
                pe.wait_ge(swap_ready, 1)
                for c in range(DC):
                    for k, (wt, col) in enumerate(((w_in, 0), (w_in, DM), (w_swap, 0), (w_in, 2 * DM))):
                        if c == 1:
                            if k == 0:
                                pe.wait_ge(dt_in, 1)
                            elif k < 3:
                                pe.wait_ge(proj_taken, 1)
                            else:
                                pe.wait_ge(gate_ready, 1)
                        for n in range(2):
                            for d in range(DC):
                                last = nc.tensor.matmul(ps[:, 2 * k + n, :], wt[:, d, col + c * P:col + (c + 1) * P],
                                                        xs[:, d, n * 512:(n + 1) * 512], start=(d == 0), stop=(d == DC - 1))
                        last.then_inc(proj_ready, 1)
                pe.wait_ge(final_ready, DC)
                pe.wait_ge(swap_ready, 2)
                pe.wait_ge(gate_ready, DC)
                for c in range(DC):
                    for n in range(2):
                        for d in range(DC):
                            last = nc.tensor.matmul(ps[:, 2 * c + n, :], mixer[:, d, c * P:(c + 1) * P],
                                                    final[:, d, n * 512:(n + 1) * 512], start=(d == 0), stop=(d == DC - 1))
                    last.then_inc(mixed, 1)
                pe.wait_ge(y_ready, DC)
                for t in range(TILES):
                    if t >= 4:
                        pe.wait_ge(out_taken, t - 3)
                    for d in range(DC):
                        last = nc.tensor.matmul(ps[:, 4 + t % 4, 0:DM], y[:, d, t * P:(t + 1) * P], w_out[:, d, :],
                                                start=(d == 0), stop=(d == DC - 1))
                    last.then_inc(out_ready, 1)


QH, KVH, HD = 16, 4, 128
REP = QH // KVH
KEYS = SEQ + CTX
KT = QT + CTX_TILES
QCOLS = REP * SEQ
CHUNKS = [(s, min(512, KEYS - s)) for s in range(0, KEYS, 512)]
NCH = len(CHUNKS)
ROUND = 1.5 * 2.0 ** 23
TWO_PI = (6.28125, 0.0019353071693331003, 1.0253131677018246e-11)


def rows_of(tile):
    return P if tile < KT - 1 else CTX_REST


def count_turns(link, engine, angle, turns, where_f, where, freq):
    wide = list(angle.shape)
    link(engine.tensor_copy(where_f, where))
    link(engine.tensor_tensor(angle, bcast(where_f, 2, wide[2]), bcast(freq, 1, wide[1]), ALU.mult))
    link(engine.tensor_scalar(turns, angle, 1.0 / (2.0 * math.pi), ROUND, ALU.mult, ALU.add))
    return engine.tensor_scalar(turns, turns, ROUND, None, ALU.subtract)


def less_turns(link, engine, angle, turns):
    for part in TWO_PI:
        link(engine.scalar_tensor_tensor(angle, turns, -part, angle, ALU.mult, ALU.add))
    return engine.tensor_scalar(angle, angle, 3.1415925, -3.1415925, ALU.min, ALU.max)


def waves(step, engine, sin, cos, angle, turns, half_pi):
    engine.activation(sin, angle, ACT.Sin)
    step(engine.activation(turns, angle, ACT.Abs))
    return engine.activation(cos, turns, ACT.Sin, scale=-1.0, bias=half_pi)


def cross_attention(nc, x, const, a, w):
    with Stage(nc, "cross") as keep:
        sb = keep.sb
        names = (("q", DC, QH * HD), ("k", DC, KVH * HD), ("v", DC, KVH * HD), ("o", QH, DM))
        W = {n: [sb(f"w_{n}_{part}", [P, c, m], BF16) for part in ("hi", "lo")] for n, c, m in names}
        k_t = [sb(f"k_t_{part}", [P, KVH, KEYS], BF16) for part in ("hi", "lo")]
        q_t = [sb(f"q_t_{part}", [P, QH, SEQ], BF16) for part in ("hi", "lo")]
        v = [sb(f"v_{part}", [P, KT, KVH * HD], BF16) for part in ("hi", "lo")]
        k_gain = sb("k_gain", [P, 2, HD])
        q_gain = sb("q_gain", [P, 2, HD])
        freq = sb("freq", [P, HD // 2])
        ones = sb("ones", [P, P])
        ones_own = sb("ones_own", [8, P], BF16)
        own8 = sb("own8", [8, 8])
        shift = sb("shift", [P, REP * QT], BF16)

        own_t = [sb(f"own_t_{part}", [P, DC, TOK], BF16) for part in ("hi", "lo")]
        own_sin = sb("own_sin", [P, TILES, HD // 2])
        own_cos = sb("own_cos", [P, TILES, HD // 2])

        with Stage(nc, "cross_w") as st:
            ps = st.banks()
            row = st.sb("row", [P, TILES, DM])
            stats = st.sb("stats", [P, TILES, 6])
            mean_var = st.sb("mean_var", [P, TILES, 2])
            rs = st.sb("rs", [P, 3, TILES])
            where = st.sb("where", [P, BATCH, QT], I32)
            where_f = st.sb("where_f", [P, TILES])
            angle = st.sb("angle", [P, TILES, HD // 2])
            turns = st.sb("turns", [P, TILES, HD // 2])
            weight_loaded = {n: st.sem(f"w_{n}_loaded") for n in "kvqo"}
            small, dve_step, act_step, rs_ready, rs_done, row_ready = (st.sem(s) for s in ("small", "dve_step", "act_step", "rs_ready", "rs_done", "row_ready"))
            angle_ready, row_t, own_hi = (st.sem(s) for s in ("angle_ready", "row_t", "own_hi"))
            raw = {n: st.sb(f"raw_{n}", [P, c, m]) for n, c, m in names}
            loaded, high_done = st.sem("loaded"), st.sem("high_done")
            with nc.Block() as block:
                @block.sync
                def _(sp):
                    sp.dma_start(where[:], a["positions"][:, :, 0:QT].rearrange("b p k -> p b k")).then_inc(small, 16)
                    sp.dma_start(freq[:], a["c_cross_freq"].partition_broadcast(P)).then_inc(small, 16)
                    for n, src in (("k", "Wk"), ("v", "Wv"), ("q", "Wq"), ("o", "Wo")):
                        sp.dma_start(raw[n][:], w[src].rearrange("(c p) n -> p c n", p=P)).then_inc(weight_loaded[n], 16)
                    for gain, src in ((k_gain, "k_norm_w"), (q_gain, "q_norm_w")):
                        sp.dma_start(gain[:, 0, :], w[src].partition_broadcast(P)).then_inc(loaded, 16)
                        sp.dma_start(gain[:, 1, 0:HD // 2], w[src][HD // 2:HD].partition_broadcast(P)).then_inc(loaded, 16)
                        sp.dma_start(gain[:, 1, HD // 2:HD], w[src][0:HD // 2].partition_broadcast(P)).then_inc(loaded, 16)
                    sp.dma_start(own8[:], a["c_cross_own"]).then_inc(loaded, 16)

                @block.gpsimd
                def _(gp):
                    nc.gpsimd.memset(ones[:], 1.0)
                    nc.gpsimd.memset(ones_own[:], 1.0)

                @block.scalar
                def _(ac):
                    step = chain(ac, act_step)
                    ac.wait_ge(rs_ready, 1)
                    nc.scalar.activation(rs[:, 1, :], rs[:, 0, :], ACT.Sqrt).then_inc(rs_done, 1)
                    ac.wait_ge(angle_ready, 1)
                    waves(step, nc.scalar, own_sin[:], own_cos[:], angle[:], turns[:], const["half_pi"][:])
                    for b in range(BATCH):
                        ac.wait_ge(row_t, b + 1)
                        nc.scalar.copy(own_t[0][:, :, b * SEQ:(b + 1) * SEQ], ps[:, b, :].rearrange("p (c n) -> p c n", c=DC)).then_inc(own_hi, 1)
                    for n in "kvqo":
                        ac.wait_ge(weight_loaded[n], 16)
                        nc.scalar.copy(W[n][0][:], raw[n][:]).then_inc(high_done, 1)

                @block.tensor
                def _(pe):
                    for b in range(BATCH):
                        pe.wait_ge(row_ready, QT * (b + 1))
                        for c in range(DC):
                            for q in range(QT):
                                last = nc.tensor.transpose(ps[:, b, c * SEQ + q * P:c * SEQ + (q + 1) * P],
                                                           row[:, b * QT + q, c * P:(c + 1) * P], const["ident"][:])
                        last.then_inc(row_t, 1)

                @block.vector
                def _(ve):
                    link = chain(ve, dve_step)
                    row_stats(nc, link, x, stats, mean_var)
                    nc.vector.tensor_scalar(rs[:, 0, :], mean_var[:, :, 1], 1e-5, None, ALU.add).then_inc(rs_ready, 1)
                    ve.wait_ge(small, 32)
                    link(count_turns(link, nc.vector, angle[:], turns[:], where_f[:], where[:].rearrange("p b k -> p (b k)"), freq[:]))
                    less_turns(link, nc.vector, angle[:], turns[:]).then_inc(angle_ready, 1)
                    ve.wait_ge(rs_done, 1)
                    link(nc.vector.reciprocal(rs[:, 2, :], rs[:, 1, :]))
                    for t in range(TILES):
                        nc.vector.tensor_scalar(row[:, t, :], x[:, t, :], mean_var[:, t, 0:1], rs[:, 2, t:t + 1],
                                                ALU.subtract, ALU.mult).then_inc(row_ready, 1)
                    for b in range(BATCH):
                        ve.wait_ge(own_hi, b + 1)
                        tok = slice(b * SEQ, (b + 1) * SEQ)
                        nc.vector.tensor_tensor(own_t[1][:, :, tok], ps[:, b, :].rearrange("p (c n) -> p c n", c=DC),
                                                own_t[0][:, :, tok], ALU.subtract)
                    for i, n in enumerate("kvqo"):
                        ve.wait_ge(weight_loaded[n], 16)
                        ve.wait_ge(high_done, i + 1)
                        nc.vector.tensor_tensor(W[n][1][:], raw[n][:], W[n][0][:], ALU.subtract)
                    ve.wait_ge(loaded, 16 * 7)
                    for gain in (k_gain, q_gain):
                        nc.vector.tensor_scalar(gain[:, 1, 0:HD // 2], gain[:, 1, 0:HD // 2], -1.0, None, ALU.mult)

        with nc.Fori(0, BATCH) as b:
            project_row(nc, const, a, b, W, own_t, own_sin, own_cos, k_t, q_t, v, k_gain, q_gain, freq, shift)
            attend_row(nc, x, const, b, W["o"], k_t, q_t, v, ones, ones_own, own8, shift)


def project_row(nc, const, a, b, W, own_t, own_sin, own_cos, k_t, q_t, v, k_gain, q_gain, freq, shift):
    with Stage(nc, "project") as st:
        sb, sem = st.sb, st.sem
        ps = st.banks()
        H2 = HD // 2
        ctx_t = sb("ctx_t", [P, DC, CTX])
        in_t = [sb(f"in_t_{part}", [P, DC, KEYS], BF16) for part in ("hi", "lo")]
        where = sb("where", [P, KT], I32)
        where_f = sb("where_f", [P, KT])
        angle = sb("angle", [P, KT, H2])
        turns = sb("turns", [P, KT, H2])
        sin = sb("sin", [P, KT, H2])
        cos = angle
        k_tab = [sb(f"k_tab_{f}", [P, KT, HD]) for f in ("cos", "sin")]
        q_tab = [sb(f"q_tab_{f}", [P, QT, HD]) for f in ("cos", "sin")]
        squares = sb("squares", [P, 4, HD], BF16)
        eps = sb("eps", [P, 1])
        ss = sb("ss", [P, 2, 4])
        dev = sb("dev", [P, 2, 4])
        rms = sb("rms", [P, 2, 4])
        by_cos = sb("by_cos", [P, 2, 4, HD])
        by_sin = sb("by_sin", [P, 2, 4, HD])
        summed = by_cos
        normed = sb("normed", [P, 2, 4, HD])
        tops = sb("tops", [P, REP * QT, NCH])
        top = sb("top", [P, REP * QT])

        loaded, ctx_loaded = sem("loaded"), sem("ctx_loaded")
        dve_step, act_step, pool_step = sem("dve_step"), sem("act_step"), sem("pool_step")
        own_ready = sem("own_ready")
        ctx_hi, ctx_ready = sem("ctx_hi"), sem("ctx_ready")
        ctx_turns, ctx_angle, ctx_waves, ctx_tabs = (sem(s) for s in ("ctx_turns", "ctx_angle", "ctx_waves", "ctx_tabs"))
        projected, v_projected, v_hi, v_taken = (sem(s) for s in ("projected", "v_projected", "v_hi", "v_taken"))
        squared, dev_ready = sem("squared"), sem("dev_ready")
        taken, q_summed, k_summed, rms_ready, normed_ready = (sem(s) for s in ("taken", "q_summed", "k_summed", "rms_ready", "normed_ready"))
        turned, hi_ready, lo_ready = sem("turned"), sem("hi_ready"), sem("lo_ready")
        piece_ready, piece_taken = sem("piece_ready"), sem("piece_taken")

        FIRST = 6
        q_units = [("q", q, g) for g in range(QH // 4) for q in range(QT)]
        units = q_units[:FIRST] + [("k", k, 0) for k in range(KT)] + q_units[FIRST:]
        LAG = 2

        def shape(u):
            kind, tile, g = units[u]
            return kind, tile, g, rows_of(tile) if kind == "k" else P, u % 2

        def wait_summed(engine, u):
            kinds = [unit[0] for unit in units[:u + 1]]
            engine.wait_ge(k_summed if kinds[-1] == "k" else q_summed, kinds.count(kinds[-1]))

        def place(u):
            kind, tile, g = units[u]
            if kind == "k":
                return [part[:, :, tile * P:tile * P + rows_of(tile)] for part in k_t]
            return [part[:, 4 * g:4 * g + 4, tile * P:(tile + 1) * P] for part in q_t]

        def chunk_end(c):
            return FIRST + min(4 * c + 3, KT - 1)

        N = len(units)
        pieces_at, waiting, c = [], [], 0
        for u in range(N):
            while c < NCH and chunk_end(c) + LAG + 1 <= u:
                waiting += [(c, n) for n in range(REP * QT)]
                c += 1
            some = 2
            pieces_at.append(waiting[:some])
            waiting = waiting[some:]
        at_end = waiting + [(cc, n) for cc in range(c, NCH) for n in range(REP * QT)]
        order = [i for group in pieces_at for i in group] + at_end
        nth = {piece: n for n, piece in enumerate(order)}

        def table(engine, tab, gain, tiles, s):
            cols, n = slice(s * H2, (s + 1) * H2), tiles.stop - tiles.start
            engine.tensor_tensor(tab[0][:, tiles, cols], cos[:, tiles], bcast(gain[:, 0, cols], 1, n), ALU.mult)
            return engine.tensor_tensor(tab[1][:, tiles, cols], sin[:, tiles], bcast(gain[:, 1, cols], 1, n), ALU.mult)

        own_tiles, ctx_tiles = slice(0, QT), slice(QT, KT)

        with nc.Block() as block:
            @block.sync
            def _(sp):
                sp.dma_start(where[:], a["positions"][bass.ds(b, 1)].rearrange("b p k -> (b p) k")).then_inc(loaded, 16)
                for c in range(DC):
                    sp.dma_start(ctx_t[:, c, :], a["ctx_t"][bass.ds(b, 1), c * P:(c + 1) * P, :].rearrange("b p n -> (b p) n")).then_inc(ctx_loaded, 16)
                    if c + 1 < DC:
                        sp.wait_ge(ctx_loaded, 16 * (c + 1))

            @block.gpsimd
            def _(gp):
                link = chain(gp, pool_step)
                gp.wait_ge(loaded, 16)
                count_turns(link, nc.gpsimd, angle[:, ctx_tiles], turns[:, ctx_tiles], where_f[:, ctx_tiles], where[:, ctx_tiles],
                            freq[:]).then_inc(ctx_turns, 1)
                for u in range(N):
                    kind, tile, g, r, k = shape(u)
                    if kind == "k":
                        gp.wait_ge(taken, u + 1)
                        nc.gpsimd.tensor_tensor(summed[0:r, k], by_cos[0:r, k], by_sin[0:r, k], ALU.add).then_inc(k_summed, 1)
                    wait_summed(gp, u)
                    gp.wait_ge(rms_ready, u + 1)
                    if u >= 2:
                        gp.wait_ge(turned, u - 1)
                    nc.gpsimd.tensor_tensor(normed[0:r, k], summed[0:r, k], bcast(rms[0:r, k, :], 2, HD),
                                            ALU.mult).then_inc(normed_ready, 1)
                    if u in (3, 4):
                        gp.wait_ge(ctx_waves, 1)
                        table(nc.gpsimd, k_tab, k_gain, ctx_tiles, u - 3).then_inc(ctx_tabs, 1)

            @block.vector
            def _(ve):
                link = chain(ve, dve_step)
                nc.vector.memset(eps[:], 1e-6)
                for part in range(2):
                    nc.vector.tensor_copy(in_t[part][:, :, 0:SEQ], own_t[part][:, :, bass.ds(b * SEQ, SEQ)]).then_inc(own_ready, 1)
                nc.vector.tensor_copy(sin[:, own_tiles], own_sin[:, bass.ds(b * QT, QT), :])
                link(nc.vector.tensor_copy(cos[:, own_tiles], own_cos[:, bass.ds(b * QT, QT), :]))
                for s in range(2):
                    table(nc.vector, q_tab, q_gain, own_tiles, s)
                    last = table(nc.vector, k_tab, k_gain, own_tiles, s)
                link(last)

                def rotate(u):
                    kind, tile, g, r, k = shape(u)
                    tab = k_tab if kind == "k" else q_tab
                    bank = ps[0:r, 2 * k, :].rearrange("p (h n) -> p h n", h=4)
                    if kind == "k" and tile == QT:
                        ve.wait_ge(ctx_tabs, 2)
                    ve.wait_ge(squared, u + 1)
                    if u >= 2:
                        ve.wait_ge(normed_ready, u - 1)
                    nc.vector.tensor_tensor(by_cos[0:r, k], bank, bcast(tab[0][0:r, tile, :], 1, 4), ALU.mult)
                    for s in range(2):
                        to, of = slice(s * H2, (s + 1) * H2), slice((1 - s) * H2, (2 - s) * H2)
                        last = nc.vector.tensor_tensor(by_sin[0:r, k, :, to], bank[:, :, of], bcast(tab[1][0:r, tile, to], 1, 4), ALU.mult)
                    last.then_inc(taken, 1)
                    ve.wait_ge(dev_ready, u + 1)
                    nc.vector.reciprocal(rms[0:r, k, :], dev[0:r, k, :]).then_inc(rms_ready, 1)
                    if kind == "q":
                        ve.wait_ge(taken, u + 1)
                        nc.vector.tensor_tensor(summed[0:r, k], by_cos[0:r, k], by_sin[0:r, k], ALU.add).then_inc(q_summed, 1)
                    else:
                        ve.wait_ge(v_hi, tile + 1)
                        nc.vector.tensor_tensor(v[1][0:r, tile, :], ps[0:r, 2 * (tile % 2) + 1, :], v[0][0:r, tile, :],
                                                ALU.subtract).then_inc(v_taken, 1)

                def low(u):
                    kind, tile, g, r, k = shape(u)
                    hi, lo = place(u)
                    ve.wait_ge(hi_ready, u + 1)
                    nc.vector.tensor_tensor(lo, ps[:, 4 + k, :].rearrange("p (h n) -> p h n", h=4)[:, :, 0:r], hi,
                                            ALU.subtract).then_inc(lo_ready, 1)

                def reduce_piece(piece):
                    n, (c, i) = nth[piece], piece
                    ve.wait_ge(piece_ready, n + 1)
                    nc.vector.tensor_reduce(tops[:, i, c:c + 1], ps[:, 6 + n % 2, 0:CHUNKS[c][1]], AX_X, ALU.max).then_inc(piece_taken, 1)

                for u in range(N + LAG):
                    if u < N:
                        rotate(u)
                        if u == 1:
                            ve.wait_ge(ctx_turns, 1)
                            less_turns(link, nc.vector, angle[:, ctx_tiles], turns[:, ctx_tiles]).then_inc(ctx_angle, 1)
                        if u in (3, 4):
                            c = u - 3
                            ve.wait_ge(ctx_hi, c + 1)
                            nc.vector.tensor_tensor(in_t[1][:, c, SEQ:KEYS], ctx_t[:, c, :], in_t[0][:, c, SEQ:KEYS],
                                                    ALU.subtract).then_inc(ctx_ready, 1)
                        for piece in pieces_at[u]:
                            reduce_piece(piece)
                    if u >= LAG:
                        low(u - LAG)
                for piece in at_end:
                    reduce_piece(piece)
                ve.wait_ge(piece_taken, len(order))
                link(nc.vector.tensor_reduce(top[:], tops[:], AX_X, ALU.max))
                link(nc.vector.tensor_scalar(shift[:], top[:], -1.0, None, ALU.mult))

            @block.scalar
            def _(ac):
                step = chain(ac, act_step)

                def square(u):
                    kind, tile, g, r, k = shape(u)
                    ac.wait_ge(projected, u + 1)
                    if u >= 2:
                        ac.wait_ge(rms_ready, u - 1)
                    if u >= 1:
                        ac.wait_ge(squared, u)
                    for h in range(4):
                        last = nc.scalar.activation(squares[0:r, h, :], ps[0:r, 2 * k, h * HD:(h + 1) * HD], ACT.Square,
                                                    accum_out=ss[0:r, k, h:h + 1])
                    last.then_inc(squared, 1)

                def deviate(u):
                    kind, tile, g, r, k = shape(u)
                    ac.wait_ge(squared, u + 1)
                    nc.scalar.activation(dev[0:r, k, :], ss[0:r, k, :], ACT.Sqrt, scale=1.0 / HD, bias=eps[0:r, :]).then_inc(dev_ready, 1)

                def v_high(tile):
                    r = rows_of(tile)
                    ac.wait_ge(v_projected, tile + 1)
                    nc.scalar.copy(v[0][0:r, tile, :], ps[0:r, 2 * (tile % 2) + 1, :]).then_inc(v_hi, 1)

                def high(u):
                    kind, tile, g, r, k = shape(u)
                    ac.wait_ge(turned, u + 1)
                    nc.scalar.copy(place(u)[0], ps[:, 4 + k, :].rearrange("p (h n) -> p h n", h=4)[:, :, 0:r]).then_inc(hi_ready, 1)

                for u in range(N + LAG):
                    if u < N:
                        square(u)
                        deviate(u)
                    if u in (2, 3):
                        ac.wait_ge(ctx_loaded, 16 * (u - 1))
                        nc.scalar.copy(in_t[0][:, u - 2, SEQ:KEYS], ctx_t[:, u - 2, :]).then_inc(ctx_hi, 1)
                    if u == 2:
                        ac.wait_ge(ctx_angle, 1)
                        waves(step, nc.scalar, sin[:, ctx_tiles], cos[:, ctx_tiles], angle[:, ctx_tiles], turns[:, ctx_tiles],
                              const["half_pi"][:]).then_inc(ctx_waves, 1)
                    if FIRST <= u < FIRST + KT:
                        v_high(u - FIRST)
                    if u >= LAG:
                        high(u - LAG)

            @block.tensor
            def _(pe):
                pe.wait_ge(own_ready, 2)

                def product(out, tile, r, name, group):
                    for n, (one, two, c) in enumerate((one, two, c) for one, two in ((0, 0), (0, 1), (1, 0)) for c in range(DC)):
                        last = nc.tensor.matmul(out, in_t[one][:, c, tile * P:tile * P + r], W[name][two][:, c, group * 512:(group + 1) * 512],
                                                start=(n == 0), stop=(n == 3 * DC - 1))
                    return last

                def project(u):
                    kind, tile, g, r, k = shape(u)
                    if kind == "k" and tile == QT:
                        pe.wait_ge(ctx_ready, DC)
                    if u >= 2:
                        pe.wait_ge(taken, u - 1)
                    product(ps[0:r, 2 * k, :], tile, r, kind, g).then_inc(projected, 1)
                    if kind == "k":
                        if tile >= 2:
                            pe.wait_ge(v_taken, tile - 1)
                        product(ps[0:r, 2 * (tile % 2) + 1, :], tile, r, "v", 0).then_inc(v_projected, 1)

                def turn(u):
                    kind, tile, g, r, k = shape(u)
                    pe.wait_ge(normed_ready, u + 1)
                    if u >= 2:
                        pe.wait_ge(lo_ready, u - 1)
                    for h in range(4):
                        last = nc.tensor.transpose(ps[:, 4 + k, h * P:h * P + r], normed[0:r, k, h, :], const["ident"][0:r, 0:r])
                    last.then_inc(turned, 1)

                def multiply_piece(piece):
                    n, (c, i) = nth[piece], piece
                    s, m = CHUNKS[c]
                    pe.wait_ge(hi_ready, chunk_end(c) + 1)
                    if n >= 2:
                        pe.wait_ge(piece_taken, n - 1)
                    nc.tensor.matmul(ps[:, 6 + n % 2, 0:m], q_t[0][:, i // QT, i % QT * P:(i % QT + 1) * P], k_t[0][:, 0, s:s + m],
                                     start=True, stop=True).then_inc(piece_ready, 1)

                for u in range(N + LAG):
                    if u < N:
                        project(u)
                        for piece in pieces_at[u]:
                            multiply_piece(piece)
                    if u >= LAG:
                        turn(u - LAG)
                for piece in at_end:
                    multiply_piece(piece)


def attend_row(nc, x, const, b, w_o, k_t, q_t, v, ones, ones_own, own8, shift):
    with Stage(nc, "attend") as st:
        sb, sem = st.sb, st.sem
        ps = st.banks()
        SCALE = float(HD) ** -0.5
        STEPS = KVH * KT
        PIECES = REP * QT * NCH
        p32 = sb("p32", [P, 2, QCOLS])
        p_hi = sb("p_hi", [P, 2, QCOLS], F16)
        p_lo = sb("p_lo", [P, 2, QCOLS], F16)
        acc = sb("acc", [P, 2, QCOLS])
        tops = sb("tops", [P, REP * QT, NCH])
        top = sb("top", [P, REP * QT])
        own = sb("own", [8, 2, 8, P], BF16)
        raw = sb("raw", [P, QCOLS])
        inv = sb("inv", [P, REP * QT])
        diag = sb("diag", [P, REP * QT, P])
        scaled = sb("scaled", [P, QCOLS])
        att = [sb(f"att_{part}", [P, QH, SEQ], BF16) for part in ("hi", "lo")]
        row = sb("row", [P, QT, DM])

        dve_step = sem("dve_step")
        side_ready, side_taken, shift_ready = sem("side_ready"), sem("side_taken"), sem("shift_ready")
        scored, p32_ready, hi_ready, lo_ready, summed = sem("scored"), sem("p32_ready"), sem("hi_ready"), sem("lo_ready"), sem("summed")
        weighed, raw_ready, att_hi, att_lo = sem("weighed"), sem("raw_ready"), sem("att_hi"), sem("att_lo")
        out_ready = sem("out_ready")

        def side_work(step):
            k, t = divmod(step, KT)
            if t == 1 and k >= 1:
                return [("sum", k - 1, 0)], [("spread", k - 1, 0)]
            if k + 1 < KVH and 2 <= t < 13:
                pieces = [("piece", k + 1, n) for n in range(3 * (t - 2), min(3 * (t - 1), PIECES))]
                return pieces[:2], pieces[2:]
            if k + 1 < KVH and t == 13:
                return [("turn", k + 1, 0)], []
            return [], []

        before = [("turn", 0, 0)]
        after = [("sum", KVH - 1, 0), ("spread", KVH - 1, 0)]
        order = before + [i for s in range(STEPS) for part in side_work(s) for i in part] + after
        at = {item: n for n, item in enumerate(order)}

        with nc.Block() as block:
            @block.tensor
            def _(pe):
                def side(item):
                    kind, k, n = item
                    if kind == "piece":
                        prior = order[at[item] - 1][0] if at[item] else None
                        done = at[item] - 1 if prior == "piece" else at[item]
                        if done >= 1:
                            pe.wait_ge(side_taken, done)
                        c, (s, m) = n // NCH, CHUNKS[n % NCH]
                        nc.tensor.matmul(ps[:, 6 + n % 2, 0:m], q_t[0][:, REP * k + c // QT, c % QT * P:(c % QT + 1) * P],
                                         k_t[0][:, k, s:s + m], start=True, stop=True).then_inc(side_ready, 1)
                    elif kind == "turn":
                        if k >= 1:
                            pe.wait_ge(side_taken, at[item])
                            pe.wait_ge(shift_ready, k)
                        nc.tensor.matmul(ps[0:8, 6, 0:P], shift[:], const["ident_b"][:], start=True, stop=True).then_inc(side_ready, 1)
                    elif kind == "sum":
                        pe.wait_ge(side_taken, at[item])
                        pe.wait_ge(summed, KT * (k + 1))
                        for c in range(REP * QT):
                            last = nc.tensor.matmul(ps[:, 6, c:c + 1], acc[:, k % 2, c * P:(c + 1) * P], ones[:, 0:1], start=True, stop=True)
                        last.then_inc(side_ready, 1)
                    else:
                        pe.wait_ge(side_taken, at[item])
                        for n in range(2):
                            last = nc.tensor.matmul(ps[:, 6 + n, :], ones[:], diag[:, 4 * n:4 * n + 4, :], start=True, stop=True)
                        last.then_inc(side_ready, 1)

                def score(step):
                    k, t = divmod(step, KT)
                    r, keys = rows_of(t), slice(t * P, t * P + rows_of(t))
                    if step >= 2:
                        pe.wait_ge(hi_ready, step - 1)
                    for n in range(2):
                        cols = slice(REP * k + 2 * n, REP * k + 2 * n + 2)
                        out = ps[0:r, 2 * (step % 2) + n, :]
                        for one, two in ((0, 0), (0, 1), (1, 0)):
                            nc.tensor.matmul(out, k_t[one][:, k, keys], q_t[two][:, cols, :], start=(one == two), stop=False)
                    if t == 0:
                        pe.wait_ge(side_taken, at[("turn", k, 0)] + 1)
                    for n in range(2):
                        last = nc.tensor.matmul(ps[0:r, 2 * (step % 2) + n, :], ones_own[:, 0:r], own[:, k % 2, 4 * n:4 * n + 4, :],
                                                start=False, stop=True)
                    last.then_inc(scored, 1)

                def weigh(step):
                    k, t = divmod(step, KT)
                    r, head = rows_of(t), slice(k * HD, (k + 1) * HD)
                    pe.wait_ge(lo_ready, step + 1)
                    if t == 0 and k >= 1:
                        pe.wait_ge(raw_ready, k)
                    for one, p in ((0, p_hi), (0, p_lo), (1, p_hi)):
                        for n in range(2):
                            last = nc.tensor.matmul(ps[:, 4 + n, :], v[one][0:r, t, head], p[0:r, step % 2, n * 512:(n + 1) * 512],
                                                    start=(t == 0 and one == 0 and p is p_hi), stop=(t == KT - 1 and one == 1))
                    last.then_inc(weighed, 1)

                for item in before:
                    side(item)
                for step in range(STEPS):
                    score(step)
                    first, second = side_work(step)
                    for item in first:
                        side(item)
                    if step >= 1:
                        weigh(step - 1)
                    for item in second:
                        side(item)
                weigh(STEPS - 1)

                def project_out(heads, q):
                    for h in heads:
                        for one, two in ((0, 0), (0, 1), (1, 0)):
                            last = nc.tensor.matmul(ps[:, q, 0:DM], att[one][:, h, q * P:(q + 1) * P], w_o[two][:, h, :],
                                                    start=(h == 0 and one == two), stop=(h == QH - 1 and one == 1))
                    return last

                pe.wait_ge(att_lo, KVH - 1)
                pe.wait_ge(hi_ready, STEPS)
                project_out(range(QH - REP), 0)
                side(("sum", KVH - 1, 0))
                project_out(range(QH // 2), 1)
                side(("spread", KVH - 1, 0))
                project_out(range(QH // 2, QH - REP), 1)
                pe.wait_ge(att_lo, KVH)
                for q in range(QT):
                    project_out(range(QH - REP, QH), q).then_inc(out_ready, 1)

            @block.scalar
            def _(ac):
                def copy_out(k):
                    ac.wait_ge(weighed, KT * (k + 1))
                    if k >= 1:
                        ac.wait_ge(side_taken, at[("spread", k - 1, 0)] + 1)
                    nc.scalar.copy(raw[:], ps[:, 4:6, :].rearrange("p a n -> p (a n)")).then_inc(raw_ready, 1)

                def high(k):
                    ac.wait_ge(side_taken, at[("spread", k, 0)] + 1)
                    nc.scalar.copy(att[0][:, REP * k:REP * (k + 1), :], scaled[:].rearrange("p (h n) -> p h n", h=REP)).then_inc(att_hi, 1)

                for step in range(STEPS):
                    k, t = divmod(step, KT)
                    r, i = rows_of(t), step % 2
                    src = ps[0:r, 2 * i:2 * i + 2, :].rearrange("p a n -> p (a n)")
                    ac.wait_ge(scored, step + 1)
                    if step >= 2:
                        ac.wait_ge(lo_ready, step - 1)
                        ac.wait_ge(summed, step - 1)
                    nc.scalar.activation(p32[0:r, i, :], src, ACT.Exp, scale=SCALE).then_inc(p32_ready, 1)
                    if step >= 2:
                        ac.wait_ge(weighed, step - 1)
                    nc.scalar.activation(p_hi[0:r, i, :], src, ACT.Exp, scale=SCALE).then_inc(hi_ready, 1)
                    if t == 0 and k >= 1:
                        copy_out(k - 1)
                    if t == 3 and k >= 1:
                        high(k - 1)
                copy_out(KVH - 1)
                high(KVH - 1)

            @block.gpsimd
            def _(gp):
                for step in range(STEPS):
                    k, t = divmod(step, KT)
                    r, i = rows_of(t), step % 2
                    gp.wait_ge(p32_ready, step + 1)
                    if t == 0:
                        if k >= 2:
                            gp.wait_ge(side_taken, at[("sum", k - 2, 0)] + 1)
                        nc.gpsimd.tensor_copy(acc[:, k % 2, :], p32[:, i, :]).then_inc(summed, 1)
                    else:
                        gp.wait_ge(summed, step)
                        nc.gpsimd.tensor_tensor(acc[0:r, k % 2, :], acc[0:r, k % 2, :], p32[0:r, i, :], ALU.add).then_inc(summed, 1)

            @block.vector
            def _(ve):
                link = chain(ve, dve_step)

                def side(item):
                    kind, k, n = item
                    ve.wait_ge(side_ready, at[item] + 1)
                    if kind == "piece":
                        c, m = n // NCH, CHUNKS[n % NCH][1]
                        nc.vector.tensor_reduce(tops[:, c, n % NCH:n % NCH + 1], ps[:, 6 + n % 2, 0:m], AX_X, ALU.max)\
                            .then_inc(side_taken, 1)
                        if n == PIECES - 1:
                            ve.wait_ge(side_taken, at[item] + 1)
                            link(nc.vector.tensor_reduce(top[:], tops[:], AX_X, ALU.max))
                            nc.vector.tensor_scalar(shift[:], top[:], -1.0, None, ALU.mult).then_inc(shift_ready, 1)
                    elif kind == "turn":
                        if k >= 2:
                            ve.wait_ge(scored, KT * (k - 1))
                        nc.vector.tensor_tensor(own[:, k % 2], bcast(ps[0:8, 6, 0:P], 1, 8), bcast(own8[:], 2, P),
                                                ALU.mult).then_inc(side_taken, 1)
                    elif kind == "sum":
                        link(nc.vector.reciprocal(inv[:], ps[:, 6, 0:REP * QT]))
                        nc.vector.tensor_tensor(diag[:], bcast(const["ident"][:], 1, REP * QT), bcast(inv[:], 2, P),
                                                ALU.mult).then_inc(side_taken, 1)
                    else:
                        ve.wait_ge(raw_ready, k + 1)
                        if k >= 1:
                            ve.wait_ge(att_lo, k)
                            ve.wait_ge(att_hi, k)
                        nc.vector.tensor_tensor(scaled[:], raw[:], ps[:, 6:8, :].rearrange("p a n -> p (a n)"), ALU.mult)\
                            .then_inc(side_taken, 1)

                def rest(k):
                    ve.wait_ge(att_hi, k + 1)
                    heads = slice(REP * k, REP * (k + 1))
                    nc.vector.tensor_tensor(att[1][:, heads, :], scaled[:].rearrange("p (h n) -> p h n", h=REP), att[0][:, heads, :],
                                            ALU.subtract).then_inc(att_lo, 1)

                for item in before:
                    side(item)
                for step in range(STEPS):
                    k, t = divmod(step, KT)
                    r, i = rows_of(t), step % 2
                    first, second = side_work(step)
                    for item in first:
                        side(item)
                    ve.wait_ge(hi_ready, step + 1)
                    if step >= 2:
                        ve.wait_ge(weighed, step - 1)
                    nc.vector.tensor_tensor(p_lo[0:r, i, :], p32[0:r, i, :], p_hi[0:r, i, :], ALU.subtract).then_inc(lo_ready, 1)
                    for item in second:
                        side(item)
                    if t == 4 and k >= 1:
                        rest(k - 1)
                for item in after:
                    side(item)
                rest(KVH - 1)
                link(nc.vector.tensor_copy(row[:], x[:, bass.ds(b * QT, QT), :]))
                ve.wait_ge(out_ready, QT)
                link(nc.vector.tensor_tensor(row[:], row[:], ps[:, 0:2, 0:DM], ALU.add))
                link(nc.vector.tensor_copy(x[:, bass.ds(b * QT, QT), :], row[:]))


def expert_ffn(nc, x, const, a, w):
    with Stage(nc, "moe") as st:
        sb, sem = st.sb, st.sem
        ps = st.banks()
        E, M = 8, 128
        w_gate = sb("w_gate", [P, DC, E])
        w_up = [sb(f"w_up{i}", [P, E, DC, M]) for i in range(2)]
        w_down = sb("w_down", [P, E, DM])
        number = sb("number", [P, E])
        stats = sb("stats", [P, TILES, 6])
        mean_var = sb("mean_var", [P, TILES, 2])
        rs = sb("rs", [P, 6, TILES])
        half = sb("half", [P, TILES])
        xn = sb("xn", [P, TILES, DM])
        xn_t = sb("xn_t", [P, DC, TOK])
        logits = sb("logits", [P, TILES, E])
        best = sb("best", [P, TILES, E])
        which = sb("which", [P, TILES, E], U32)
        which_f = sb("which_f", [P, TILES, E])
        two = sb("two", [P, 3, TILES])
        hit = sb("hit", [P, 2, TILES, E])
        share = sb("share", [P, TILES, E])
        act = sb("act", [P, 2, 512])
        inner = sb("inner", [P, 2, TOK])

        loaded = sem("weights_loaded")
        dve_step, rs_ready, rs_done = sem("dve_step"), sem("rs_ready"), sem("rs_done")
        xn_ready, xt_ready, xnt_ready = sem("xn_ready"), sem("xt_ready"), sem("xnt_ready")
        logits_ready, diff_ready, exp_ready = sem("logits_ready"), sem("diff_ready"), sem("exp_ready")
        up_ready, act_ready, inner_ready, down_ready, added = sem("up_ready"), sem("act_ready"), sem("inner_ready"), sem("down_ready"), sem("added")

        with nc.Block() as block:
            @block.sync
            def _(sp):
                sp.dma_start(w_gate[:], w["w_gate"].rearrange("(c p) n -> p c n", p=P)).then_inc(loaded, 16)
                sp.dma_start(number[:], a["c_number"].partition_broadcast(P)).then_inc(loaded, 16)
                for i in range(2):
                    sp.dma_start(w_up[i][:], w[f"wi_{i}"].rearrange("e (c p) m -> p e c m", p=P)).then_inc(loaded, 16)
                sp.dma_start(w_down[:], w["wo"].rearrange("e p n -> p e n")).then_inc(loaded, 16)

            @block.gpsimd
            def _(gp):
                nc.gpsimd.memset(half[:], -0.5).then_inc(rs_done, 1)
                gp.wait_ge(rs_done, 1)
                gp.wait_ge(rs_ready, 1)
                nc.gpsimd.tensor_tensor(rs[:, 1, :], rs[:, 0, :], half[:], ALU.pow).then_inc(rs_done, 1)

            @block.vector
            def _(ve):
                link = chain(ve, dve_step)
                row_stats(nc, link, x, stats, mean_var)
                nc.vector.tensor_scalar(rs[:, 0, :], mean_var[:, :, 1], 1e-5, None, ALU.add).then_inc(rs_ready, 1)
                ve.wait_ge(rs_done, 2)
                for t in range(TILES):
                    nc.vector.tensor_scalar(xn[:, t, :], x[:, t, :], mean_var[:, t, 0:1], rs[:, 1, t:t + 1],
                                            ALU.subtract, ALU.mult).then_inc(xn_ready, 1)
                ve.wait_ge(loaded, 80)
                ve.wait_ge(logits_ready, 1)
                link(nc.vector.tensor_copy(logits[:].rearrange("p t e -> p (t e)"), ps[:, 4, 0:TILES * E]))
                for t in range(TILES):
                    last = nc.vector.max(best[:, t, :], logits[:, t, :])
                link(last)
                for t in range(TILES):
                    last = nc.vector.max_index(which[:, t, :], best[:, t, :], logits[:, t, :])
                nc.vector.tensor_tensor(two[:, 0, :], best[:, :, 1], best[:, :, 0], ALU.subtract).then_inc(diff_ready, 1)
                ve.wait_ge(diff_ready, 1)
                link(nc.vector.tensor_copy(which_f[:], which[:]))
                ve.wait_ge(exp_ready, 1)
                link(nc.vector.tensor_scalar(two[:, 1, :], two[:, 0, :], 1.0, None, ALU.add))
                link(nc.vector.reciprocal(two[:, 1, :], two[:, 1, :]))
                link(nc.vector.tensor_tensor(two[:, 2, :], two[:, 0, :], two[:, 1, :], ALU.mult))
                for i in range(2):
                    last = nc.vector.tensor_tensor(hit[:, i], bcast(number[:], 1, TILES), bcast(which_f[:, :, i], 2, E), ALU.is_equal)
                link(last)
                for i in range(2):
                    last = nc.vector.tensor_tensor(hit[:, i], hit[:, i], bcast(two[:, 1 + i, :], 2, E), ALU.mult)
                link(last)
                link(nc.vector.tensor_tensor(share[:], hit[:, 0], hit[:, 1], ALU.add))

                def multiply(e):
                    for n in range(2):
                        j = 2 * e + n
                        ve.wait_ge(act_ready, j + 1)
                        nc.vector.tensor_tensor(inner[:, e % 2, n * 512:(n + 1) * 512], act[:, n, :], ps[:, 2 * n + 1, :],
                                                ALU.mult).then_inc(inner_ready, 1)

                multiply(0)
                for e in range(E):
                    if e + 1 < E:
                        multiply(e + 1)
                    for t in range(TILES):
                        j = TILES * e + t
                        ve.wait_ge(down_ready, j + 1)
                        if e >= 1:
                            ve.wait_ge(added, j + 1 - TILES)
                        nc.vector.scalar_tensor_tensor(x[:, t, :], ps[:, 4 + t % 4, 0:DM], share[:, t, e:e + 1], x[:, t, :],
                                                       ALU.mult, ALU.add).then_inc(added, 1)

            @block.scalar
            def _(ac):
                for b in range(BATCH):
                    ac.wait_ge(xt_ready, b + 1)
                    nc.scalar.copy(xn_t[:, :, b * SEQ:(b + 1) * SEQ],
                                   ps[:, b, :].rearrange("p (c n) -> p c n", c=DC)).then_inc(xnt_ready, 1)
                ac.wait_ge(diff_ready, 1)
                nc.scalar.activation(two[:, 0, :], two[:, 0, :], ACT.Exp).then_inc(exp_ready, 1)
                for j in range(2 * E):
                    ac.wait_ge(up_ready, j + 1)
                    if j >= 2:
                        ac.wait_ge(inner_ready, j - 1)
                    nc.scalar.activation(act[:, j % 2, :], ps[:, 2 * (j % 2), :], ACT.Silu).then_inc(act_ready, 1)

            @block.tensor
            def _(pe):
                for b in range(BATCH):
                    pe.wait_ge(xn_ready, 2 * b + 2)
                    for c in range(DC):
                        for q in range(QT):
                            last = nc.tensor.transpose(ps[:, b, c * SEQ + q * P:c * SEQ + (q + 1) * P],
                                                       xn[:, b * QT + q, c * P:(c + 1) * P], const["ident"][:])
                    last.then_inc(xt_ready, 1)
                pe.wait_ge(xnt_ready, BATCH)
                pe.wait_ge(loaded, 80)
                for t in range(TILES):
                    for c in range(DC):
                        last = nc.tensor.matmul(ps[:, 4, t * E:(t + 1) * E], xn_t[:, c, t * P:(t + 1) * P], w_gate[:, c, :],
                                                start=(c == 0), stop=(c == DC - 1))
                last.then_inc(logits_ready, 1)

                def up(e):
                    for n in range(2):
                        if e >= 1:
                            pe.wait_ge(inner_ready, 2 * e - 1 + n)
                        for i in range(2):
                            for c in range(DC):
                                last = nc.tensor.matmul(ps[:, 2 * n + i, :], w_up[i][:, e, c, :], xn_t[:, c, n * 512:(n + 1) * 512],
                                                        start=(c == 0), stop=(c == DC - 1))
                        last.then_inc(up_ready, 1)

                up(0)
                pe.wait_ge(diff_ready, 1)
                for e in range(E):
                    if e + 1 < E:
                        up(e + 1)
                    pe.wait_ge(inner_ready, 2 * e + 2)
                    for t in range(TILES):
                        j = TILES * e + t
                        if j >= 4:
                            pe.wait_ge(added, j - 3)
                        nc.tensor.matmul(ps[:, 4 + t % 4, 0:DM], inner[:, e % 2, t * P:(t + 1) * P], w_down[:, e, :],
                                         start=True, stop=True).then_inc(down_ready, 1)



def run_self(nc, x, const, a, layer):
    w = layer("L0_attn_")
    w.update(cos=a["c_self_cos"], sin=a["c_self_sin"], causal=a["c_self_causal"])
    self_attention(nc, x, const, w)


def run_memory(nc, x, const, a, layer):
    memory_attention(nc, x, const, a)


def run_ffn(nc, x, const, a, layer):
    ternary_ffn(nc, x, const, a)


def run_scan(nc, x, const, a, layer):
    gated_scan(nc, x, const, a, layer("L1_attn_"))


def run_cross(nc, x, const, a, layer):
    cross_attention(nc, x, const, a, layer("L1_xattn_"))


def run_experts(nc, x, const, a, layer):
    expert_ffn(nc, x, const, a, layer("L1_ffn_"))


STAGES = [run_self, run_memory, run_ffn, run_scan, run_cross, run_experts]


def decoder(nc, a, out):
    with Stage(nc, "model") as st:
        x = st.sb("x", [P, TILES, DM])
        ident = st.sb("ident", [P, P])
        ident_b = st.sb("ident_b", [P, P], BF16)
        half_pi = st.sb("half_pi", [P, 1])
        const = {"ident": ident, "ident_b": ident_b, "half_pi": half_pi}
        x_loaded, x_stored = st.sem("x_loaded"), st.sem("x_stored")
        with nc.Block() as block:
            @block.sync
            def _(sp):
                sp.dma_start(x[:], a["x"].rearrange("b (t p) d -> p (b t) d", p=P)).then_inc(x_loaded, 16)
                sp.dma_start(ident[:], a["c_ident"]).then_inc(x_loaded, 16)
                sp.wait_ge(x_loaded, 32)

            @block.vector
            def _(ve):
                nc.vector.memset(half_pi[:], math.pi / 2)
                ve.wait_ge(x_loaded, 32)
                nc.vector.tensor_copy(ident_b[:], ident[:])

        def layer(prefix):
            return {k[len(prefix):]: v for k, v in a.items() if k.startswith(prefix)}

        for n, stage in enumerate(STAGES):
            stage(nc, x, const, a, layer)
        with nc.Block() as block:
            @block.sync
            def _(sp):
                sp.dma_start(out.rearrange("b (t p) d -> p (b t) d", p=P), x[:]).then_inc(x_stored, 16)
                sp.wait_ge(x_stored, 16)


def constants():
    c = {}
    c["c_ident"] = np.eye(P, dtype=np.float32)
    c["c_number"] = np.arange(8, dtype=np.float32)
    pick = np.zeros((BATCH, BATCH, P), np.float32)
    for b in range(BATCH):
        pick[b, b] = 1.0
    c["c_pick"] = pick
    pos = np.arange(SEQ, dtype=np.float32)
    f0 = np.arange(0, HD0, 2, dtype=np.float32) / np.float32(HD0) * np.log(np.float32(30000.0))
    ang = (pos[:, None] * f0[None, :]).astype(np.float32)
    for n, f in (("cos", np.cos), ("sin", np.sin)):
        c["c_self_" + n] = f(ang).astype(np.float32).reshape(QT, P, HD0 // 2).transpose(1, 0, 2).copy()
    causal = np.zeros((P, SEQ), np.float32)
    causal[:, P:] = np.where(np.tril(np.ones((P, P), bool)), 0.0, MASKED)
    c["c_self_causal"] = causal
    f1 = 1.0 / np.float32(10000.0) ** (np.arange(0, 16, 2, dtype=np.float32) / np.float32(16))
    ang = (pos[:, None] * f1[None, :].astype(np.float32)).astype(np.float32)
    ch = np.arange(P)
    c["c_scan_cos"] = np.cos(ang).astype(np.float32)[:, ch % 8].T.copy()
    c["c_scan_sin"] = (np.sin(ang).astype(np.float32)[:, ch % 8].T * np.where(ch % 16 < 8, -1.0, 1.0)[:, None]).astype(np.float32)
    c["c_scan_same"] = (ch[:, None] % 16 == np.arange(16)[None, :]).astype(np.float32)
    c["c_cross_freq"] = (1.0 / np.float32(10000.0) ** (np.arange(0, P, 2, dtype=np.float32) / np.float32(P))).astype(np.float32)
    c["c_cross_own"] = np.eye(8, dtype=np.float32)
    return c


def layouts(i):
    def column(v):
        return v.reshape(-1, P).T
    o = {k: i[k] for k in ("x", "ctx_2048", "L0_attn_Wq", "L0_attn_bq", "L0_attn_Wkv", "L0_attn_bkv", "L0_attn_Wo", "L0_attn_bo",
                           "L0_attn_ln_g", "L0_attn_ln_b", "L1_xattn_q_norm_w", "L1_xattn_k_norm_w",
                           "L1_ffn_w_gate", "L1_ffn_wi_0", "L1_ffn_wi_1", "L1_ffn_wo")}
    for k in ("L0_attn_qn_g", "L0_attn_qn_b", "L0_attn_kvn_g", "L0_attn_kvn_b", "L1_attn_norm_scale", "L1_attn_conv_b",
              "L1_attn_dt_bias"):
        o[k] = column(i[k])
    o["L1_attn_conv_w"] = i["L1_attn_conv_w"].reshape(DC, P, 4).transpose(1, 0, 2)
    for k in ("L0_ffn_w_fc", "L0_ffn_w_proj", "L1_attn_in_proj_w", "L1_attn_out_proj_w", "L1_xattn_Wq", "L1_xattn_Wk",
              "L1_xattn_Wv", "L1_xattn_Wo"):
        o[k] = i[k].T
    o["mix_rows"] = np.repeat(i["L1_attn_head_mix"], HD0, axis=0).reshape(DC, P, HEADS).transpose(1, 0, 2)
    place = np.zeros((BATCH, KT * P), i["pos_BxS2"].dtype)
    place[:, 0:SEQ] = i["itok_BxS_4096_4607"]
    place[:, SEQ:KEYS] = i["pos_BxS2"]
    o["positions"] = place.reshape(BATCH, KT, P).transpose(0, 2, 1)
    o["ctx_t"] = i["ctx_2048"].transpose(0, 2, 1)
    o["mask_BxS2_bk0"] = i["mask_BxS2_bk0"]
    return o


def kernel(**inputs):
    import concourse.bacc as _bacc
    from concourse.bass_utils import run_bass_kernel_spmd as _run

    nc = _bacc.Bacc("TRN2", target_bir_lowering=False, num_devices=1)
    arrays, args = {}, {}
    inputs = {k: np.asarray(v) for k, v in inputs.items()}
    for name, value in {**layouts(inputs), **constants()}.items():
        v = np.ascontiguousarray(value)
        arrays[f"in_{name}"] = v
        args[name] = nc.dram_tensor(f"in_{name}", v.shape, mybir.dt.from_np(v.dtype), kind="ExternalInput").ap()
    out = nc.dram_tensor("out_0", (BATCH, SEQ, DM), F32, kind="ExternalOutput").ap()
    decoder(nc, args, out)
    r = _run(nc, [arrays], core_ids=[0])
    return r.results[0]["out_0"]
```
